# Optimizing a Trainium2 kernel written in Bass

```python
import numpy as np
import jax
import jax.numpy as jnp

def _softmax(x, axis=-1):
    return jax.nn.softmax(x, axis=axis)

def _gelu(x):
    return jax.nn.gelu(x, approximate=True)

def _silu(x):
    return jax.nn.silu(x)

def _sigmoid(x):
    return jax.nn.sigmoid(x)

def _layernorm(x, axis=-1, eps=1e-05):
    m = jnp.mean(x, axis=axis, keepdims=True)
    v = jnp.var(x, axis=axis, keepdims=True)
    return (x - m) / jnp.sqrt(v + eps)

def _scatter_add(tgt, idx, src, axis=0):
    return tgt.at[idx].add(src)

def _segment_sum(src, seg, n):
    return jax.ops.segment_sum(src, seg, n)
kernel_name = 'mk_xattn_ffn_d1_seqx_r4_0ca18f'

def setup_inputs(seed: int=0):
    np.random.seed(seed)
    _w = jnp.asarray

    def _rec_inputs():
        import jax
        import jax.numpy as jnp
        _rk = jax.random.key(seed)
        x = -0.0003929 + 0.9999 * jax.random.normal(jax.random.fold_in(_rk, 1), (16, 128, 1024), jnp.float32)
        _lenS = 128 - jax.random.randint(jax.random.fold_in(_rk, 7), (16,), 0, max(1, 128 // 4) + 1, jnp.int32)
        _lenS2 = 128 - jax.random.randint(jax.random.fold_in(_rk, 8), (16,), 0, max(1, 128 // 4) + 1, jnp.int32)
        _ctx_4096P = jax.random.normal(jax.random.fold_in(_rk, 11), (16, 16, 1024), jnp.float32)
        _ctx_4096c = jax.random.dirichlet(jax.random.fold_in(_rk, 511), 0.3 * jnp.ones((16,), jnp.float32), (16, 128))
        _ctx_4096t = jnp.einsum('bsk,bkd->bsd', _ctx_4096c, _ctx_4096P)
        _ctx_4096t = _ctx_4096t * jax.lax.rsqrt(jnp.mean(jnp.square(_ctx_4096t)) + 1e-12) * 0.953939
        ctx_4096 = 2.81802e-05 + 1.00001 * (_ctx_4096t + 0.3 * jax.random.normal(jax.random.fold_in(_rk, 611), (16, 128, 1024), jnp.float32))
        return (x, ctx_4096)
    x, ctx_4096 = _rec_inputs()

    def _L0_xattn_setup():
        import jax, jax.numpy as jnp
        import numpy as np
        DIM = 128
        HEADS = 8
        DIM_HEAD = 64
        HIDDEN = HEADS * DIM_HEAD
        SCALE = DIM_HEAD ** (-0.5)
        key = jax.random.key(seed)
        ks = jax.random.split(key, 9)
        b, n = (8, 1024)
        std = 1.0 / np.sqrt(DIM)
        return {'q': jax.random.normal(ks[0], (b, DIM, n), jnp.float32), 'k': jax.random.normal(ks[1], (b, DIM, n), jnp.float32), 'v': jax.random.normal(ks[2], (b, DIM, n), jnp.float32), 'Wq': jax.random.normal(ks[3], (HIDDEN, DIM), jnp.float32) * std, 'Wk': jax.random.normal(ks[4], (HIDDEN, DIM), jnp.float32) * std, 'Wv': jax.random.normal(ks[5], (HIDDEN, DIM), jnp.float32) * std, 'Wo': jax.random.normal(ks[6], (DIM, HIDDEN), jnp.float32) * (1.0 / np.sqrt(HIDDEN)), 'bo': jax.random.normal(ks[7], (DIM,), jnp.float32) * 0.01, 'g': jnp.ones((1, DIM, 1), jnp.float32)}
    _L0_xattn_all = _L0_xattn_setup()
    _L0_xattn_in = {k: v for k, v in _L0_xattn_all.items() if k in ('Wq', 'Wk', 'Wv', 'Wo', 'bo', 'g')}
    del _L0_xattn_all

    def _L0_ffn_setup():
        import jax, jax.numpy as jnp
        import numpy as np
        HID, BOT, RDIM, NSLOT, K, VB = (1024, 64, 48, 256, 8, 64)
        TAU_LOW, TAU_HIGH, EARLY_EXIT = (0.5, 2.0, 0.05)

        def _uncertainty(h, Wu1, bu1, Wu2, bu2):
            var = jnp.var(h, axis=-1)
            log_var = jnp.log1p(var)
            norm_var = log_var / (jnp.mean(log_var) + 1e-06)
            learned = (jax.nn.gelu(h @ Wu1.T + bu1) @ Wu2.T + bu2)[..., 0]
            return jnp.clip(norm_var * 0.5 + jax.nn.sigmoid(learned) * 2.5, 0.0, 5.0)
        key = jax.random.key(seed)
        ks = jax.random.split(key, 12)
        B, S = (2, 512)
        return {'hidden_states': jax.random.normal(ks[0], (B, S, HID), dtype=jnp.float32), 'Wq': jax.random.normal(ks[1], (BOT, HID), dtype=jnp.float32) / np.sqrt(HID), 'Wr': jax.random.normal(ks[2], (RDIM, BOT), dtype=jnp.float32) / np.sqrt(BOT), 'aux_keys': jax.random.normal(ks[3], (NSLOT, BOT), dtype=jnp.float32) * 0.01, 'aux_values': jax.random.normal(ks[4], (NSLOT, HID), dtype=jnp.float32) * 0.02, 'Wvd': jax.random.normal(ks[5], (VB, HID), dtype=jnp.float32) * 0.1 / np.sqrt(HID), 'Wvu': jax.random.normal(ks[6], (HID, VB), dtype=jnp.float32) * 0.1 / np.sqrt(VB), 'Wu1': jax.random.normal(ks[7], (HID // 4, HID), dtype=jnp.float32) / np.sqrt(HID), 'bu1': jnp.zeros((HID // 4,), dtype=jnp.float32), 'Wu2': jax.random.normal(ks[8], (1, HID // 4), dtype=jnp.float32) * 0.01, 'bu2': jnp.zeros((1,), dtype=jnp.float32), 'gate_w1': jnp.float32(0.5), 'gate_bias': jnp.float32(-1.0), 'log_rel': jnp.zeros((NSLOT,), dtype=jnp.float32)}
    _L0_ffn_all = _L0_ffn_setup()
    _L0_ffn_in = {k: v for k, v in _L0_ffn_all.items() if k in ('Wq', 'Wr', 'aux_keys', 'aux_values', 'Wvd', 'Wvu', 'Wu1', 'bu1', 'Wu2', 'bu2', 'gate_w1', 'gate_bias', 'log_rel')}
    del _L0_ffn_all
    return {'x': x, 'ctx_4096': ctx_4096, 'L0_xattn_Wq': _L0_xattn_in['Wq'], 'L0_xattn_Wk': _L0_xattn_in['Wk'], 'L0_xattn_Wv': _L0_xattn_in['Wv'], 'L0_xattn_Wo': _L0_xattn_in['Wo'], 'L0_xattn_bo': _L0_xattn_in['bo'], 'L0_xattn_g': _L0_xattn_in['g'], 'L0_ffn_Wq': _L0_ffn_in['Wq'], 'L0_ffn_Wr': _L0_ffn_in['Wr'], 'L0_ffn_aux_keys': _L0_ffn_in['aux_keys'], 'L0_ffn_aux_values': _L0_ffn_in['aux_values'], 'L0_ffn_Wvd': _L0_ffn_in['Wvd'], 'L0_ffn_Wvu': _L0_ffn_in['Wvu'], 'L0_ffn_Wu1': _L0_ffn_in['Wu1'], 'L0_ffn_bu1': _L0_ffn_in['bu1'], 'L0_ffn_Wu2': _L0_ffn_in['Wu2'], 'L0_ffn_bu2': _L0_ffn_in['bu2'], 'L0_ffn_gate_w1': _L0_ffn_in['gate_w1'], 'L0_ffn_gate_bias': _L0_ffn_in['gate_bias'], 'L0_ffn_log_rel': _L0_ffn_in['log_rel']}

def reference(x, ctx_4096, L0_xattn_Wq, L0_xattn_Wk, L0_xattn_Wv, L0_xattn_Wo, L0_xattn_bo, L0_xattn_g, L0_ffn_Wq, L0_ffn_Wr, L0_ffn_aux_keys, L0_ffn_aux_values, L0_ffn_Wvd, L0_ffn_Wvu, L0_ffn_Wu1, L0_ffn_bu1, L0_ffn_Wu2, L0_ffn_bu2, L0_ffn_gate_w1, L0_ffn_gate_bias, L0_ffn_log_rel):
    import jax
    import jax.numpy as jnp

    def _L0_xattn_ref(q, k, v, Wq, Wk, Wv, Wo, bo, g):
        import jax, jax.numpy as jnp
        import numpy as np
        DIM = 128
        HEADS = 8
        DIM_HEAD = 64
        HIDDEN = HEADS * DIM_HEAD
        SCALE = DIM_HEAD ** (-0.5)
        b = q.shape[0]
        qh = jnp.einsum('bcn,oc->bon', q, Wq).reshape(b, HEADS, DIM_HEAD, -1)
        kh = jnp.einsum('bcn,oc->bon', k, Wk).reshape(b, HEADS, DIM_HEAD, -1)
        vh = jnp.einsum('bcn,oc->bon', v, Wv).reshape(b, HEADS, DIM_HEAD, -1)
        qh = jax.nn.softmax(qh, axis=-2) * SCALE
        kh = jax.nn.softmax(kh, axis=-1)
        context = jnp.einsum('bhdn,bhen->bhde', kh, vh)
        out = jnp.einsum('bhde,bhdn->bhen', context, qh)
        out = out.reshape(b, HIDDEN, -1)
        out = jnp.einsum('bcn,oc->bon', out, Wo) + bo[None, :, None]
        norm = jnp.maximum(jnp.sqrt(jnp.sum(out * out, axis=1, keepdims=True)), 1e-12)
        return out / norm * g * np.sqrt(DIM)

    def _L0_ffn_ref(hidden_states, Wq, Wr, aux_keys, aux_values, Wvd, Wvu, Wu1, bu1, Wu2, bu2, gate_w1, gate_bias, log_rel):
        import jax, jax.numpy as jnp
        import numpy as np
        HID, BOT, RDIM, NSLOT, K, VB = (1024, 64, 48, 256, 8, 64)
        TAU_LOW, TAU_HIGH, EARLY_EXIT = (0.5, 2.0, 0.05)

        def _uncertainty(h, Wu1, bu1, Wu2, bu2):
            var = jnp.var(h, axis=-1)
            log_var = jnp.log1p(var)
            norm_var = log_var / (jnp.mean(log_var) + 1e-06)
            learned = (jax.nn.gelu(h @ Wu1.T + bu1) @ Wu2.T + bu2)[..., 0]
            return jnp.clip(norm_var * 0.5 + jax.nn.sigmoid(learned) * 2.5, 0.0, 5.0)
        query = hidden_states @ Wq.T
        rq = query @ Wr.T
        rk = aux_keys @ Wr.T
        router_scores = jnp.einsum('bsr,nr->bsn', rq, rk) / np.sqrt(RDIM) + log_rel
        top_scores, top_idx = jax.lax.top_k(router_scores, K)
        sel_keys = aux_keys[top_idx]
        attn = jnp.einsum('bsd,bskd->bsk', query, sel_keys) / np.sqrt(BOT) + log_rel[top_idx]
        w = jax.nn.softmax(attn, axis=-1)
        sel_vals = aux_values[top_idx]
        aux_out = jnp.einsum('bsk,bskh->bsh', w, sel_vals)
        aux_out = aux_out @ Wvd.T @ Wvu.T
        u = _uncertainty(hidden_states, Wu1, bu1, Wu2, bu2)
        u_norm = jnp.clip((u - TAU_LOW) / (TAU_HIGH - TAU_LOW), 0.0, 1.0)
        gate = jax.nn.sigmoid(gate_w1 * u_norm + gate_bias)
        gate = jnp.where(gate < EARLY_EXIT, 0.0, gate)
        return hidden_states + gate[..., None] * aux_out
    x = x + _L0_xattn_ref(_layernorm(x, axis=-1), ctx_4096, ctx_4096, L0_xattn_Wq, L0_xattn_Wk, L0_xattn_Wv, L0_xattn_Wo, L0_xattn_bo, L0_xattn_g)
    x = x + _L0_ffn_ref(_layernorm(x, axis=-1), L0_ffn_Wq, L0_ffn_Wr, L0_ffn_aux_keys, L0_ffn_aux_values, L0_ffn_Wvd, L0_ffn_Wvu, L0_ffn_Wu1, L0_ffn_bu1, L0_ffn_Wu2, L0_ffn_bu2, L0_ffn_gate_w1, L0_ffn_gate_bias, L0_ffn_log_rel)
    return x

_drawn_inputs = setup_inputs


def setup_inputs(seed=0):
    import zlib

    import numpy as np

    out = dict(_drawn_inputs(seed))
    spreads = {'L0_xattn_g': (1.0, 0.2), 'L0_ffn_bu1': (0.0, 2.0), 'L0_ffn_log_rel': (0.0, 2.0)}
    factors = {'L0_ffn_Wq': 64.0,
     'L0_ffn_Wr': 64.0,
     'L0_ffn_aux_keys': 63.089,
     'L0_ffn_aux_values': 62.484,
     'L0_ffn_Wvd': 62.958,
     'L0_ffn_Wvu': 62.297,
     'L0_ffn_Wu1': 64.0,
     'L0_ffn_Wu2': 64.0}
    for name, (base, spread) in spreads.items():
        noise = np.random.default_rng([zlib.crc32(name.encode()), seed]).standard_normal(out[name].shape)
        drawn = base * np.exp(spread * noise) if base else spread * noise
        out[name] = jnp.asarray(drawn.astype(out[name].dtype))
    for name, factor in factors.items():
        out[name] = (out[name] * factor).astype(out[name].dtype)
    return out
```

```python
import concourse.bass as bass
from concourse import mybir
from contextlib import ExitStack

F32 = mybir.dt.float32
F32R = mybir.dt.float32r
ALU = mybir.AluOpType
ACT = mybir.ActivationFunctionType
AX = mybir.AxisListType.X

P = 128
B = 16
C = 128
N = 1024
H, DH = 8, 64
HD = H * DH
T = HD // P
DL = DH // T
J = N // P
HALF = N // 2
LN_EPS = 1e-5
NORM_FLOOR = 1e-24

BOT, RDIM, NSLOT, TOPK, VB = 64, 48, 256, 8, 64
UH = N // 4
G = 4
GT = G * C
NEG = -3.0e38
TAU_LOW, TAU_HIGH, EARLY_EXIT = 0.5, 2.0, 0.05


def wait(engine, sem, value):
    if isinstance(value, int) and value <= 0:
        return
    engine.wait_ge(sem, value)


def place(h):
    return (h % 2) * (H // 2) + h // 2


def attention_ffn_kernel(nc, x, ctx_4096, L0_xattn_Wq, L0_xattn_Wk, L0_xattn_Wv, L0_xattn_Wo, L0_xattn_bo,
                         L0_xattn_g, L0_ffn_Wq, L0_ffn_Wr, L0_ffn_aux_keys, L0_ffn_aux_values, L0_ffn_Wvd,
                         L0_ffn_Wvu, L0_ffn_Wu1, L0_ffn_bu1, L0_ffn_Wu2, L0_ffn_bu2, L0_ffn_gate_w1,
                         L0_ffn_gate_bias, L0_ffn_log_rel, identity, block_ones, select_q, select_r, out):
    ctx = ExitStack()
    with ctx:
        def sb(name, shape, dt=F32, scope=ctx):
            return scope.enter_context(nc.sbuf_tensor(name, shape, dt))

        def sem(name):
            return ctx.enter_context(nc.semaphore(name))

        X = sb("x_all", [P, B, N])
        ident = sb("ident", [P, P])
        ones = sb("ones", [P, P])
        var2 = sb("var2", [P, B, 1])
        mean2 = sb("mean2", [P, B, 1])

        def ps(name, shape):
            return ctx.enter_context(nc.psum_tensor(name, shape, F32))
        slot = [ps("slot0", [P, N]), ps("slot1", [P, N])]
        bcast = ps("bcast", [P, N])
        bank6 = ps("bank6", [P, 512])
        bank7 = ps("bank7", [P, 512])

        att = ExitStack()
        ctx_in = sb("ctx_in", [P, N], scope=att)
        ctx_hi = sb("ctx_hi", [P, N], F32R, att)
        ctx_lo = sb("ctx_lo", [P, N], F32R, att)
        xn = sb("xn", [P, N], scope=att)
        xn_hi = sb("xn_hi", [P, N], F32R, att)
        xn_lo = sb("xn_lo", [P, N], F32R, att)
        ctxT = sb("ctxT", [P, J, C], scope=att)
        ksb = sb("ksb", [P, J, HD], scope=att)
        qsb = sb("qsb", [P, T, N], scope=att)
        eq = sb("eq", [P, T, N], scope=att)
        qred = sb("qred", [P, N], scope=att)
        kred = sb("kred", [P, 2, HD], scope=att)
        WqT = [sb(f"WqT{s}", [P, HD], F32R, att) for s in ("_hi", "_lo")]
        WkT = [sb(f"WkT{s}", [P, HD], F32R, att) for s in ("_hi", "_lo")]
        U = sb("U", [P, H, C], scope=att)
        g_sb = sb("g_sb", [P, HD], scope=att)
        m_sb = sb("m_sb", [P, HD], scope=att)
        mt_sb = sb("mt_sb", [P, T, C], scope=att)
        o_sb = sb("o_sb", [P, N], scope=att)
        o_sq = sb("o_sq", [P, N], scope=att)
        sel_q = sb("sel_q", [P, J, P], F32R, att)
        sel_r = sb("sel_r", [2 * J, J, P], F32R, att)
        block1 = sb("block1", [P, H], scope=att)
        diag = sb("diag", [P, T, P], scope=att)
        qm = sb("qm", [P, J * H], scope=att)
        qm_hl = sb("qm_hl", [P, 2 * J * H], F32R, att)
        qmT = sb("qmT", [P, P], F32R, att)
        km = sb("km", [P, T], scope=att)
        krec = sb("krec", [P, T], scope=att)
        kscale = sb("kscale", [P, T], scope=att)
        l2c = sb("l2c", [P, J], scope=att)
        rn = sb("rn", [P, J], scope=att)
        rn_hl = sb("rn_hl", [P, 2 * J], F32R, att)
        rnT = sb("rnT", [2 * J, P], F32R, att)
        st1 = sb("st1", [P, 12], scope=att)
        st2 = sb("st2", [P, 12], scope=att)
        mv1 = sb("mv1", [P, 2], scope=att)
        mv2 = sb("mv2", [P, 2], scope=att)
        ve = sb("ve", [P, 1], scope=att)
        rstd = sb("rstd", [P, 1], scope=att)
        nb = sb("nb", [P, 1], scope=att)
        bo = sb("bo", [P, 1], scope=att)
        g_in = sb("g_in", [P, 1], scope=att)
        gs = sb("gs", [P, 1], scope=att)
        half_neg = sb("half_neg", [P, J], scope=att)
        Wq_in = qsb[:, 0, 0:HD].rearrange("p (t c) -> p t c", t=T)
        Wk_in = qsb[:, 0, HD:N].rearrange("p (t c) -> p t c", t=T)
        Wv_in = qsb[:, 1, 0:HD].rearrange("p (t c) -> p t c", t=T)
        Wo_in = qsb[:, 1, HD:N]
        WoT = qsb[:, 2, 0:HD].rearrange("p (t c) -> p t c", t=T)
        selq_in = eq[:, 0, :].rearrange("p (j q) -> p j q", j=J)
        selr_in = eq[0:2 * J, 1, :].rearrange("p (j q) -> p j q", j=J)
        att.close()

        ffn = ExitStack()
        Wu1_in = sb("Wu1_in", [P, UH // P, N], scope=ffn)
        Wqf_in = sb("Wqf_in", [BOT, N], scope=ffn)
        Wvd_in = sb("Wvd_in", [VB, N], scope=ffn)
        values_in = sb("values_in", [P, NSLOT // P, N], scope=ffn)
        Wvu_in = sb("Wvu_in", [P, J, VB], scope=ffn)
        keys_in = sb("keys_in", [P, NSLOT // P, BOT], scope=ffn)
        Wr_in = sb("Wr_in", [RDIM, BOT], scope=ffn)
        Wu1T = [sb(f"Wu1T{s}", [P, J, UH], F32R, ffn) for s in ("_hi", "_lo")]
        WqfT = [sb(f"WqfT{s}", [P, J, BOT], F32R, ffn) for s in ("_hi", "_lo")]
        WvdT = sb("WvdT", [P, J, VB], scope=ffn)
        valuesT = sb("valuesT", [P, J, NSLOT], scope=ffn)
        WvuT = sb("WvuT", [VB, N], scope=ffn)
        WrT = sb("WrT", [BOT, RDIM], scope=ffn)
        keysT = sb("keysT", [BOT, NSLOT], scope=ffn)
        rkT = sb("rkT", [RDIM, NSLOT], scope=ffn)
        VV = sb("VV", [P, NSLOT // P, VB], scope=ffn)
        scoreB = sb("scoreB", [BOT + 1, 2 * NSLOT], scope=ffn)
        bu1 = sb("bu1", [P, UH // P], scope=ffn)
        Wu2 = sb("Wu2", [P, UH // P], scope=ffn)
        bu2 = sb("bu2", [P, 1], scope=ffn)
        gate_w = sb("gate_w", [P, 1], scope=ffn)
        gate_b = sb("gate_b", [P, 1], scope=ffn)
        half3 = sb("half3", [P, 3], scope=ffn)
        half_neg2 = sb("half_neg2", [P, B], scope=ffn)
        ve2 = sb("ve2", [P, B], scope=ffn)
        rstd2 = sb("rstd2", [P, B, 1], scope=ffn)
        nb2 = sb("nb2", [P, B, 1], scope=ffn)
        varh = sb("varh", [P, B], scope=ffn)
        logv = sb("logv", [P, B], scope=ffn)
        logsum = sb("logsum", [P, 1], scope=ffn)
        logmean = sb("logmean", [P, 1], scope=ffn)
        logrec = sb("logrec", [P, 1], scope=ffn)
        normv = sb("normv", [P, B // G, G], scope=ffn)
        hbuf = sb("hbuf", [P, 2, N], scope=ffn)
        hT = [sb(f"hT{s}", [P, J, GT], F32R, ffn) for s in ("_hi", "_lo")]
        units = sb("units", [P, UH // P, GT], scope=ffn)
        query = sb("query", [BOT + 1, GT], scope=ffn)
        top8 = sb("top8", [P, TOPK], scope=ffn)
        replaced = sb("replaced", [P, NSLOT], scope=ffn)
        outside = sb("outside", [P, NSLOT], scope=ffn)
        logits = sb("logits", [P, NSLOT], scope=ffn)
        nlmax = sb("nlmax", [P, 1], scope=ffn)
        w_sb = sb("w_sb", [P, NSLOT], scope=ffn)
        wsum = sb("wsum", [P, G], scope=ffn)
        wrec = sb("wrec", [P, 1], scope=ffn)
        oscale = sb("oscale", [P, 1], scope=ffn)
        wT = sb("wT", [P, NSLOT // P, C], scope=ffn)
        zT = sb("zT", [VB, C], scope=ffn)
        ga = sb("ga", [P, G], scope=ffn)
        gb = sb("gb", [P, G], scope=ffn)
        gate = sb("gate", [P, G], scope=ffn)
        y_out = sb("y_out", [P, 2, N], scope=ffn)
        ffn.close()

        weights_in = sem("weights_in")
        waits_apart = sem("waits_apart")
        x_in = sem("x_in")
        ctx_loaded = sem("ctx_loaded")
        consts = sem("consts")
        setup_T = sem("setup_T")
        setup_w = sem("setup_w")
        setup_u = sem("setup_u")
        u_done = sem("u_done")
        x_split = sem("x_split")
        x_norm = sem("x_norm")
        x_stats = sem("x_stats")
        x_mv = sem("x_mv")
        x_ve = sem("x_ve")
        x_rstd = sem("x_rstd")
        x_nb = sem("x_nb")
        x_hi = sem("x_hi")
        ctx_hi_done = sem("ctx_hi_done")
        ctx_lo_done = sem("ctx_lo_done")
        q_prod = sem("q_prod")
        q_evac = sem("q_evac")
        k_prod = sem("k_prod")
        k_evac = sem("k_evac")
        qmax_step = sem("qmax_step")
        qmax_T = sem("qmax_T")
        qm_done = sem("qm_done")
        qm_hi_done = sem("qm_hi_done")
        qm_split = sem("qm_split")
        qm_T = sem("qm_T")
        qmT_copied = sem("qmT_copied")
        qshift = sem("qshift")
        q_sub = sem("q_sub")
        q_exp = sem("q_exp")
        qsum_step = sem("qsum_step")
        q_sum = sem("q_sum")
        k_sum = sem("k_sum")
        qrec = sem("qrec")
        qr_hi_done = sem("qr_hi_done")
        qr_split = sem("qr_split")
        qr_T = sem("qr_T")
        qrT_copied = sem("qrT_copied")
        q_rbc = sem("q_rbc")
        q_mul = sem("q_mul")
        kmax_step = sem("kmax_step")
        kmax_T = sem("kmax_T")
        km_done = sem("km_done")
        diag_done = sem("diag_done")
        kshift = sem("kshift")
        k_sub = sem("k_sub")
        k_exp = sem("k_exp")
        ksum_step = sem("ksum_step")
        krec_done = sem("krec_done")
        kscale_done = sem("kscale_done")
        ctxT_prod = sem("ctxT_prod")
        ctxT_copied = sem("ctxT_copied")
        g_prod = sem("g_prod")
        g_copied = sem("g_copied")
        m_prod = sem("m_prod")
        m_copied = sem("m_copied")
        mt_T = sem("mt_T")
        mt_copied = sem("mt_copied")
        out_prod = sem("out_prod")
        o_copied = sem("o_copied")
        o_squared = sem("o_squared")
        ss_prod = sem("ss_prod")
        l2_clamped = sem("l2_clamped")
        rn_pow = sem("rn_pow")
        rn_hi_done = sem("rn_hi_done")
        rn_split = sem("rn_split")
        rn_T = sem("rn_T")
        rnT_copied = sem("rnT_copied")
        rn_bc = sem("rn_bc")
        t_mul = sem("t_mul")
        x1_done = sem("x1_done")
        stats2 = sem("stats2")
        mv2_done = sem("mv2_done")
        var2_done = sem("var2_done")
        ffn_in = sem("ffn_in")
        out_stored = sem("out_stored")
        ffn_consts = sem("ffn_consts")
        wu1_T = sem("wu1_T")
        wu1_split = sem("wu1_split")
        wq_T = sem("wq_T")
        wq_split = sem("wq_split")
        val_T = sem("val_T")
        val_copied = sem("val_copied")
        vv_prod = sem("vv_prod")
        vv_copied = sem("vv_copied")
        key_T = sem("key_T")
        key_copied = sem("key_copied")
        rk_prod = sem("rk_prod")
        rk_copied = sem("rk_copied")
        b1_prod = sem("b1_prod")
        score_ready = sem("score_ready")
        ve2_done = sem("ve2_done")
        rstd2_done = sem("rstd2_done")
        nb2_done = sem("nb2_done")
        varh_step = sem("varh_step")
        logv_done = sem("logv_done")
        logsum_done = sem("logsum_done")
        logtotal = sem("logtotal")
        normv_step = sem("normv_step")
        h_done = sem("h_done")
        y_done = sem("y_done")
        h_T = sem("h_T")
        hT_hi_done = sem("hT_hi_done")
        hT_lo_done = sem("hT_lo_done")
        units_prod = sem("units_prod")
        units_done = sem("units_done")
        query_prod = sem("query_prod")
        query_done = sem("query_done")
        learned = sem("learned")
        gate_tanh = sem("gate_tanh")
        gate_step = sem("gate_step")
        gate_arg = sem("gate_arg")
        gate_done = sem("gate_done")
        scores = sem("scores")
        select_step = sem("select_step")
        logits_ready = sem("logits_ready")
        w_done = sem("w_done")
        w_T = sem("w_T")
        wT_copied = sem("wT_copied")
        z_prod = sem("z_prod")
        z_copied = sem("z_copied")
        f_prod = sem("f_prod")
        wrec_done = sem("wrec_done")
        oscale_done = sem("oscale_done")
        y_ready = sem("y_ready")
        masked = sem("masked")

        block = ctx.enter_context(nc.Block())

        ATT_DMAS, FFN_DMAS = 10, 14

        def wait_apart(engine, sem, value):
            wait(engine, sem, value)
            engine.sem_inc(waits_apart, 1)

        @block.sync
        def _(sp):
            for src, dst in ((L0_xattn_Wq, Wq_in), (L0_xattn_Wk, Wk_in), (L0_xattn_Wv, Wv_in)):
                sp.dma_start(dst, src.rearrange("(t p) c -> p t c", p=P)).then_inc(weights_in, 16)
            sp.dma_start(Wo_in, L0_xattn_Wo).then_inc(weights_in, 16)
            sp.dma_start(ident[:, :], identity).then_inc(weights_in, 16)
            sp.dma_start(block1[:, :], block_ones).then_inc(weights_in, 16)
            sp.dma_start(selq_in, select_q).then_inc(weights_in, 16)
            sp.dma_start(selr_in, select_r).then_inc(weights_in, 16)
            sp.dma_start(bo[:, :], L0_xattn_bo).then_inc(weights_in, 16)
            sp.dma_start(g_in[:, :], L0_xattn_g).then_inc(weights_in, 16)

            def load(b):
                wait_apart(sp, x_in, 16 * b)
                sp.dma_start(X[:, b, :], x[b]).then_inc(x_in, 16)
                wait_apart(sp, ctx_hi_done, b)
                wait_apart(sp, ctx_lo_done, b)
                wait_apart(sp, ctxT_prod, b)
                sp.dma_start(ctx_in[:, :], ctx_4096[b]).then_inc(ctx_loaded, 16)

            load(0)
            with sp.Fori(1, B) as b:
                load(b)

            sp.wait_ge(var2_done, 2 * B)
            sp.wait_ge(ksum_step, 4 * B)
            for src, dst in (
                (L0_ffn_Wu1.rearrange("(s p) n -> p s n", p=P), Wu1_in[:, :, :]),
                (L0_ffn_Wq, Wqf_in[:, :]),
                (L0_ffn_Wvd, Wvd_in[:, :]),
                (L0_ffn_aux_values.rearrange("(s p) n -> p s n", p=P), values_in[:, :, :]),
                (L0_ffn_Wvu.rearrange("(j p) v -> p j v", p=P), Wvu_in[:, :, :]),
                (L0_ffn_aux_keys.rearrange("(s p) d -> p s d", p=P), keys_in[:, :, :]),
                (L0_ffn_Wr, Wr_in[:, :]),
                (L0_ffn_log_rel, scoreB[BOT:BOT + 1, 0:NSLOT]),
                (L0_ffn_log_rel, scoreB[BOT:BOT + 1, NSLOT:2 * NSLOT]),
                (L0_ffn_bu1, bu1[:, :]),
                (L0_ffn_Wu2, Wu2[:, :]),
                (L0_ffn_bu2.broadcast_to([P, 1]), bu2[:, :]),
                (L0_ffn_gate_w1.broadcast_to([P, 1]), gate_w[:, :]),
                (L0_ffn_gate_bias.broadcast_to([P, 1]), gate_b[:, :]),
            ):
                sp.dma_start(dst, src).then_inc(ffn_in, 16)

            def store(b, k):
                wait_apart(sp, out_stored, 16 * b)
                wait_apart(sp, y_ready, b + 1)
                sp.dma_start(out[b], y_out[:, k % 2, :]).then_inc(out_stored, 16)

            for k in range(G):
                store(k, k)
            with sp.Fori(1, B // G) as g:
                for k in range(G):
                    store(g * G + k, k)
            sp.wait_ge(out_stored, 16 * B)

        @block.tensor
        def _(pe):
            pe.wait_ge(weights_in, 16 * ATT_DMAS)
            for dst, src in ((bank6, Wq_in), (bank7, Wk_in), (bcast, Wo_in.rearrange("p (t c) -> p t c", t=T))):
                for t in range(T):
                    last = nc.tensor.transpose(dst[:, t * P:(t + 1) * P], src[:, t, :], ident[:, :])
                last.then_inc(setup_T, 1)
            pe.wait_ge(setup_w, 1)
            for h in range(H):
                r = DH * (h % 2)
                last = nc.tensor.matmul(slot[0][:, place(h) * C:(place(h) + 1) * C], Wv_in[r:r + DH, h // 2, :],
                                        WoT[r:r + DH, h // 2, :], start=True, stop=True)
            last.then_inc(setup_u, 1)

            def product(dst, lhs, rhs):
                nc.tensor.matmul(dst, lhs[0], rhs[0], start=True, stop=False)
                nc.tensor.matmul(dst, lhs[1], rhs[0], start=False, stop=False)
                return nc.tensor.matmul(dst, lhs[0], rhs[1], start=False, stop=True)

            def q_tile(b, t):
                for n in range(2):
                    cols = slice(n * HALF, (n + 1) * HALF)
                    last = product(slot[t % 2][:, cols], [w[:, t * P:(t + 1) * P] for w in WqT],
                                   [xn_hi[:, cols], xn_lo[:, cols]])
                last.then_inc(q_prod, 1)

            def k_pair(b, u):
                for j in range(2):
                    cols = slice((2 * u + j) * P, (2 * u + j + 1) * P)
                    last = product(slot[u % 2][:, j * HD:(j + 1) * HD], [ctx_hi[:, cols], ctx_lo[:, cols]],
                                   [w[:, :] for w in WkT])
                last.then_inc(k_prod, 1)

            def r_transpose(b):
                pe.wait_ge(qr_split, b + 1)
                nc.tensor.transpose(bcast[:, 0:P], qm_hl[:, :].bitcast(F32), ident[:, :]).then_inc(qr_T, 1)

            def spread(src, done):
                for j in range(J):
                    last = nc.tensor.matmul(bcast[:, j * P:(j + 1) * P], sel_q[:, j, :], src[:, :],
                                            start=True, stop=True)
                last.then_inc(done, 1)

            def m_product(b):
                pe.wait_ge(g_copied, b + 1)
                pe.wait_ge(k_sub, 2 * (b + 1))
                gv = g_sb[:, :].rearrange("p (t h d) -> p t h d", t=T, h=H)
                mv = bank6[:, :].rearrange("p (t h d) -> p t h d", t=T, h=H)
                for h in range(H):
                    last = nc.tensor.matmul(mv[:, :, h, :], U[:, place(h), :], gv[:, :, h, :], start=True, stop=True)
                last.then_inc(m_prod, 1)

            def mt_transpose(b):
                pe.wait_ge(m_copied, b + 1)
                pe.wait_ge(g_copied, b + 1)
                for t in range(T):
                    last = nc.tensor.transpose(bank7[:, t * P:(t + 1) * P], m_sb[:, t * P:(t + 1) * P], ident[:, :])
                last.then_inc(mt_T, 1)

            def out_half(b, n):
                pe.wait_ge(q_mul, 2 * b + n + 1)
                pe.wait_ge(mt_copied, b + 1)
                dst = (bank6, bank7)[n]
                for t in range(T):
                    last = nc.tensor.matmul(dst[:, :], mt_sb[:, t, :], eq[:, t, n * HALF:(n + 1) * HALF],
                                            start=(t == 0), stop=(t == T - 1))
                last.then_inc(out_prod, 1)

            def early(b, first, last_one):
                p = b - 1
                if not last_one:
                    pe.wait_ge(x_split, b + 1)
                    wait(pe, ctxT_copied, b)
                    wait(pe, qm_done, b)
                    if first != 0:
                        if first == 2:
                            wait(pe, t_mul, b - 1)
                    q_tile(b, 0)
                if first:
                    r_transpose(p)
                    m_product(p)
                if not last_one:
                    q_tile(b, 1)
                if first:
                    pe.wait_ge(qrT_copied, p + 1)
                    spread(qmT, q_rbc)
                    mt_transpose(p)
                if not last_one:
                    pe.wait_ge(q_evac, 4 * b + 1)
                    q_tile(b, 2)
                    pe.wait_ge(q_evac, 4 * b + 2)
                    q_tile(b, 3)
                    pe.wait_ge(ctx_hi_done, b + 1)
                    pe.wait_ge(ctx_lo_done, b + 1)
                    for u in range(4):
                        if u < 2:
                            pe.wait_ge(q_evac, 4 * b + 3 + u)
                        else:
                            pe.wait_ge(k_evac, 4 * b + u - 1)
                        k_pair(b, u)
                    pe.wait_ge(k_evac, 4 * b + 3)
                    pe.wait_ge(qmax_step, 3 * (b + 1))
                    for j in range(J):
                        last = nc.tensor.transpose(slot[0][:, j * P:(j + 1) * P], qred[:, j * P:(j + 1) * P],
                                                   ident[:, :])
                    last.then_inc(qmax_T, 1)
                if first:
                    out_half(p, 0)
                if not last_one:
                    pe.wait_ge(qm_split, b + 1)
                    wait(pe, q_mul, 2 * b)
                    nc.tensor.transpose(bcast[:, 0:P], qm_hl[:, :].bitcast(F32), ident[:, :]).then_inc(qm_T, 1)
                if first:
                    out_half(p, 1)

            def late(b, first, last_one):
                p = b - 1
                if not last_one:
                    pe.wait_ge(qmT_copied, b + 1)
                    spread(qmT, qshift)
                    pe.wait_ge(kmax_step, 4 * (b + 1))
                    if first:
                        pe.wait_ge(o_copied, 2 * b - 1)
                    for t in range(T):
                        last = nc.tensor.transpose(bank6[:, t * P:(t + 1) * P], kred[:, 0, t * P:(t + 1) * P],
                                                   ident[:, :])
                    last.then_inc(kmax_T, 1)
                if first:
                    pe.wait_ge(o_squared, 2 * b)
                    for j in range(J):
                        last = nc.tensor.matmul(bank7[:, j:j + 1], o_sq[:, j * P:(j + 1) * P], ones[:, 0:1],
                                                start=True, stop=True)
                    last.then_inc(ss_prod, 1)
                if not last_one:
                    pe.wait_ge(k_evac, 4 * b + 4)
                    for j in range(J):
                        last = nc.tensor.transpose(slot[1][:, j * P:(j + 1) * P], ctx_in[:, j * P:(j + 1) * P],
                                                   ident[:, :])
                    last.then_inc(ctxT_prod, 1)
                    pe.wait_ge(diag_done, b + 1)
                    nc.tensor.matmul(bank6[:, :], ones[:, :], diag[:, :, :].rearrange("p t c -> p (t c)"),
                                     start=True, stop=True).then_inc(kshift, 1)
                if first:
                    pe.wait_ge(rn_split, p + 1)
                    nc.tensor.transpose(bank7[0:2 * J, 0:P], rn_hl[:, :].bitcast(F32), ident[:, :]).then_inc(rn_T, 1)
                    pe.wait_ge(rnT_copied, p + 1)
                    if not last_one:
                        pe.wait_ge(qm_done, b + 1)
                    for j in range(J):
                        last = nc.tensor.matmul(slot[0][:, j * P:(j + 1) * P], sel_r[:, j, :], rnT[:, :],
                                                start=True, stop=True)
                    last.then_inc(rn_bc, 1)
                if not last_one:
                    pe.wait_ge(ctxT_copied, b + 1)
                    for j in range(J):
                        if j % 4 == 0:
                            pe.wait_ge(k_exp, 2 * b + 1 + j // 4)
                        last = nc.tensor.matmul(bank7[:, :], ctxT[:, j, :], ksb[:, j, :],
                                                start=(j == 0), stop=(j == J - 1))
                    last.then_inc(g_prod, 1)
                    pe.wait_ge(q_sub, 2 * (b + 1))
                    pe.wait_ge(qsum_step, 6 * (b + 1))
                    for j in range(J):
                        last = nc.tensor.matmul(bcast[:, j * H:(j + 1) * H], qred[:, j * P:(j + 1) * P],
                                                block1[:, :], start=True, stop=True)
                    last.then_inc(q_sum, 1)
                    pe.wait_ge(ksum_step, 4 * (b + 1))
                    for t in range(T):
                        last = nc.tensor.matmul(bcast[:, HALF + t:HALF + t + 1], kred[:, 0, t * P:(t + 1) * P],
                                                ones[:, 0:1], start=True, stop=True)
                    last.then_inc(k_sum, 1)

            pe.wait_ge(u_done, 1)
            early(0, 0, False)
            late(0, 0, False)
            early(1, 1, False)
            late(1, 1, False)
            with pe.Fori(2, B) as b:
                early(b, 2, False)
                late(b, 2, False)
            early(B, 2, True)
            late(B, 2, True)

            pe.wait_ge(ffn_in, 16 * FFN_DMAS)
            pe.wait_ge(var2_done, 2 * B)
            def wide_T(src, done, base, freed):
                for j in range(J):
                    if j == J // 2 and freed is not None:
                        pe.wait_ge(*freed)
                    for s in range(2):
                        last = nc.tensor.transpose(
                            slot[j // 4][:, (j % 4) * UH + s * P:(j % 4) * UH + (s + 1) * P],
                            src[:, s, j * P:(j + 1) * P], ident[:, :])
                    if j % 4 == 3:
                        last.then_inc(done, 1)
            wide_T(Wu1_in, wu1_T, 0, None)
            for j in range(J):
                nc.tensor.transpose(bcast[:, j * BOT:(j + 1) * BOT], Wqf_in[:, j * P:(j + 1) * P],
                                    ident[0:BOT, 0:BOT])
            for j in range(J):
                last = nc.tensor.transpose(bcast[:, HALF + j * VB:HALF + (j + 1) * VB],
                                           Wvd_in[:, j * P:(j + 1) * P], ident[0:VB, 0:VB])
            last.then_inc(wq_T, 1)
            for s in range(2):
                nc.tensor.transpose(bank6[0:BOT, s * P:(s + 1) * P], keys_in[:, s, :], ident[:, :])
            nc.tensor.transpose(bank6[0:BOT, NSLOT:NSLOT + RDIM], Wr_in[:, :],
                                ident[0:RDIM, 0:RDIM]).then_inc(key_T, 1)
            pe.wait_ge(wu1_split, 4)
            wide_T(values_in, val_T, 0, None)
            pe.wait_ge(wq_split, 3)
            for j in range(J):
                last = nc.tensor.transpose(bcast[0:VB, j * P:(j + 1) * P], Wvu_in[:, j, :], ident[:, :])
            last.then_inc(wq_T, 1)
            pe.wait_ge(key_copied, 2)
            nc.tensor.matmul(bank7[0:RDIM, 0:NSLOT], WrT[:, :], keysT[:, :], start=True, stop=True).then_inc(rk_prod, 1)
            pe.wait_ge(rk_copied, 1)
            nc.tensor.matmul(bank6[0:BOT, 0:NSLOT], Wr_in[:, :], rkT[:, :], start=True, stop=True).then_inc(b1_prod, 1)
            pe.wait_ge(val_copied, 2)
            for s in range(NSLOT // P):
                for j in range(J):
                    last = nc.tensor.matmul(bank7[:, s * VB:(s + 1) * VB], valuesT[:, j, s * P:(s + 1) * P],
                                            WvdT[:, j, :], start=(j == 0), stop=(j == J - 1))
            last.then_inc(vv_prod, 1)
            pe.wait_ge(logsum_done, 1)
            pe.wait_ge(score_ready, 4)
            nc.tensor.matmul(bank6[:, 0:1], ones[:, :], logsum[:, :], start=True, stop=True).then_inc(logtotal, 1)
            pe.wait_ge(vv_copied, 1)
            pe.wait_ge(normv_step, 4)

            def h_transpose(b, k):
                pe.wait_ge(h_done, b + 1)
                wait(pe, hT_hi_done, b)
                wait(pe, hT_lo_done, b)
                for j in range(J):
                    last = nc.tensor.transpose(slot[1][:, j * P:(j + 1) * P], hbuf[:, k % 2, j * P:(j + 1) * P],
                                               ident[:, :])
                last.then_inc(h_T, 1)

            def group_products(g):
                pe.wait_ge(hT_lo_done, G * (g + 1))
                wait(pe, z_copied, G * g)
                for s in range(UH // P):
                    dst = (bank6, bank7)[s]
                    for j in range(J):
                        lhs = [w[:, j, s * P:(s + 1) * P] for w in Wu1T]
                        rhs = [h[:, j, :] for h in hT]
                        for n, (a, c) in enumerate(((0, 0), (1, 0), (0, 1))):
                            last = nc.tensor.matmul(dst[:, :], lhs[a], rhs[c], start=(j == 0 and n == 0),
                                                    stop=(j == J - 1 and n == 2))
                    last.then_inc(units_prod, 1)
                wait(pe, gate_tanh, 2 * g)
                for j in range(J):
                    for n, (a, c) in enumerate(((0, 0), (1, 0), (0, 1))):
                        last = nc.tensor.matmul(bcast[0:BOT, 0:GT], WqfT[a][:, j, :], hT[c][:, j, :],
                                                start=(j == 0 and n == 0), stop=(j == J - 1 and n == 2))
                last.then_inc(query_prod, 1)

            def score(b, k):
                wait(pe, logits_ready, b)
                nc.tensor.matmul(bcast[:, GT:2 * GT], query[:, k * C:(k + 1) * C], scoreB[:, :],
                                 start=True, stop=True).then_inc(scores, 1)

            def group_tail(g, more):
                pe.wait_ge(query_done, g + 1)
                score(g * G, 0)
                pe.wait_ge(units_done, 2 * (g + 1))
                for k in range(G):
                    for s in range(UH // P):
                        last = nc.tensor.matmul(bcast[:, k:k + 1], units[:, s, k * C:(k + 1) * C], Wu2[:, s:s + 1],
                                                start=(s == 0), stop=(s == UH // P - 1))
                last.then_inc(learned, 1)
                for k in range(G):
                    b = g * G + k
                    if k < G - 1:
                        score(b + 1, k + 1)
                    pe.wait_ge(w_done, b + 1)
                    for s in range(NSLOT // P):
                        last = nc.tensor.transpose(bank6[:, s * C:(s + 1) * C], w_sb[:, s * P:(s + 1) * P],
                                                   ident[:, :])
                    last.then_inc(w_T, 1)
                    pe.wait_ge(wT_copied, b + 1)
                    for s in range(NSLOT // P):
                        last = nc.tensor.matmul(bank7[0:VB, 0:C], VV[:, s, :], wT[:, s, :],
                                                start=(s == 0), stop=(s == NSLOT // P - 1))
                    last.then_inc(z_prod, 1)
                    if more:
                        h_transpose(b + G, k)
                    pe.wait_ge(z_copied, b + 1)
                    wait(pe, y_ready, b)
                    for n in range(2):
                        last = nc.tensor.matmul(slot[0][:, n * HALF:(n + 1) * HALF], zT[:, :],
                                                WvuT[:, n * HALF:(n + 1) * HALF], start=True, stop=True)
                    last.then_inc(f_prod, 1)

            for k in range(G):
                h_transpose(k, k)
            group_products(0)
            group_tail(0, True)
            group_products(1)
            with pe.Fori(1, B // G - 1) as g:
                group_tail(g, True)
                group_products(g + 1)
            group_tail(B // G - 1, False)

        @block.scalar
        def _(act):
            def prepare(b):
                act.wait_ge(ctx_loaded, 16 * (b + 1))
                wait(act, k_prod, 4 * b)
                nc.scalar.copy(ctx_hi[:, :], ctx_in[:, :]).then_inc(ctx_hi_done, 1)
                act.wait_ge(x_in, 16 * (b + 1))
                act.wait_ge(x_rstd, b + 1)
                act.wait_ge(x_nb, b + 1)
                wait(act, x_split, b)
                nc.scalar.activation(xn[:, :], X[:, b, :], ACT.Identity, bias=nb[:, :],
                                     scale=rstd[:, :]).then_inc(x_norm, 1)

            def out_evac(p):
                for n in range(2):
                    cols = slice(n * HALF, (n + 1) * HALF)
                    act.wait_ge(out_prod, 2 * p + n + 1)
                    wait(act, x1_done, p)
                    nc.scalar.activation(o_sb[:, cols], (bank6, bank7)[n][:, :], ACT.Identity,
                                         bias=bo[:, :]).then_inc(o_copied, 1)
                    act.wait_ge(o_copied, 2 * p + n + 1)
                    wait(act, ss_prod, p)
                    nc.scalar.activation(o_sq[:, cols], o_sb[:, cols], ACT.Square).then_inc(o_squared, 1)

            def body(b, first):
                for t in range(T):
                    act.wait_ge(q_prod, 4 * b + t + 1)
                    wait(act, q_exp, 2 * b)
                    nc.scalar.copy(qsb[:, t, :], slot[t % 2][:, :]).then_inc(q_evac, 1)
                for u in range(4):
                    act.wait_ge(k_prod, 4 * b + u + 1)
                    wait(act, g_prod, b)
                    wait(act, ksum_step, 4 * b)
                    nc.scalar.copy(ksb[:, 2 * u:2 * u + 2, :].rearrange("p j d -> p (j d)"),
                                   slot[u % 2][:, :]).then_inc(k_evac, 1)
                if first:
                    out_evac(b - 1)
                act.wait_ge(ctxT_prod, b + 1)
                nc.scalar.copy(ctxT[:, :, :].rearrange("p j c -> p (j c)"), slot[1][:, :]).then_inc(ctxT_copied, 1)
                for n in range(2):
                    cols = slice(n * HALF, (n + 1) * HALF)
                    act.wait_ge(q_sub, 2 * b + n + 1)
                    wait(act, out_prod, 2 * b)
                    nc.scalar.activation(eq[:, :, cols], qsb[:, :, cols], ACT.Exp).then_inc(q_exp, 1)
                for n in range(2):
                    act.wait_ge(k_sub, 2 * b + n + 1)
                    kk = ksb[:, 4 * n:4 * n + 4, :]
                    nc.scalar.activation(kk, kk, ACT.Exp).then_inc(k_exp, 1)

            act.wait_ge(weights_in, 16 * ATT_DMAS)
            prepare(0)
            act.wait_ge(setup_w, 6)
            act.wait_ge(u_done, 1)
            body(0, False)
            prepare(1)
            body(1, True)
            prepare(2)
            with act.Fori(2, B - 1) as b:
                body(b, True)
                prepare(b + 1)
            body(B - 1, True)
            out_evac(B - 1)

            act.wait_ge(varh_step, 2)
            nc.scalar.activation(logv[:, :], varh[:, :], ACT.Ln, bias=ones[:, 0:1]).then_inc(logv_done, 1)

            def hT_high(b, k):
                act.wait_ge(h_T, b + 1)
                nc.scalar.copy(hT[0][:, :, k * C:(k + 1) * C],
                               slot[1][:, :].rearrange("p (j c) -> p j c", j=J)).then_inc(hT_hi_done, 1)

            def group_units(g):
                wait(act, learned, g)
                for s in range(UH // P):
                    act.wait_ge(units_prod, 2 * g + s + 1)
                    nc.scalar.activation(units[:, s, :], (bank6, bank7)[s][:, :], ACT.Gelu_apprx_tanh,
                                         bias=bu1[:, s:s + 1]).then_inc(units_done, 1)

            def group_rest(g, more):
                for k in range(G):
                    b = g * G + k
                    act.wait_ge(logits_ready, b + 1)
                    wait(act, w_T, b)
                    if k == 0:
                        wait(act, oscale_done, b)
                    nc.scalar.activation(w_sb[:, :], logits[:, :], ACT.Exp, bias=nlmax[:, :],
                                         accum_out=wsum[:, k:k + 1]).then_inc(w_done, 1)
                    if k == 0:
                        act.wait_ge(learned, g + 1)
                        wait(act, gate_done, g)
                        nc.scalar.activation(ga[:, :], bcast[:, 0:G], ACT.Tanh, bias=half3[:, 0:1],
                                             scale=0.5).then_inc(gate_tanh, 1)
                    act.wait_ge(w_T, b + 1)
                    wait(act, z_prod, b)
                    nc.scalar.copy(wT[:, :, :].rearrange("p s c -> p (s c)"), bank6[:, 0:NSLOT]).then_inc(wT_copied, 1)
                    if k == 0:
                        act.wait_ge(gate_arg, g + 1)
                        nc.scalar.activation(gb[:, :], ga[:, :], ACT.Tanh, bias=half3[:, 2:3],
                                             scale=half3[:, 1:2]).then_inc(gate_tanh, 1)
                    act.wait_ge(z_prod, b + 1)
                    wait(act, f_prod, b)
                    nc.scalar.copy(zT[:, :], bank7[0:VB, 0:C]).then_inc(z_copied, 1)
                    if more:
                        act.wait_ge(h_T, b + G + 1)
                        if k == 0:
                            act.wait_ge(query_prod, g + 1)
                        nc.scalar.copy(hT[0][:, :, k * C:(k + 1) * C],
                                       slot[1][:, :].rearrange("p (j c) -> p j c", j=J)).then_inc(hT_hi_done, 1)

            act.wait_ge(ffn_in, 16 * FFN_DMAS)
            for k in range(G):
                hT_high(k, k)
            group_units(0)
            act.wait_ge(normv_step, 4)
            group_rest(0, True)
            group_units(1)
            with act.Fori(1, B // G - 1) as g:
                group_rest(g, True)
                group_units(g + 1)
            group_rest(B // G - 1, False)

        @block.gpsimd
        def _(pool):
            nc.gpsimd.memset(ones[:, :], 1.0).then_inc(consts, 1)
            nc.gpsimd.memset(half_neg[:, :], -0.5).then_inc(consts, 1)
            pool.wait_ge(consts, 2)

            def chain(done, base, ops):
                for s, (dst, a, c, sem_in, val) in enumerate(ops):
                    pool.wait_ge(sem_in, val)
                    if s:
                        pool.wait_ge(done, base + s)
                    nc.gpsimd.tensor_tensor(dst, a, c, ALU.add).then_inc(done, 1)

            def split(b):
                pool.wait_ge(ctx_hi_done, b + 1)
                nc.gpsimd.tensor_tensor(ctx_lo[:, :], ctx_in[:, :], ctx_hi[:, :].bitcast(F32),
                                        ALU.subtract).then_inc(ctx_lo_done, 1)
                pool.wait_ge(x_hi, b + 1)
                nc.gpsimd.tensor_tensor(xn_lo[:, :], xn[:, :], xn_hi[:, :].bitcast(F32),
                                        ALU.subtract).then_inc(x_split, 1)

            def rstd_pow(b):
                pool.wait_ge(x_ve, b + 1)
                wait(pool, x_norm, b)
                wait(pool, x_nb, b)
                nc.gpsimd.tensor_tensor(rstd[:, :], ve[:, :], half_neg[:, 0:1], ALU.pow).then_inc(x_rstd, 1)

            def norm_pow(b):
                pool.wait_ge(l2_clamped, b + 1)
                wait(pool, rn_split, b)
                nc.gpsimd.tensor_tensor(rn[:, :], l2c[:, :], half_neg[:, :], ALU.pow).then_inc(rn_pow, 1)

            def sums(b):
                pool.wait_ge(qmax_T, b + 1)
                for n in range(2):
                    cols = slice(n * HALF, (n + 1) * HALF)
                    e = [eq[:, t, cols] for t in range(T)]
                    r = qred[:, cols]
                    chain(qsum_step, 6 * b + 3 * n, [
                        (r, e[0], e[1], q_exp, 2 * b + n + 1),
                        (r, r, e[2], q_exp, 2 * b + n + 1),
                        (r, r, e[3], q_exp, 2 * b + n + 1)])
                pool.wait_ge(kmax_T, b + 1)
                k = [ksb[:, 2 * u:2 * u + 2, :] for u in range(4)]
                r = kred[:, :, :]
                chain(ksum_step, 4 * b, [
                    (r, k[0], k[1], k_exp, 2 * b + 1),
                    (r, r, k[2], k_exp, 2 * b + 2),
                    (r, r, k[3], k_exp, 2 * b + 2),
                    (kred[:, 0, :], kred[:, 0, :], kred[:, 1, :], k_exp, 2 * b + 2)])

            rstd_pow(0)
            split(0)
            rstd_pow(1)
            sums(0)
            split(1)
            def body(b):
                rstd_pow(b + 1)
                norm_pow(b - 1)
                sums(b)
                split(b + 1)

            body(1)
            with pool.Fori(2, B - 1) as b:
                body(b)
            norm_pow(B - 2)
            sums(B - 1)
            norm_pow(B - 1)

            pool.wait_ge(var2_done, 2 * B)
            nc.gpsimd.memset(half_neg2[:, :], -0.5).then_inc(ffn_consts, 1)
            pool.wait_ge(ffn_consts, 1)
            nc.gpsimd.memset(query[BOT:BOT + 1, :], 1.0).then_inc(ffn_consts, 1)
            pool.wait_ge(ve2_done, 1)
            pool.wait_ge(ffn_consts, 2)
            nc.gpsimd.tensor_tensor(rstd2[:, :, 0], ve2[:, :], half_neg2[:, :], ALU.pow).then_inc(rstd2_done, 1)

            def add_h(b, k):
                pool.wait_ge(h_done, b + 1)
                nc.gpsimd.tensor_tensor(X[:, b, :], X[:, b, :], hbuf[:, k % 2, :], ALU.add).then_inc(y_done, 1)

            for k in range(G):
                add_h(k, k)
            with pool.Fori(1, B // G) as g:
                for k in range(G):
                    add_h(g * G + k, k)

        @block.vector
        def _(dve):
            V = nc.vector

            def x_statistics(b):
                dve.wait_ge(x_in, 16 * (b + 1))
                wait_apart(dve, x_norm, b)
                for s in range(2):
                    V.bn_stats(st1[:, 6 * s:6 * s + 6], X[:, b, s * HALF:(s + 1) * HALF]).then_inc(x_stats, 1)
                wait_apart(dve, x_stats, 2 * (b + 1))
                V.bn_aggr(mv1[:, :], st1[:, :]).then_inc(x_mv, 1)
                dve.wait_ge(x_mv, b + 1)
                V.tensor_scalar_add(ve[:, :], mv1[:, 1:2], LN_EPS).then_inc(x_ve, 1)

            def x_bias(b):
                dve.wait_ge(x_rstd, b + 1)
                V.scalar_tensor_tensor(nb[:, :], mv1[:, 0:1], -1.0, rstd[:, :], ALU.mult,
                                       ALU.mult).then_inc(x_nb, 1)

            def x_high(b):
                dve.wait_ge(x_norm, b + 1)
                wait(dve, q_prod, 4 * b)
                wait(dve, x_split, b)
                V.tensor_copy(xn_hi[:, :], xn[:, :]).then_inc(x_hi, 1)

            def two_parts(b, hl, src, n, hi_done, done):
                V.tensor_copy(hl[:, 0:n], src).then_inc(hi_done, 1)
                dve.wait_ge(hi_done, b + 1)
                V.tensor_tensor(hl[:, n:2 * n], src, hl[:, 0:n].bitcast(F32), ALU.subtract).then_inc(done, 1)

            def finish_softmax(p):
                dve.wait_ge(k_sum, p + 1)
                V.reciprocal(qm[:, :], bcast[:, 0:J * H]).then_inc(qrec, 1)
                V.reciprocal(krec[:, :], bcast[:, HALF:HALF + T]).then_inc(krec_done, 1)
                dve.wait_ge(qrec, p + 1)
                two_parts(p, qm_hl, qm[:, :], J * H, qr_hi_done, qr_split)
                dve.wait_ge(krec_done, p + 1)
                V.tensor_scalar_mul(kscale[:, :], krec[:, :], float(DH) ** -0.5).then_inc(kscale_done, 1)
                dve.wait_ge(g_prod, p + 1)
                V.tensor_copy(g_sb[:, :], bank7[:, :]).then_inc(g_copied, 1)
                dve.wait_ge(qr_T, p + 1)
                V.tensor_copy(qmT[:, :], bcast[:, 0:P]).then_inc(qrT_copied, 1)
                dve.wait_ge(m_prod, p + 1)
                V.tensor_copy(m_sb[:, :], bank6[:, :]).then_inc(m_copied, 1)
                dve.wait_ge(mt_T, p + 1)
                wait(dve, out_prod, 2 * p)
                dve.wait_ge(kscale_done, p + 1)
                V.tensor_tensor(mt_sb[:, :, :], bank7[:, :].rearrange("p (t c) -> p t c", t=T),
                                kscale[:, :].unsqueeze(2).broadcast_to([P, T, C]), ALU.mult).then_inc(mt_copied, 1)

            def q_scale(p, n):
                cols = slice(n * HALF, (n + 1) * HALF)
                dve.wait_ge(q_rbc, p + 1)
                V.tensor_tensor(eq[:, :, cols], eq[:, :, cols],
                                bcast[:, cols].unsqueeze(1).broadcast_to([P, T, HALF]),
                                ALU.mult).then_inc(q_mul, 1)

            def max_chain(done, base, ops):
                for s, (dst, a, c, sem_in, val) in enumerate(ops):
                    dve.wait_ge(sem_in, val)
                    if s:
                        dve.wait_ge(done, base + s)
                    V.tensor_tensor(dst, a, c, ALU.max).then_inc(done, 1)

            def q_tile_max(b):
                wait(dve, q_sum, b)
                q = [qsb[:, t, :] for t in range(T)]
                r = qred[:, :]
                max_chain(qmax_step, 3 * b, [(r, q[0], q[1], q_evac, 4 * b + 2), (r, r, q[2], q_evac, 4 * b + 3),
                                             (r, r, q[3], q_evac, 4 * b + 4)])

            def k_block_max(b):
                wait(dve, k_sum, b)
                k = [ksb[:, 2 * u:2 * u + 2, :] for u in range(4)]
                r = kred[:, :, :]
                max_chain(kmax_step, 4 * b, [(r, k[0], k[1], k_evac, 4 * b + 2), (r, r, k[2], k_evac, 4 * b + 3),
                                             (r, r, k[3], k_evac, 4 * b + 4),
                                             (kred[:, 0, :], kred[:, 0, :], kred[:, 1, :], k_evac, 4 * b + 4)])

            def maxima(b):
                dve.wait_ge(qmax_T, b + 1)
                V.tensor_reduce(qm[:, :], slot[0][:, :].rearrange("p (m d) -> p m d", d=DL), AX,
                                ALU.max).then_inc(qm_done, 1)
                dve.wait_ge(qm_done, b + 1)
                two_parts(b, qm_hl, qm[:, :], J * H, qm_hi_done, qm_split)
                dve.wait_ge(qm_T, b + 1)
                V.tensor_copy(qmT[:, :], bcast[:, 0:P]).then_inc(qmT_copied, 1)

            def shifts(b):
                dve.wait_ge(qshift, b + 1)
                def q_half(n):
                    cols = slice(n * HALF, (n + 1) * HALF)
                    V.tensor_tensor(qsb[:, :, cols], qsb[:, :, cols],
                                    bcast[:, cols].unsqueeze(1).broadcast_to([P, T, HALF]),
                                    ALU.subtract).then_inc(q_sub, 1)
                q_half(0)
                dve.wait_ge(kmax_T, b + 1)
                V.tensor_reduce(km[:, :], bank6[:, :].rearrange("p (t c) -> p t c", t=T), AX,
                                ALU.max).then_inc(km_done, 1)
                dve.wait_ge(km_done, b + 1)
                V.tensor_tensor(diag[:, :, :], ident[:, :].unsqueeze(1).broadcast_to([P, T, P]),
                                km[:, :].unsqueeze(2).broadcast_to([P, T, P]), ALU.mult).then_inc(diag_done, 1)
                q_half(1)

            def k_shift(b):
                dve.wait_ge(kshift, b + 1)
                for n in range(2):
                    kk = ksb[:, 4 * n:4 * n + 4, :]
                    V.tensor_tensor(kk, kk, bank6[:, :].unsqueeze(1).broadcast_to([P, 4, HD]),
                                    ALU.subtract).then_inc(k_sub, 1)

            def norm_clamp(p):
                dve.wait_ge(ss_prod, p + 1)
                V.tensor_scalar_max(l2c[:, :], bank7[:, 0:J], NORM_FLOOR).then_inc(l2_clamped, 1)

            def norm_spread(p):
                dve.wait_ge(rn_pow, p + 1)
                two_parts(p, rn_hl, rn[:, :], J, rn_hi_done, rn_split)
                dve.wait_ge(rn_T, p + 1)
                V.tensor_copy(rnT[:, :], bank7[0:2 * J, 0:P]).then_inc(rnT_copied, 1)

            def residual(p):
                dve.wait_ge(rn_bc, p + 1)
                V.tensor_tensor(o_sb[:, :], o_sb[:, :], slot[0][:, :], ALU.mult).then_inc(t_mul, 1)
                dve.wait_ge(t_mul, p + 1)
                V.scalar_tensor_tensor(X[:, p, :], o_sb[:, :], gs[:, :], X[:, p, :], ALU.mult,
                                       ALU.add).then_inc(x1_done, 1)
                wait_apart(dve, x1_done, p + 1)
                for s in range(2):
                    V.bn_stats(st2[:, 6 * s:6 * s + 6], X[:, p, s * HALF:(s + 1) * HALF]).then_inc(stats2, 1)
                dve.wait_ge(stats2, 2 * (p + 1))
                wait_apart(dve, var2_done, 2 * p)
                V.bn_aggr(mv2[:, :], st2[:, :]).then_inc(mv2_done, 1)
                dve.wait_ge(mv2_done, p + 1)
                V.tensor_copy(mean2[:, p, :], mv2[:, 0:1]).then_inc(var2_done, 1)
                V.tensor_copy(var2[:, p, :], mv2[:, 1:2]).then_inc(var2_done, 1)

            def body(b, first, last_one):
                if first:
                    finish_softmax(b - 1)
                    q_scale(b - 1, 0)
                q_tile_max(b)
                if first:
                    q_scale(b - 1, 1)
                k_block_max(b)
                maxima(b)
                if not last_one:
                    x_statistics(b + 1)
                shifts(b)
                if not last_one:
                    x_bias(b + 1)
                if first:
                    norm_clamp(b - 1)
                k_shift(b)
                if first:
                    norm_spread(b - 1)
                    residual(b - 1)
                if not last_one:
                    x_high(b + 1)

            dve.wait_ge(weights_in, 16 * ATT_DMAS)
            V.tensor_scalar_mul(gs[:, :], g_in[:, :], float(C) ** 0.5)
            dve.wait_ge(setup_T, 3)
            V.tensor_copy(WoT, bcast[:, 0:HD].rearrange("p (t c) -> p t c", t=T)).then_inc(setup_w, 1)
            for n, (parts, src) in enumerate(((WqT, bank6), (WkT, bank7))):
                hi, lo = [w[:, :].rearrange("p (t h d) -> p h t d", t=T, h=H) for w in parts]
                v = src[:, :].rearrange("p (h t d) -> p h t d", t=T, h=H)
                V.tensor_copy(hi, v).then_inc(setup_w, 1)
                dve.wait_ge(setup_w, 2 + 2 * n)
                V.tensor_tensor(lo, v, hi.bitcast(F32), ALU.subtract).then_inc(setup_w, 1)
            V.tensor_copy(sel_q[:, :, :], selq_in)
            V.tensor_copy(sel_r[:, :, :], selr_in).then_inc(setup_w, 1)
            x_statistics(0)
            x_bias(0)
            x_high(0)
            dve.wait_ge(setup_u, 1)
            V.tensor_copy(U[:, :, :].rearrange("p h c -> p (h c)"), slot[0][:, :]).then_inc(u_done, 1)

            body(0, False, False)
            body(1, True, False)
            with dve.Fori(2, B - 1) as b:
                body(b, True, False)
            body(B - 1, True, True)
            finish_softmax(B - 1)
            q_scale(B - 1, 0)
            q_scale(B - 1, 1)
            norm_clamp(B - 1)
            norm_spread(B - 1)
            residual(B - 1)

            dve.wait_ge(var2_done, 2 * B)
            V.tensor_scalar_add(ve2[:, :], var2[:, :, 0], LN_EPS).then_inc(ve2_done, 1)
            dve.wait_ge(rstd2_done, 1)
            V.scalar_tensor_tensor(nb2[:, :, 0], mean2[:, :, 0], -1.0, rstd2[:, :, 0], ALU.mult,
                                   ALU.mult).then_inc(nb2_done, 1)
            V.tensor_tensor(varh[:, :], var2[:, :, 0], rstd2[:, :, 0], ALU.mult).then_inc(varh_step, 1)
            dve.wait_ge(varh_step, 1)
            V.tensor_tensor(varh[:, :], varh[:, :], rstd2[:, :, 0], ALU.mult).then_inc(varh_step, 1)
            dve.wait_ge(logv_done, 1)
            V.reduce_sum(logsum[:, :], logv[:, :], AX).then_inc(logsum_done, 1)

            def h_scale(b, k):
                dve.wait_ge(nb2_done, 1)
                wait(dve, h_T, b - 1)
                wait(dve, y_done, b - 1)
                V.tensor_scalar(hbuf[:, k % 2, :], X[:, b, :], rstd2[:, b, :], nb2[:, b, :], ALU.mult,
                                ALU.add).then_inc(h_done, 1)

            def hT_low(b, k):
                dve.wait_ge(hT_hi_done, b + 1)
                cols = slice(k * C, (k + 1) * C)
                V.tensor_tensor(hT[1][:, :, cols], slot[1][:, :].rearrange("p (j c) -> p j c", j=J),
                                hT[0][:, :, cols].bitcast(F32), ALU.subtract).then_inc(hT_lo_done, 1)

            h_scale(0, 0)
            h_scale(1, 1)
            for n in range(2):
                dve.wait_ge(wu1_T, n + 1)
                hi, lo = [w[:, 4 * n:4 * n + 4, :].rearrange("p j u -> p (j u)") for w in Wu1T]
                V.tensor_copy(hi, slot[n][:, :]).then_inc(wu1_split, 1)
                dve.wait_ge(wu1_split, 2 * n + 1)
                V.tensor_tensor(lo, slot[n][:, :], hi.bitcast(F32), ALU.subtract).then_inc(wu1_split, 1)
            dve.wait_ge(wq_T, 1)
            hi, lo = [w[:, :, :].rearrange("p j d -> p (j d)") for w in WqfT]
            V.tensor_copy(hi, bcast[:, 0:HALF]).then_inc(wq_split, 1)
            dve.wait_ge(wq_split, 1)
            V.tensor_tensor(lo, bcast[:, 0:HALF], hi.bitcast(F32), ALU.subtract).then_inc(wq_split, 1)
            V.tensor_copy(WvdT[:, :, :].rearrange("p j d -> p (j d)"), bcast[:, HALF:N]).then_inc(wq_split, 1)
            dve.wait_ge(key_T, 1)
            V.tensor_copy(keysT[:, :], bank6[0:BOT, 0:NSLOT]).then_inc(key_copied, 1)
            V.tensor_copy(WrT[:, :], bank6[0:BOT, NSLOT:NSLOT + RDIM]).then_inc(key_copied, 1)
            dve.wait_ge(rk_prod, 1)
            V.tensor_copy(rkT[:, :], bank7[0:RDIM, 0:NSLOT]).then_inc(rk_copied, 1)
            for n in range(2):
                dve.wait_ge(val_T, n + 1)
                V.tensor_copy(valuesT[:, 4 * n:4 * n + 4, :].rearrange("p j u -> p (j u)"),
                              slot[n][:, :]).then_inc(val_copied, 1)
            dve.wait_ge(wq_T, 2)
            V.tensor_copy(WvuT[:, :], bcast[0:VB, :]).then_inc(score_ready, 1)
            dve.wait_ge(ffn_in, 16 * FFN_DMAS)
            V.tensor_scalar_mul(scoreB[0:BOT, NSLOT:2 * NSLOT], keysT[:, :], float(BOT) ** -0.5).then_inc(score_ready, 1)
            dve.wait_ge(b1_prod, 1)
            V.tensor_scalar_mul(scoreB[0:BOT, 0:NSLOT], bank6[0:BOT, 0:NSLOT], float(RDIM) ** -0.5).then_inc(score_ready, 1)
            for n, src in enumerate((bu2, gate_w, gate_b)):
                last = V.tensor_scalar_mul(half3[:, n:n + 1], src[:, :], 0.5)
            last.then_inc(score_ready, 1)
            dve.wait_ge(vv_prod, 1)
            V.tensor_copy(VV[:, :, :].rearrange("p s d -> p (s d)"), bank7[:, 0:2 * VB]).then_inc(vv_copied, 1)
            dve.wait_ge(logtotal, 1)
            V.tensor_scalar(logmean[:, :], bank6[:, 0:1], 1.0 / (B * C), 1e-6, ALU.mult, ALU.add).then_inc(normv_step, 1)
            dve.wait_ge(normv_step, 1)
            V.reciprocal(logrec[:, :], logmean[:, :]).then_inc(normv_step, 1)
            dve.wait_ge(normv_step, 2)
            V.tensor_scalar(varh[:, :], logv[:, :], logrec[:, :], 0.5, ALU.mult, ALU.mult).then_inc(normv_step, 1)
            dve.wait_ge(normv_step, 3)
            V.tensor_scalar_add(normv[:, :, :].rearrange("p g k -> p (g k)"), varh[:, :], 1.25).then_inc(normv_step, 1)

            def select(b, k):
                s0 = 3 * b
                dve.wait_ge(scores, b + 1)
                wait(dve, w_done, b)
                wait_apart(dve, select_step, s0)
                V.max(top8[:, :], bcast[:, GT:GT + NSLOT]).then_inc(select_step, 1)
                wait_apart(dve, select_step, s0 + 1)
                V.match_replace(replaced[:, :], top8[:, :], bcast[:, GT:GT + NSLOT], NEG).then_inc(select_step, 1)
                dve.wait_ge(select_step, s0 + 2)
                V.tensor_tensor(outside[:, :], replaced[:, :], bcast[:, GT:GT + NSLOT],
                                ALU.is_equal).then_inc(select_step, 1)
                dve.wait_ge(select_step, s0 + 3)
                V.scalar_tensor_tensor(logits[:, :], outside[:, :], NEG, bcast[:, GT + NSLOT:2 * GT], ALU.mult,
                                       ALU.add).then_inc(masked, 1)
                dve.wait_ge(masked, b + 1)
                V.tensor_reduce(nlmax[:, :], logits[:, :], AX, ALU.max, negate=True).then_inc(logits_ready, 1)

            def gate_first(g):
                s0 = 4 * g
                dve.wait_ge(gate_tanh, 2 * g + 1)
                V.scalar_tensor_tensor(gate[:, :], ga[:, :], 1.25, normv[:, g, :], ALU.mult, ALU.add).then_inc(gate_step, 1)
                dve.wait_ge(gate_step, s0 + 1)
                V.tensor_scalar(ga[:, :], gate[:, :], 0.0, 5.0, ALU.max, ALU.min).then_inc(gate_step, 1)
                dve.wait_ge(gate_step, s0 + 2)
                V.tensor_scalar(gate[:, :], ga[:, :], -TAU_LOW, 1.0 / (TAU_HIGH - TAU_LOW), ALU.add,
                                ALU.mult).then_inc(gate_step, 1)
                dve.wait_ge(gate_step, s0 + 3)
                V.tensor_scalar(ga[:, :], gate[:, :], 0.0, 1.0, ALU.max, ALU.min).then_inc(gate_arg, 1)

            def gate_second(g):
                dve.wait_ge(gate_tanh, 2 * g + 2)
                V.tensor_scalar(ga[:, :], gb[:, :], 0.5, 0.5, ALU.mult, ALU.add).then_inc(gate_step, 1)
                dve.wait_ge(gate_step, 4 * g + 4)
                V.scalar_tensor_tensor(gate[:, :], ga[:, :], EARLY_EXIT, ga[:, :], ALU.is_ge, ALU.mult).then_inc(gate_done, 1)

            def finish(b, k):
                V.reciprocal(wrec[:, :], wsum[:, k:k + 1]).then_inc(wrec_done, 1)
                dve.wait_ge(wrec_done, b + 1)
                wait(dve, y_ready, b)
                V.tensor_tensor(oscale[:, :], wrec[:, :], gate[:, k:k + 1], ALU.mult).then_inc(oscale_done, 1)
                dve.wait_ge(oscale_done, b + 1)
                dve.wait_ge(f_prod, b + 1)
                dve.wait_ge(y_done, b + 1)
                wait(dve, out_stored, 16 * (b - 1))
                V.scalar_tensor_tensor(y_out[:, k % 2, :], slot[0][:, :], oscale[:, :], X[:, b, :], ALU.mult,
                                       ALU.add).then_inc(y_ready, 1)

            def group(g, more):
                dve.wait_ge(query_prod, g + 1)
                V.tensor_copy(query[0:BOT, :], bcast[0:BOT, 0:GT]).then_inc(query_done, 1)
                for k in range(G):
                    b = g * G + k
                    select(b, k)
                    if more:
                        h_scale(b + G, k)
                    if k == 0:
                        gate_first(g)
                        gate_second(g)
                    if more:
                        hT_low(b + G, k)
                    dve.wait_ge(w_done, b + 1)
                    finish(b, k)

            hT_low(0, 0)
            h_scale(2, 2)
            hT_low(1, 1)
            h_scale(3, 3)
            hT_low(2, 2)
            hT_low(3, 3)
            group(0, True)
            with dve.Fori(1, B // G - 1) as g:
                group(g, True)
            group(B // G - 1, False)


def constants():
    import numpy as np
    block_ones = (np.arange(P)[:, None] // DL == np.arange(H)[None]).astype(np.float32)
    select_q = np.zeros((2, J, H, J, H, DL), np.float32)
    select_r = np.zeros((2, J, J, P), np.float32)
    for j in range(J):
        select_r[:, j, j] = 1
        for h in range(H):
            select_q[:, j, h, j, h] = 1
    return {"identity": np.eye(P, dtype=np.float32), "block_ones": block_ones,
            "select_q": select_q.reshape(2 * J * H, J, P), "select_r": select_r.reshape(2 * J, J, P)}


INPUTS = ["x", "ctx_4096", "L0_xattn_Wq", "L0_xattn_Wk", "L0_xattn_Wv", "L0_xattn_Wo", "L0_xattn_bo", "L0_xattn_g",
          "L0_ffn_Wq", "L0_ffn_Wr", "L0_ffn_aux_keys", "L0_ffn_aux_values", "L0_ffn_Wvd", "L0_ffn_Wvu",
          "L0_ffn_Wu1", "L0_ffn_bu1", "L0_ffn_Wu2", "L0_ffn_bu2", "L0_ffn_gate_w1", "L0_ffn_gate_bias",
          "L0_ffn_log_rel"]


def layout(name, a):
    if name in ("L0_xattn_bo", "L0_xattn_g"):
        return a.reshape(C, 1)
    if name in ("L0_ffn_bu1", "L0_ffn_Wu2"):
        return a.reshape(UH // P, P).T
    if name in ("L0_ffn_bu2", "L0_ffn_gate_w1", "L0_ffn_gate_bias", "L0_ffn_log_rel"):
        return a.reshape(1, -1)
    return a


def kernel(**inputs):
    import numpy as np
    import concourse.bacc as bacc
    from concourse.bass_utils import run_bass_kernel_spmd

    nc = bacc.Bacc("TRN2", target_bir_lowering=False, num_devices=1)
    arrays = {n: np.ascontiguousarray(layout(n, np.asarray(inputs[n]))) for n in INPUTS} | constants()
    aps = {n: nc.dram_tensor(n, a.shape, mybir.dt.from_np(a.dtype), kind="ExternalInput").ap()
           for n, a in arrays.items()}
    out = nc.dram_tensor("out", (B, C, N), F32, kind="ExternalOutput").ap()
    attention_ffn_kernel(nc, out=out, **aps)
    r = run_bass_kernel_spmd(nc, [arrays], core_ids=[0])
    return r.results[0]["out"]
```

```python
import concourse.bass as bass
from concourse import mybir
from contextlib import ExitStack

F32 = mybir.dt.float32
F32R = mybir.dt.float32r
ALU = mybir.AluOpType
ACT = mybir.ActivationFunctionType
AX = mybir.AxisListType.X

P = 128
B = 16
C = 128
N = 1024
H, DH = 8, 64
HD = H * DH
T = HD // P
DL = DH // T
J = N // P
HALF = N // 2
LN_EPS = 1e-5
NORM_FLOOR = 1e-24

BOT, RDIM, NSLOT, TOPK, VB = 64, 48, 256, 8, 64
UH = N // 4
G = 4
GT = G * C
NEG = -3.0e38
TAU_LOW, TAU_HIGH, EARLY_EXIT = 0.5, 2.0, 0.05


def wait(engine, sem, value):
    if isinstance(value, int) and value <= 0:
        return
    engine.wait_ge(sem, value)


def place(h):
    return (h % 2) * (H // 2) + h // 2


def attention_ffn_kernel(nc, x, ctx_4096, L0_xattn_Wq, L0_xattn_Wk, L0_xattn_Wv, L0_xattn_Wo, L0_xattn_bo,
                         L0_xattn_g, L0_ffn_Wq, L0_ffn_Wr, L0_ffn_aux_keys, L0_ffn_aux_values, L0_ffn_Wvd,
                         L0_ffn_Wvu, L0_ffn_Wu1, L0_ffn_bu1, L0_ffn_Wu2, L0_ffn_bu2, L0_ffn_gate_w1,
                         L0_ffn_gate_bias, L0_ffn_log_rel, identity, head_ones, select_q, out):
    ctx = ExitStack()
    with ctx:
        def sb(name, shape, dt=F32, scope=ctx):
            return scope.enter_context(nc.sbuf_tensor(name, shape, dt))

        def sem(name):
            return ctx.enter_context(nc.semaphore(name))

        X = sb("x_all", [P, B, N])
        ident = sb("ident", [P, P])
        ones = sb("ones", [P, P])
        var2 = sb("var2", [P, B, 1])
        mean2 = sb("mean2", [P, B, 1])

        def ps(name, shape):
            return ctx.enter_context(nc.psum_tensor(name, shape, F32))
        slot = [ps("slot0", [P, N]), ps("slot1", [P, N])]
        bcast = ps("bcast", [P, N])
        work = ps("work", [P, N])
        bank6, bank7 = work[:, 0:HALF], work[:, HALF:N]
        bank_q, bank_g = bcast[:, 0:HALF], bcast[:, HALF:N]

        NS = 1
        k_slot = [slot[0], slot[1], slot[1], slot[1]]

        att = ExitStack()
        ctx_in = sb("ctx_in", [P, N], scope=att)
        ctx_hi = sb("ctx_hi", [P, N], F32R, att)
        ctx_lo = sb("ctx_lo", [P, N], F32R, att)
        xn = sb("xn", [P, N], scope=att)
        xn_hi = sb("xn_hi", [P, N], F32R, att)
        xn_lo = sb("xn_lo", [P, N], F32R, att)
        ctxT = sb("ctxT", [P, J, C], scope=att)
        ek = sb("ek", [P, 2, N], scope=att)
        ekT = sb("ekT", [P, J, HD], scope=att)
        qsb = sb("qsb", [P, T, N], scope=att)
        eq = sb("eq", [P, T, N], scope=att)
        qred = sb("qred", [P, N], scope=att)
        qtot = sb("qtot", [P, N], scope=att)
        WqT = [sb(f"WqT{s}", [P, HD], F32R, att) for s in ("_hi", "_lo")]
        WkT = [sb(f"WkT{s}", [P, HD], F32R, att) for s in ("_hi", "_lo")]
        U = sb("U", [P, H, C], scope=att)
        g_sb = sb("g_sb", [P, HD], scope=att)
        m_sb = sb("m_sb", [P, HD], scope=att)
        mt_sb = sb("mt_sb", [P, T, C], scope=att)
        o_sb = sb("o_sb", [P, N], scope=att)
        r_sb = sb("r_sb", [P, N], scope=att)
        sq_sb = sb("sq_sb", [P, N], scope=att)
        t_sb = sb("t_sb", [P, N], scope=att)
        l2c = sb("l2c", [P, J], scope=att)
        rn = sb("rn", [P, J], scope=att)
        rn_hl = sb("rn_hl", [P, 2 * J * H], F32R, att)
        rnT = sb("rnT", [P, P], F32R, att)
        sel_q = sb("sel_q", [P, J, P], F32R, att)
        same_head = sb("same_head", [P, P], scope=att)
        qm = sb("qm", [P, J * H], scope=att)
        qm_hl = sb("qm_hl", [P, 2 * J * H], F32R, att)
        qmT = sb("qmT", [P, P], F32R, att)
        nkm = sb("nkm", [P, T], scope=att)
        ksum = sb("ksum", [P, T], scope=att)
        krec = sb("krec", [P, T], scope=att)
        kscale = sb("kscale", [P, T], scope=att)
        st1 = sb("st1", [P, 12], scope=att)
        st2 = sb("st2", [P, 12], scope=att)
        mv1 = sb("mv1", [P, 2], scope=att)
        mv2 = sb("mv2", [P, 2], scope=att)
        ve = sb("ve", [P, 1], scope=att)
        rstd = sb("rstd", [P, 1], scope=att)
        nb = sb("nb", [P, 1], scope=att)
        bo = sb("bo", [P, 1], scope=att)
        g_in = sb("g_in", [P, 1], scope=att)
        gs = sb("gs", [P, 1], scope=att)
        half_neg = sb("half_neg", [P, J], scope=att)
        Wq_in = qsb[:, 0, 0:HD].rearrange("p (t c) -> p t c", t=T)
        Wk_in = qsb[:, 0, HD:N].rearrange("p (t c) -> p t c", t=T)
        Wv_in = qsb[:, 1, 0:HD].rearrange("p (t c) -> p t c", t=T)
        Wo_in = qsb[:, 1, HD:N]
        WoT = qsb[:, 2, 0:HD].rearrange("p (t c) -> p t c", t=T)
        selq_in = eq[:, 0, :].rearrange("p (j q) -> p j q", j=J)
        att.close()

        ffn = ExitStack()
        Wu1_in = sb("Wu1_in", [P, UH // P, N], scope=ffn)
        Wqf_in = sb("Wqf_in", [BOT, N], scope=ffn)
        Wvd_in = sb("Wvd_in", [VB, N], scope=ffn)
        values_in = sb("values_in", [P, NSLOT // P, N], scope=ffn)
        Wvu_in = sb("Wvu_in", [P, J, VB], scope=ffn)
        keys_in = sb("keys_in", [P, NSLOT // P, BOT], scope=ffn)
        Wr_in = sb("Wr_in", [RDIM, BOT], scope=ffn)
        Wu1T = [sb(f"Wu1T{s}", [P, J, UH], F32R, ffn) for s in ("_hi", "_lo")]
        WqfT = [sb(f"WqfT{s}", [P, J, BOT], F32R, ffn) for s in ("_hi", "_lo")]
        WvdT = sb("WvdT", [P, J, VB], scope=ffn)
        valuesT = sb("valuesT", [P, J, NSLOT], scope=ffn)
        WvuT = sb("WvuT", [VB, N], scope=ffn)
        WrT = sb("WrT", [BOT, RDIM], scope=ffn)
        keysT = sb("keysT", [BOT, NSLOT], scope=ffn)
        rkT = sb("rkT", [RDIM, NSLOT], scope=ffn)
        VV = sb("VV", [P, NSLOT // P, VB], scope=ffn)
        scoreB = sb("scoreB", [BOT + 1, 2 * NSLOT], scope=ffn)
        bu1 = sb("bu1", [P, UH // P], scope=ffn)
        Wu2 = sb("Wu2", [P, UH // P], scope=ffn)
        bu2 = sb("bu2", [P, 1], scope=ffn)
        gate_w = sb("gate_w", [P, 1], scope=ffn)
        gate_b = sb("gate_b", [P, 1], scope=ffn)
        half3 = sb("half3", [P, 3], scope=ffn)
        half_neg2 = sb("half_neg2", [P, B], scope=ffn)
        ve2 = sb("ve2", [P, B], scope=ffn)
        rstd2 = sb("rstd2", [P, B, 1], scope=ffn)
        nb2 = sb("nb2", [P, B, 1], scope=ffn)
        varh = sb("varh", [P, B], scope=ffn)
        logv = sb("logv", [P, B], scope=ffn)
        logsum = sb("logsum", [P, 1], scope=ffn)
        logmean = sb("logmean", [P, 1], scope=ffn)
        logrec = sb("logrec", [P, 1], scope=ffn)
        normv = sb("normv", [P, B // G, G], scope=ffn)
        hbuf = sb("hbuf", [P, 2, N], scope=ffn)
        hT = [sb(f"hT{s}", [P, J, GT], F32R, ffn) for s in ("_hi", "_lo")]
        units = sb("units", [P, UH // P, GT], scope=ffn)
        query = sb("query", [BOT + 1, GT], scope=ffn)
        top8 = sb("top8", [P, TOPK], scope=ffn)
        replaced = sb("replaced", [P, NSLOT], scope=ffn)
        outside = sb("outside", [P, NSLOT], scope=ffn)
        logits = sb("logits", [P, NSLOT], scope=ffn)
        nlmax = sb("nlmax", [P, 1], scope=ffn)
        w_sb = sb("w_sb", [P, NSLOT], scope=ffn)
        wsum = sb("wsum", [P, G], scope=ffn)
        wrec = sb("wrec", [P, 1], scope=ffn)
        oscale = sb("oscale", [P, 1], scope=ffn)
        wT = sb("wT", [P, NSLOT // P, C], scope=ffn)
        zT = sb("zT", [VB, C], scope=ffn)
        ga = sb("ga", [P, G], scope=ffn)
        gb = sb("gb", [P, G], scope=ffn)
        gate = sb("gate", [P, G], scope=ffn)
        y_out = sb("y_out", [P, 2, N], scope=ffn)
        ffn.close()

        weights_in = sem("weights_in")
        waits_apart = sem("waits_apart")
        x_in = sem("x_in")
        ctx_loaded = sem("ctx_loaded")
        consts = sem("consts")
        setup_T = sem("setup_T")
        setup_w = sem("setup_w")
        setup_u = sem("setup_u")
        u_done = sem("u_done")
        x_split = sem("x_split")
        x_norm = sem("x_norm")
        x_stats = sem("x_stats")
        x_mv = sem("x_mv")
        x_ve = sem("x_ve")
        x_rstd = sem("x_rstd")
        x_nb = sem("x_nb")
        x_hi = sem("x_hi")
        ctx_hi_done = sem("ctx_hi_done")
        ctx_lo_done = sem("ctx_lo_done")
        q_prod = sem("q_prod")
        q_evac = sem("q_evac")
        k_prod = sem("k_prod")
        k_max = sem("k_max")
        k_exp = sem("k_exp")
        k_T = sem("k_T")
        ekT_front = sem("ekT_front")
        ekT_back = sem("ekT_back")
        ctxT_prod = sem("ctxT_prod")
        ctxT_front = sem("ctxT_front")
        ctxT_back = sem("ctxT_back")
        qmax_step = sem("qmax_step")
        qmax_T = sem("qmax_T")
        qm_done = sem("qm_done")
        qm_hi_done = sem("qm_hi_done")
        qm_split = sem("qm_split")
        qm_T = sem("qm_T")
        qmT_copied = sem("qmT_copied")
        qshift = sem("qshift")
        q_sub = sem("q_sub")
        q_exp = sem("q_exp")
        qsum_step = sem("qsum_step")
        q_sum = sem("q_sum")
        r_done = sem("r_done")
        q_mul = sem("q_mul")
        krec_done = sem("krec_done")
        kscale_done = sem("kscale_done")
        g_prod = sem("g_prod")
        g_copied = sem("g_copied")
        m_prod = sem("m_prod")
        m_copied = sem("m_copied")
        mt_T = sem("mt_T")
        mt_copied = sem("mt_copied")
        out_prod = sem("out_prod")
        o_copied = sem("o_copied")
        o_squared = sem("o_squared")
        ss_prod = sem("ss_prod")
        l2_clamped = sem("l2_clamped")
        rn_pow = sem("rn_pow")
        rn_hi_done = sem("rn_hi_done")
        rn_split = sem("rn_split")
        rn_T = sem("rn_T")
        rnT_copied = sem("rnT_copied")
        rn_spread = sem("rn_spread")
        t_scaled = sem("t_scaled")
        x1_done = sem("x1_done")
        stats2 = sem("stats2")
        mv2_done = sem("mv2_done")
        var2_done = sem("var2_done")
        ffn_in = sem("ffn_in")
        out_stored = sem("out_stored")
        ffn_consts = sem("ffn_consts")
        wu1_T = sem("wu1_T")
        wu1_split = sem("wu1_split")
        wq_T = sem("wq_T")
        wq_split = sem("wq_split")
        val_T = sem("val_T")
        val_copied = sem("val_copied")
        vv_prod = sem("vv_prod")
        vv_copied = sem("vv_copied")
        key_T = sem("key_T")
        key_copied = sem("key_copied")
        rk_prod = sem("rk_prod")
        rk_copied = sem("rk_copied")
        b1_prod = sem("b1_prod")
        score_ready = sem("score_ready")
        ve2_done = sem("ve2_done")
        rstd2_done = sem("rstd2_done")
        nb2_done = sem("nb2_done")
        varh_step = sem("varh_step")
        logv_done = sem("logv_done")
        logsum_done = sem("logsum_done")
        logtotal = sem("logtotal")
        normv_step = sem("normv_step")
        h_done = sem("h_done")
        y_done = sem("y_done")
        h_T = sem("h_T")
        hT_hi_done = sem("hT_hi_done")
        hT_lo_done = sem("hT_lo_done")
        units_prod = sem("units_prod")
        units_done = sem("units_done")
        query_prod = sem("query_prod")
        query_done = sem("query_done")
        learned = sem("learned")
        gate_tanh = sem("gate_tanh")
        gate_step = sem("gate_step")
        gate_arg = sem("gate_arg")
        gate_done = sem("gate_done")
        scores = sem("scores")
        select_step = sem("select_step")
        logits_ready = sem("logits_ready")
        w_done = sem("w_done")
        w_T = sem("w_T")
        wT_copied = sem("wT_copied")
        z_prod = sem("z_prod")
        z_copied = sem("z_copied")
        f_prod = sem("f_prod")
        wrec_done = sem("wrec_done")
        oscale_done = sem("oscale_done")
        y_ready = sem("y_ready")
        masked = sem("masked")

        block = ctx.enter_context(nc.Block())

        ATT_DMAS, FFN_DMAS = 9, 14

        def wait_apart(engine, sem, value):
            wait(engine, sem, value)
            engine.sem_inc(waits_apart, 1)

        @block.sync
        def _(sp):
            for src, dst in ((L0_xattn_Wq, Wq_in), (L0_xattn_Wk, Wk_in), (L0_xattn_Wv, Wv_in)):
                sp.dma_start(dst, src.rearrange("(t p) c -> p t c", p=P)).then_inc(weights_in, 16)
            sp.dma_start(Wo_in, L0_xattn_Wo).then_inc(weights_in, 16)
            sp.dma_start(ident[:, :], identity).then_inc(weights_in, 16)
            sp.dma_start(same_head[:, :], head_ones).then_inc(weights_in, 16)
            sp.dma_start(selq_in, select_q).then_inc(weights_in, 16)
            sp.dma_start(bo[:, :], L0_xattn_bo).then_inc(weights_in, 16)
            sp.dma_start(g_in[:, :], L0_xattn_g).then_inc(weights_in, 16)

            def load(b):
                wait_apart(sp, x_in, 16 * b)
                sp.dma_start(X[:, b, :], x[b]).then_inc(x_in, 16)
                wait_apart(sp, ctx_hi_done, b)
                wait_apart(sp, ctx_lo_done, b)
                wait_apart(sp, ctxT_prod, 2 * b)
                sp.dma_start(ctx_in[:, :], ctx_4096[b]).then_inc(ctx_loaded, 16)

            load(0)
            with sp.Fori(1, B) as b:
                load(b)

            sp.wait_ge(var2_done, 2 * B)
            for src, dst in (
                (L0_ffn_Wu1.rearrange("(s p) n -> p s n", p=P), Wu1_in[:, :, :]),
                (L0_ffn_Wq, Wqf_in[:, :]),
                (L0_ffn_Wvd, Wvd_in[:, :]),
                (L0_ffn_aux_values.rearrange("(s p) n -> p s n", p=P), values_in[:, :, :]),
                (L0_ffn_Wvu.rearrange("(j p) v -> p j v", p=P), Wvu_in[:, :, :]),
                (L0_ffn_aux_keys.rearrange("(s p) d -> p s d", p=P), keys_in[:, :, :]),
                (L0_ffn_Wr, Wr_in[:, :]),
                (L0_ffn_log_rel, scoreB[BOT:BOT + 1, 0:NSLOT]),
                (L0_ffn_log_rel, scoreB[BOT:BOT + 1, NSLOT:2 * NSLOT]),
                (L0_ffn_bu1, bu1[:, :]),
                (L0_ffn_Wu2, Wu2[:, :]),
                (L0_ffn_bu2.broadcast_to([P, 1]), bu2[:, :]),
                (L0_ffn_gate_w1.broadcast_to([P, 1]), gate_w[:, :]),
                (L0_ffn_gate_bias.broadcast_to([P, 1]), gate_b[:, :]),
            ):
                sp.dma_start(dst, src).then_inc(ffn_in, 16)

            def store(b, k):
                wait_apart(sp, out_stored, 16 * b)
                wait_apart(sp, y_ready, b + 1)
                sp.dma_start(out[b], y_out[:, k % 2, :]).then_inc(out_stored, 16)

            for k in range(G):
                store(k, k)
            with sp.Fori(1, B // G) as g:
                for k in range(G):
                    store(g * G + k, k)
            sp.wait_ge(out_stored, 16 * B)

        @block.tensor
        def _(pe):
            pe.wait_ge(weights_in, 16 * ATT_DMAS)
            for dst, src in ((bank6, Wq_in), (bank7, Wk_in), (bcast, Wo_in.rearrange("p (t c) -> p t c", t=T))):
                for t in range(T):
                    last = nc.tensor.transpose(dst[:, t * P:(t + 1) * P], src[:, t, :], ident[:, :])
                last.then_inc(setup_T, 1)
            pe.wait_ge(setup_w, 1)
            for h in range(H):
                r = DH * (h % 2)
                last = nc.tensor.matmul(slot[0][:, place(h) * C:(place(h) + 1) * C], Wv_in[r:r + DH, h // 2, :],
                                        WoT[r:r + DH, h // 2, :], start=True, stop=True)
            last.then_inc(setup_u, 1)

            def product(dst, lhs, rhs):
                nc.tensor.matmul(dst, lhs[0], rhs[0], start=True, stop=False)
                nc.tensor.matmul(dst, lhs[1], rhs[0], start=False, stop=False)
                return nc.tensor.matmul(dst, lhs[0], rhs[1], start=False, stop=True)

            def q_tile(b, t):
                for n in range(2):
                    cols = slice(n * HALF, (n + 1) * HALF)
                    last = product(slot[t % 2][:, cols], [w[:, t * P:(t + 1) * P] for w in WqT],
                                   [xn_hi[:, cols], xn_lo[:, cols]])
                last.then_inc(q_prod, 1)

            def k_tile(b, t):
                for n in range(2):
                    cols = slice(n * HALF, (n + 1) * HALF)
                    last = product(k_slot[t][:, cols], [w[:, t * P:(t + 1) * P] for w in WkT],
                                   [ctx_hi[:, cols], ctx_lo[:, cols]])
                last.then_inc(k_prod, 1)

            def blocks_T(src, done):
                for j in range(J):
                    last = nc.tensor.transpose(work[:, j * P:(j + 1) * P], src[:, j * P:(j + 1) * P], ident[:, :])
                    if j % 4 == 3:
                        last.then_inc(done, 1)

            def k_transpose(b, t):
                pe.wait_ge(k_exp, 4 * b + t + 1)
                if t:
                    pe.wait_ge(ekT_front, 4 * b + t)
                    pe.wait_ge(ekT_back, 4 * b + t)
                else:
                    pe.wait_ge(ctxT_front, b + 1)
                    pe.wait_ge(ctxT_back, b + 1)
                blocks_T(ek[:, t % 2, :], k_T)

            def ctx_transpose(b):
                wait(pe, r_done, 2 * b)
                blocks_T(ctx_in, ctxT_prod)

            def q_max_T(b, n):
                if n == 0:
                    pe.wait_ge(qmax_step, 3 * (b + 1))
                    wait(pe, t_scaled, 2 * (b - 1))
                else:
                    pe.wait_ge(qm_done, 2 * b + 1)
                for j in range(4):
                    last = nc.tensor.transpose(bank_q[:, j * P:(j + 1) * P],
                                               qred[:, n * HALF + j * P:n * HALF + (j + 1) * P], ident[:, :])
                last.then_inc(qmax_T, 1)

            def q_max_turn(b):
                pe.wait_ge(qm_split, b + 1)
                nc.tensor.transpose(bank_q[:, 0:P], qm_hl[:, :].bitcast(F32), ident[:, :]).then_inc(qm_T, 1)

            def q_shift_spread(b, n):
                if n == 0:
                    pe.wait_ge(qmT_copied, b + 1)
                else:
                    pe.wait_ge(q_sub, 2 * b + 1)
                for j in range(4):
                    last = nc.tensor.matmul(bank_q[:, j * P:(j + 1) * P], sel_q[:, 4 * n + j, :], qmT[:, :],
                                            start=True, stop=True)
                last.then_inc(qshift, 1)

            def q_denominator(b, n):
                pe.wait_ge(qsum_step, 6 * b + 3 * (n + 1))
                if n == 0:
                    pe.wait_ge(ekT_front, 4 * (b + 1))
                else:
                    pe.wait_ge(ekT_back, 4 * (b + 1))
                nc.tensor.matmul((bank6, bank7)[n], same_head[:, :], qtot[:, n * HALF:(n + 1) * HALF], start=True,
                                 stop=True).then_inc(q_sum, 1)

            def norm_turn(b, shifts):
                pe.wait_ge(rn_split, b + 1)
                pe.wait_ge(q_sub, shifts)
                nc.tensor.transpose(bank_q[:, 0:P], rn_hl[:, :].bitcast(F32), ident[:, :]).then_inc(rn_T, 1)

            def norm_spread(b, n):
                if n == 0:
                    pe.wait_ge(rnT_copied, b + 1)
                else:
                    pe.wait_ge(t_scaled, 2 * b + 1)
                for j in range(4):
                    last = nc.tensor.matmul(bank_q[:, j * P:(j + 1) * P], sel_q[:, 4 * n + j, :], rnT[:, :],
                                            start=True, stop=True)
                last.then_inc(rn_spread, 1)

            def g_tile(b, t):
                if t == 0:
                    wait(pe, mt_copied, b)
                pe.wait_ge(ekT_front, 4 * b + t + 1)
                pe.wait_ge(ekT_back, 4 * b + t + 1)
                for j in range(J):
                    last = nc.tensor.matmul(bank_g[:, t * P:(t + 1) * P], ctxT[:, j, :],
                                            ekT[:, j, t * P:(t + 1) * P], start=(j == 0), stop=(j == J - 1))
                last.then_inc(g_prod, 1)

            def m_product(b):
                pe.wait_ge(g_copied, b + 1)
                gv = g_sb[:, :].rearrange("p (t h d) -> p t h d", t=T, h=H)
                mv = bank_g.rearrange("p (t h d) -> p t h d", t=T, h=H)
                for h in range(H):
                    last = nc.tensor.matmul(mv[:, :, h, :], U[:, place(h), :], gv[:, :, h, :], start=True, stop=True)
                last.then_inc(m_prod, 1)

            def m_transpose(b):
                pe.wait_ge(m_copied, b + 1)
                for t in range(T):
                    last = nc.tensor.transpose(bank_g[:, t * P:(t + 1) * P], m_sb[:, t * P:(t + 1) * P], ident[:, :])
                last.then_inc(mt_T, 1)

            def out_half(b, n, slot_free):
                if slot_free is not None:
                    pe.wait_ge(k_exp, slot_free)
                pe.wait_ge(q_mul, 2 * b + n + 1)
                pe.wait_ge(mt_copied, b + 1)
                cols = slice(n * HALF, (n + 1) * HALF)
                for t in range(T):
                    last = nc.tensor.matmul(slot[0][:, cols], mt_sb[:, t, :], eq[:, t, cols],
                                            start=(t == 0), stop=(t == T - 1))
                last.then_inc(out_prod, 1)

            def square_sums(b):
                pe.wait_ge(o_squared, 2 * (b + 1))
                for j in range(J):
                    last = nc.tensor.matmul(slot[0][:, j * NS:(j + 1) * NS], sq_sb[:, j * P:(j + 1) * P],
                                            ones[:, 0:NS], start=True, stop=True)
                last.then_inc(ss_prod, 1)

            def body(b, lag, new):
                p = b - 1
                if new:
                    pe.wait_ge(x_split, b + 1)
                    wait(pe, k_exp, 4 * b - 3)
                    wait(pe, l2_clamped, b - 1)
                    q_tile(b, 0)
                if lag:
                    k_transpose(p, 3)
                if lag > 1:
                    norm_turn(p - 1, 2 * b)
                if new:
                    wait(pe, k_exp, 4 * b)
                    q_tile(b, 1)
                if lag:
                    q_denominator(p, 0)
                    g_tile(p, 3)
                if lag > 1:
                    norm_spread(p - 1, 0)
                if new:
                    pe.wait_ge(q_evac, 4 * b + 1)
                    q_tile(b, 2)
                if lag:
                    q_denominator(p, 1)
                    m_product(p)
                if lag > 1:
                    norm_spread(p - 1, 1)
                if new:
                    pe.wait_ge(q_evac, 4 * b + 2)
                    q_tile(b, 3)
                    pe.wait_ge(ctx_hi_done, b + 1)
                    pe.wait_ge(ctx_lo_done, b + 1)
                    pe.wait_ge(q_evac, 4 * b + 3)
                    k_tile(b, 0)
                if lag:
                    m_transpose(p)
                if new:
                    ctx_transpose(b)
                    pe.wait_ge(q_evac, 4 * b + 4)
                    k_tile(b, 1)
                    q_max_T(b, 0)
                    k_transpose(b, 0)
                if lag:
                    out_half(p, 0, 4 * b + 1 if new else None)
                if new:
                    q_max_T(b, 1)
                    g_tile(b, 0)
                    pe.wait_ge(k_exp, 4 * b + 2)
                    k_tile(b, 2)
                    k_transpose(b, 1)
                    q_max_turn(b)
                if lag:
                    out_half(p, 1, None)
                if new:
                    q_shift_spread(b, 0)
                    g_tile(b, 1)
                    pe.wait_ge(k_exp, 4 * b + 3)
                    k_tile(b, 3)
                    k_transpose(b, 2)
                if lag:
                    square_sums(p)
                if new:
                    g_tile(b, 2)
                    q_shift_spread(b, 1)

            pe.wait_ge(u_done, 1)
            body(0, 0, True)
            body(1, 1, True)
            body(2, 2, True)
            with pe.Fori(3, B) as b:
                body(b, 2, True)
            body(B, 2, False)
            norm_turn(B - 1, 2 * B)
            norm_spread(B - 1, 0)
            norm_spread(B - 1, 1)

            pe.wait_ge(ffn_in, 16 * FFN_DMAS)
            pe.wait_ge(var2_done, 2 * B)
            def wide_T(src, done, base, freed):
                for j in range(J):
                    if j == J // 2 and freed is not None:
                        pe.wait_ge(*freed)
                    for s in range(2):
                        last = nc.tensor.transpose(
                            slot[j // 4][:, (j % 4) * UH + s * P:(j % 4) * UH + (s + 1) * P],
                            src[:, s, j * P:(j + 1) * P], ident[:, :])
                    if j % 4 == 3:
                        last.then_inc(done, 1)
            wide_T(Wu1_in, wu1_T, 0, None)
            for j in range(J):
                nc.tensor.transpose(bcast[:, j * BOT:(j + 1) * BOT], Wqf_in[:, j * P:(j + 1) * P],
                                    ident[0:BOT, 0:BOT])
            for j in range(J):
                last = nc.tensor.transpose(bcast[:, HALF + j * VB:HALF + (j + 1) * VB],
                                           Wvd_in[:, j * P:(j + 1) * P], ident[0:VB, 0:VB])
            last.then_inc(wq_T, 1)
            for s in range(2):
                nc.tensor.transpose(bank6[0:BOT, s * P:(s + 1) * P], keys_in[:, s, :], ident[:, :])
            nc.tensor.transpose(bank6[0:BOT, NSLOT:NSLOT + RDIM], Wr_in[:, :],
                                ident[0:RDIM, 0:RDIM]).then_inc(key_T, 1)
            pe.wait_ge(wu1_split, 4)
            wide_T(values_in, val_T, 0, None)
            pe.wait_ge(wq_split, 3)
            for j in range(J):
                last = nc.tensor.transpose(bcast[0:VB, j * P:(j + 1) * P], Wvu_in[:, j, :], ident[:, :])
            last.then_inc(wq_T, 1)
            pe.wait_ge(key_copied, 2)
            nc.tensor.matmul(bank7[0:RDIM, 0:NSLOT], WrT[:, :], keysT[:, :], start=True, stop=True).then_inc(rk_prod, 1)
            pe.wait_ge(rk_copied, 1)
            nc.tensor.matmul(bank6[0:BOT, 0:NSLOT], Wr_in[:, :], rkT[:, :], start=True, stop=True).then_inc(b1_prod, 1)
            pe.wait_ge(val_copied, 2)
            for s in range(NSLOT // P):
                for j in range(J):
                    last = nc.tensor.matmul(bank7[:, s * VB:(s + 1) * VB], valuesT[:, j, s * P:(s + 1) * P],
                                            WvdT[:, j, :], start=(j == 0), stop=(j == J - 1))
            last.then_inc(vv_prod, 1)
            pe.wait_ge(logsum_done, 1)
            pe.wait_ge(score_ready, 4)
            nc.tensor.matmul(bank6[:, 0:1], ones[:, :], logsum[:, :], start=True, stop=True).then_inc(logtotal, 1)
            pe.wait_ge(vv_copied, 1)
            pe.wait_ge(normv_step, 4)

            def h_transpose(b, k):
                pe.wait_ge(h_done, b + 1)
                wait(pe, hT_hi_done, b)
                wait(pe, hT_lo_done, b)
                for j in range(J):
                    last = nc.tensor.transpose(slot[1][:, j * P:(j + 1) * P], hbuf[:, k % 2, j * P:(j + 1) * P],
                                               ident[:, :])
                last.then_inc(h_T, 1)

            def group_products(g):
                pe.wait_ge(hT_lo_done, G * (g + 1))
                wait(pe, z_copied, G * g)
                for s in range(UH // P):
                    dst = (bank6, bank7)[s]
                    for j in range(J):
                        lhs = [w[:, j, s * P:(s + 1) * P] for w in Wu1T]
                        rhs = [h[:, j, :] for h in hT]
                        for n, (a, c) in enumerate(((0, 0), (1, 0), (0, 1))):
                            last = nc.tensor.matmul(dst, lhs[a], rhs[c], start=(j == 0 and n == 0),
                                                    stop=(j == J - 1 and n == 2))
                    last.then_inc(units_prod, 1)
                wait(pe, gate_tanh, 2 * g)
                for j in range(J):
                    for n, (a, c) in enumerate(((0, 0), (1, 0), (0, 1))):
                        last = nc.tensor.matmul(bcast[0:BOT, 0:GT], WqfT[a][:, j, :], hT[c][:, j, :],
                                                start=(j == 0 and n == 0), stop=(j == J - 1 and n == 2))
                last.then_inc(query_prod, 1)

            def score(b, k):
                wait(pe, logits_ready, b)
                nc.tensor.matmul(bcast[:, GT:2 * GT], query[:, k * C:(k + 1) * C], scoreB[:, :],
                                 start=True, stop=True).then_inc(scores, 1)

            def group_tail(g, more):
                pe.wait_ge(query_done, g + 1)
                score(g * G, 0)
                pe.wait_ge(units_done, 2 * (g + 1))
                for k in range(G):
                    for s in range(UH // P):
                        last = nc.tensor.matmul(bcast[:, k:k + 1], units[:, s, k * C:(k + 1) * C], Wu2[:, s:s + 1],
                                                start=(s == 0), stop=(s == UH // P - 1))
                last.then_inc(learned, 1)
                for k in range(G):
                    b = g * G + k
                    if k < G - 1:
                        score(b + 1, k + 1)
                    pe.wait_ge(w_done, b + 1)
                    for s in range(NSLOT // P):
                        last = nc.tensor.transpose(bank6[:, s * C:(s + 1) * C], w_sb[:, s * P:(s + 1) * P],
                                                   ident[:, :])
                    last.then_inc(w_T, 1)
                    pe.wait_ge(wT_copied, b + 1)
                    for s in range(NSLOT // P):
                        last = nc.tensor.matmul(bank7[0:VB, 0:C], VV[:, s, :], wT[:, s, :],
                                                start=(s == 0), stop=(s == NSLOT // P - 1))
                    last.then_inc(z_prod, 1)
                    if more:
                        h_transpose(b + G, k)
                    pe.wait_ge(z_copied, b + 1)
                    wait(pe, y_ready, b)
                    for n in range(2):
                        last = nc.tensor.matmul(slot[0][:, n * HALF:(n + 1) * HALF], zT[:, :],
                                                WvuT[:, n * HALF:(n + 1) * HALF], start=True, stop=True)
                    last.then_inc(f_prod, 1)

            for k in range(G):
                h_transpose(k, k)
            group_products(0)
            group_tail(0, True)
            group_products(1)
            with pe.Fori(1, B // G - 1) as g:
                group_tail(g, True)
                group_products(g + 1)
            group_tail(B // G - 1, False)

        @block.scalar
        def _(act):
            def ctx_high(b):
                act.wait_ge(ctx_loaded, 16 * (b + 1))
                wait(act, k_prod, 4 * b)
                wait(act, ctx_lo_done, b)
                nc.scalar.copy(ctx_hi[:, :], ctx_in[:, :]).then_inc(ctx_hi_done, 1)

            def x_layernorm(b):
                act.wait_ge(x_in, 16 * (b + 1))
                act.wait_ge(x_rstd, b + 1)
                act.wait_ge(x_nb, b + 1)
                wait(act, x_split, b)
                nc.scalar.activation(xn[:, :], X[:, b, :], ACT.Identity, bias=nb[:, :],
                                     scale=rstd[:, :]).then_inc(x_norm, 1)
                act.wait_ge(x_norm, b + 1)
                wait(act, q_prod, 4 * b)
                nc.scalar.copy(xn_hi[:, :], xn[:, :]).then_inc(x_hi, 1)

            def q_copy(b, t):
                act.wait_ge(q_prod, 4 * b + t + 1)
                wait(act, q_exp, 2 * b)
                nc.scalar.copy(qsb[:, t, :], slot[t % 2][:, :]).then_inc(q_evac, 1)

            def k_exponential(b, t):
                act.wait_ge(k_max, 4 * b + t + 1)
                wait(act, k_T, 8 * b + 2 * t - 2)
                wait(act, krec_done, b)
                nc.scalar.activation(ek[:, t % 2, :], k_slot[t][:, :], ACT.Exp, bias=nkm[:, t:t + 1],
                                     accum_out=ksum[:, t:t + 1]).then_inc(k_exp, 1)

            def k_front(b, t):
                act.wait_ge(k_T, 8 * b + 2 * t + 1)
                wait(act, g_prod, 4 * b)
                nc.scalar.copy(ekT[:, 0:4, t * P:(t + 1) * P],
                               bank6.rearrange("p (j d) -> p j d", d=P)).then_inc(ekT_front, 1)

            def ctx_front(b):
                act.wait_ge(ctxT_prod, 2 * b + 1)
                wait(act, g_prod, 4 * b)
                nc.scalar.copy(ctxT[:, 0:4, :], bank6.rearrange("p (j c) -> p j c", c=P)).then_inc(ctxT_front, 1)

            def out_copy(p, n):
                cols = slice(n * HALF, (n + 1) * HALF)
                act.wait_ge(out_prod, 2 * p + n + 1)
                wait(act, t_scaled, 2 * p)
                nc.scalar.activation(o_sb[:, cols], slot[0][:, cols], ACT.Identity,
                                     bias=bo[:, :]).then_inc(o_copied, 1)
                act.wait_ge(o_copied, 2 * p + n + 1)
                wait(act, ss_prod, p)
                nc.scalar.activation(sq_sb[:, cols], o_sb[:, cols], ACT.Square).then_inc(o_squared, 1)

            def q_exponential(b, n):
                cols = slice(n * HALF, (n + 1) * HALF)
                act.wait_ge(q_sub, 2 * b + n + 1)
                wait(act, out_prod, 2 * b)
                nc.scalar.activation(eq[:, :, cols], qsb[:, :, cols], ACT.Exp).then_inc(q_exp, 1)

            def g_copy(p):
                act.wait_ge(g_prod, 4 * (p + 1))
                wait(act, m_prod, p)
                nc.scalar.copy(g_sb[:, :], bank_g).then_inc(g_copied, 1)

            def m_copy(p):
                act.wait_ge(m_prod, p + 1)
                wait(act, mt_T, p)
                nc.scalar.copy(m_sb[:, :], bank_g).then_inc(m_copied, 1)

            def body(b, lag, new, more):
                p = b - 1
                if new:
                    q_copy(b, 0)
                if lag:
                    k_front(p, 3)
                if new:
                    q_copy(b, 1)
                if lag:
                    g_copy(p)
                if new:
                    q_copy(b, 2)
                if lag:
                    m_copy(p)
                if new:
                    q_copy(b, 3)
                    ctx_front(b)
                    k_exponential(b, 0)
                    k_front(b, 0)
                    k_exponential(b, 1)
                if lag:
                    out_copy(p, 0)
                if more:
                    x_layernorm(b + 1)
                if new:
                    k_front(b, 1)
                    k_exponential(b, 2)
                if lag:
                    out_copy(p, 1)
                if new:
                    q_exponential(b, 0)
                    k_front(b, 2)
                    k_exponential(b, 3)
                    if more:
                        ctx_high(b + 1)
                    q_exponential(b, 1)

            act.wait_ge(weights_in, 16 * ATT_DMAS)
            ctx_high(0)
            x_layernorm(0)
            act.wait_ge(setup_w, 6)
            act.wait_ge(u_done, 1)
            body(0, 0, True, True)
            body(1, 1, True, True)
            body(2, 2, True, True)
            with act.Fori(3, B - 1) as b:
                body(b, 2, True, True)
            body(B - 1, 2, True, False)
            body(B, 2, False, False)

            act.wait_ge(varh_step, 2)
            nc.scalar.activation(logv[:, :], varh[:, :], ACT.Ln, bias=ones[:, 0:1]).then_inc(logv_done, 1)

            def hT_high(b, k):
                act.wait_ge(h_T, b + 1)
                nc.scalar.copy(hT[0][:, :, k * C:(k + 1) * C],
                               slot[1][:, :].rearrange("p (j c) -> p j c", j=J)).then_inc(hT_hi_done, 1)

            def group_units(g):
                wait(act, learned, g)
                for s in range(UH // P):
                    act.wait_ge(units_prod, 2 * g + s + 1)
                    nc.scalar.activation(units[:, s, :], (bank6, bank7)[s], ACT.Gelu_apprx_tanh,
                                         bias=bu1[:, s:s + 1]).then_inc(units_done, 1)

            def group_rest(g, more):
                for k in range(G):
                    b = g * G + k
                    act.wait_ge(logits_ready, b + 1)
                    wait(act, w_T, b)
                    if k == 0:
                        wait(act, oscale_done, b)
                    nc.scalar.activation(w_sb[:, :], logits[:, :], ACT.Exp, bias=nlmax[:, :],
                                         accum_out=wsum[:, k:k + 1]).then_inc(w_done, 1)
                    if k == 0:
                        act.wait_ge(learned, g + 1)
                        wait(act, gate_done, g)
                        nc.scalar.activation(ga[:, :], bcast[:, 0:G], ACT.Tanh, bias=half3[:, 0:1],
                                             scale=0.5).then_inc(gate_tanh, 1)
                    act.wait_ge(w_T, b + 1)
                    wait(act, z_prod, b)
                    nc.scalar.copy(wT[:, :, :].rearrange("p s c -> p (s c)"), bank6[:, 0:NSLOT]).then_inc(wT_copied, 1)
                    if k == 0:
                        act.wait_ge(gate_arg, g + 1)
                        nc.scalar.activation(gb[:, :], ga[:, :], ACT.Tanh, bias=half3[:, 2:3],
                                             scale=half3[:, 1:2]).then_inc(gate_tanh, 1)
                    act.wait_ge(z_prod, b + 1)
                    wait(act, f_prod, b)
                    nc.scalar.copy(zT[:, :], bank7[0:VB, 0:C]).then_inc(z_copied, 1)
                    if more:
                        act.wait_ge(h_T, b + G + 1)
                        if k == 0:
                            act.wait_ge(query_prod, g + 1)
                        nc.scalar.copy(hT[0][:, :, k * C:(k + 1) * C],
                                       slot[1][:, :].rearrange("p (j c) -> p j c", j=J)).then_inc(hT_hi_done, 1)

            act.wait_ge(ffn_in, 16 * FFN_DMAS)
            for k in range(G):
                hT_high(k, k)
            group_units(0)
            act.wait_ge(normv_step, 4)
            group_rest(0, True)
            group_units(1)
            with act.Fori(1, B // G - 1) as g:
                group_rest(g, True)
                group_units(g + 1)
            group_rest(B // G - 1, False)

        @block.gpsimd
        def _(pool):
            nc.gpsimd.memset(ones[:, :], 1.0).then_inc(consts, 1)
            nc.gpsimd.memset(half_neg[:, :], -0.5).then_inc(consts, 1)
            pool.wait_ge(consts, 2)

            def chain(done, base, ops):
                for s, (dst, a, c, sem_in, val) in enumerate(ops):
                    pool.wait_ge(sem_in, val)
                    if s:
                        pool.wait_ge(done, base + s)
                    nc.gpsimd.tensor_tensor(dst, a, c, ALU.add).then_inc(done, 1)

            def x_low(b):
                pool.wait_ge(x_hi, b + 1)
                wait(pool, q_prod, 4 * b)
                nc.gpsimd.tensor_tensor(xn_lo[:, :], xn[:, :], xn_hi[:, :].bitcast(F32),
                                        ALU.subtract).then_inc(x_split, 1)

            def ctx_low(b):
                pool.wait_ge(ctx_hi_done, b + 1)
                nc.gpsimd.tensor_tensor(ctx_lo[:, :], ctx_in[:, :], ctx_hi[:, :].bitcast(F32),
                                        ALU.subtract).then_inc(ctx_lo_done, 1)

            def rstd_pow(b):
                pool.wait_ge(x_ve, b + 1)
                wait(pool, x_norm, b)
                wait(pool, x_nb, b)
                nc.gpsimd.tensor_tensor(rstd[:, :], ve[:, :], half_neg[:, 0:1], ALU.pow).then_inc(x_rstd, 1)

            def q_scale(p, n):
                pool.wait_ge(r_done, 2 * p + n + 1)
                cols = slice(n * HALF, (n + 1) * HALF)
                nc.gpsimd.tensor_tensor(eq[:, :, cols], eq[:, :, cols],
                                        r_sb[:, cols].unsqueeze(1).broadcast_to([P, T, HALF]),
                                        ALU.mult).then_inc(q_mul, 1)

            def norm_pow(p):
                pool.wait_ge(l2_clamped, p + 1)
                wait(pool, rn_split, p)
                nc.gpsimd.tensor_tensor(rn[:, :], l2c[:, :], half_neg[:, :], ALU.pow).then_inc(rn_pow, 1)

            def residual(p):
                pool.wait_ge(t_scaled, 2 * (p + 1))
                nc.gpsimd.tensor_tensor(X[:, p, :], X[:, p, :], t_sb[:, :], ALU.add).then_inc(x1_done, 1)

            def q_sums(b, n):
                wait(pool, q_sum, 2 * b)
                cols = slice(n * HALF, (n + 1) * HALF)
                e = [eq[:, t, cols] for t in range(T)]
                r = qtot[:, cols]
                chain(qsum_step, 6 * b + 3 * n, [
                    (r, e[0], e[1], q_exp, 2 * b + n + 1),
                    (r, r, e[2], q_exp, 2 * b + n + 1),
                    (r, r, e[3], q_exp, 2 * b + n + 1)])

            def body(b, lag, new, more):
                p = b - 1
                if lag:
                    q_scale(p, 0)
                    q_scale(p, 1)
                if more:
                    rstd_pow(b + 1)
                if lag > 1:
                    residual(p - 1)
                if more:
                    x_low(b + 1)
                if new:
                    q_sums(b, 0)
                if lag:
                    norm_pow(p)
                if more:
                    ctx_low(b + 1)
                if new:
                    q_sums(b, 1)

            rstd_pow(0)
            ctx_low(0)
            x_low(0)
            body(0, 0, True, True)
            body(1, 1, True, True)
            body(2, 2, True, True)
            with pool.Fori(3, B - 1) as b:
                body(b, 2, True, True)
            body(B - 1, 2, True, False)
            body(B, 2, False, False)
            residual(B - 1)

            pool.wait_ge(var2_done, 2 * B)
            nc.gpsimd.memset(half_neg2[:, :], -0.5).then_inc(ffn_consts, 1)
            pool.wait_ge(ffn_consts, 1)
            nc.gpsimd.memset(query[BOT:BOT + 1, :], 1.0).then_inc(ffn_consts, 1)
            pool.wait_ge(ve2_done, 1)
            pool.wait_ge(ffn_consts, 2)
            nc.gpsimd.tensor_tensor(rstd2[:, :, 0], ve2[:, :], half_neg2[:, :], ALU.pow).then_inc(rstd2_done, 1)

            def add_h(b, k):
                pool.wait_ge(h_done, b + 1)
                nc.gpsimd.tensor_tensor(X[:, b, :], X[:, b, :], hbuf[:, k % 2, :], ALU.add).then_inc(y_done, 1)

            for k in range(G):
                add_h(k, k)
            with pool.Fori(1, B // G) as g:
                for k in range(G):
                    add_h(g * G + k, k)

        @block.vector
        def _(dve):
            V = nc.vector

            def x_statistics(b):
                dve.wait_ge(x_in, 16 * (b + 1))
                wait_apart(dve, x_norm, b)
                for s in range(2):
                    V.bn_stats(st1[:, 6 * s:6 * s + 6], X[:, b, s * HALF:(s + 1) * HALF]).then_inc(x_stats, 1)
                wait_apart(dve, x_stats, 2 * (b + 1))
                V.bn_aggr(mv1[:, :], st1[:, :]).then_inc(x_mv, 1)
                dve.wait_ge(x_mv, b + 1)
                V.tensor_scalar_add(ve[:, :], mv1[:, 1:2], LN_EPS).then_inc(x_ve, 1)

            def x_bias(b):
                dve.wait_ge(x_rstd, b + 1)
                V.scalar_tensor_tensor(nb[:, :], mv1[:, 0:1], -1.0, rstd[:, :], ALU.mult,
                                       ALU.mult).then_inc(x_nb, 1)

            def k_reciprocals(p):
                dve.wait_ge(k_exp, 4 * (p + 1))
                V.reciprocal(krec[:, :], ksum[:, :]).then_inc(krec_done, 1)
                dve.wait_ge(krec_done, p + 1)
                wait(dve, mt_copied, p)
                V.tensor_scalar_mul(kscale[:, :], krec[:, :], float(DH) ** -0.5).then_inc(kscale_done, 1)

            def mt_scale(p):
                dve.wait_ge(mt_T, p + 1)
                dve.wait_ge(kscale_done, p + 1)
                wait(dve, out_prod, 2 * p)
                V.tensor_tensor(mt_sb[:, :, :], bank_g.rearrange("p (t c) -> p t c", t=T),
                                kscale[:, :].unsqueeze(2).broadcast_to([P, T, C]), ALU.mult).then_inc(mt_copied, 1)

            def q_tile_max(b, s):
                q = [qsb[:, t, :] for t in range(T)]
                if s == 0:
                    wait(dve, qmax_T, 2 * b)
                else:
                    dve.wait_ge(qmax_step, 3 * b + s)
                dve.wait_ge(q_evac, 4 * b + 2 + s)
                V.tensor_tensor(qred[:, :], q[0] if s == 0 else qred[:, :], q[s + 1], ALU.max).then_inc(qmax_step, 1)

            def k_maximum(b, t):
                dve.wait_ge(k_prod, 4 * b + t + 1)
                wait(dve, k_exp, 4 * b)
                V.tensor_reduce(nkm[:, t:t + 1], k_slot[t][:, :], AX, ALU.max, negate=True).then_inc(k_max, 1)

            def k_back(b, t):
                dve.wait_ge(k_T, 8 * b + 2 * t + 2)
                wait(dve, g_prod, 4 * b)
                V.tensor_copy(ekT[:, 4:J, t * P:(t + 1) * P],
                              bank7.rearrange("p (j d) -> p j d", d=P)).then_inc(ekT_back, 1)

            def ctx_back(b):
                dve.wait_ge(ctxT_prod, 2 * b + 2)
                wait(dve, g_prod, 4 * b)
                V.tensor_copy(ctxT[:, 4:J, :], bank7.rearrange("p (j c) -> p j c", c=P)).then_inc(ctxT_back, 1)

            def q_block_max(b, n):
                dve.wait_ge(qmax_T, 2 * b + n + 1)
                wait(dve, qm_split, b)
                V.tensor_reduce(qm[:, 4 * n * H:4 * (n + 1) * H], bank_q.rearrange("p (m d) -> p m d", d=DL), AX,
                                ALU.max).then_inc(qm_done, 1)

            def q_max_parts(b):
                dve.wait_ge(qm_done, 2 * (b + 1))
                wait(dve, qm_T, b)
                hi, lo = qm_hl[:, 0:J * H], qm_hl[:, J * H:2 * J * H]
                V.tensor_copy(hi, qm[:, :]).then_inc(qm_hi_done, 1)
                dve.wait_ge(qm_hi_done, b + 1)
                V.tensor_tensor(lo, qm[:, :], hi.bitcast(F32), ALU.subtract).then_inc(qm_split, 1)

            def q_max_turned(b):
                dve.wait_ge(qm_T, b + 1)
                wait(dve, qshift, 2 * b)
                V.tensor_copy(qmT[:, :], bank_q[:, 0:P]).then_inc(qmT_copied, 1)

            def q_shift(b, n):
                cols = slice(n * HALF, (n + 1) * HALF)
                dve.wait_ge(qshift, 2 * b + n + 1)
                V.tensor_tensor(qsb[:, :, cols], qsb[:, :, cols],
                                bank_q.unsqueeze(1).broadcast_to([P, T, HALF]), ALU.subtract).then_inc(q_sub, 1)

            def q_reciprocal(p, n):
                dve.wait_ge(q_sum, 2 * p + n + 1)
                wait(dve, q_mul, 2 * p)
                V.reciprocal(r_sb[:, n * HALF:(n + 1) * HALF], (bank6, bank7)[n]).then_inc(r_done, 1)

            def norm_clamp(p):
                dve.wait_ge(ss_prod, p + 1)
                wait(dve, rn_pow, p)
                sums = slot[0][:, 0:J * NS].rearrange("p (j s) -> p j s", s=NS)[:, :, 0]
                V.tensor_scalar_max(l2c[:, :], sums, NORM_FLOOR).then_inc(l2_clamped, 1)

            def norm_parts(p):
                hi, lo = [rn_hl[:, s * J * H:(s + 1) * J * H].rearrange("p (j h) -> p j h", j=J) for s in (0, 1)]
                src = rn[:, :].unsqueeze(2).broadcast_to([P, J, H])
                dve.wait_ge(rn_pow, p + 1)
                wait(dve, rn_T, p)
                V.tensor_copy(hi, src).then_inc(rn_hi_done, 1)
                dve.wait_ge(rn_hi_done, p + 1)
                V.tensor_tensor(lo, src, hi.bitcast(F32), ALU.subtract).then_inc(rn_split, 1)

            def norm_turned(p):
                dve.wait_ge(rn_T, p + 1)
                wait(dve, rn_spread, 2 * p)
                V.tensor_copy(rnT[:, :], bank_q[:, 0:P]).then_inc(rnT_copied, 1)

            def norm_scale(p, n):
                cols = slice(n * HALF, (n + 1) * HALF)
                dve.wait_ge(rn_spread, 2 * p + n + 1)
                wait(dve, x1_done, p)
                V.scalar_tensor_tensor(t_sb[:, cols], o_sb[:, cols], gs[:, :], bank_q, ALU.mult,
                                       ALU.mult).then_inc(t_scaled, 1)

            def statistics(p):
                wait_apart(dve, x1_done, p + 1)
                for s in range(2):
                    V.bn_stats(st2[:, 6 * s:6 * s + 6], X[:, p, s * HALF:(s + 1) * HALF]).then_inc(stats2, 1)
                dve.wait_ge(stats2, 2 * (p + 1))
                wait_apart(dve, var2_done, 2 * p)
                V.bn_aggr(mv2[:, :], st2[:, :]).then_inc(mv2_done, 1)
                dve.wait_ge(mv2_done, p + 1)
                V.tensor_copy(mean2[:, p, :], mv2[:, 0:1]).then_inc(var2_done, 1)
                V.tensor_copy(var2[:, p, :], mv2[:, 1:2]).then_inc(var2_done, 1)

            def body(b, lag, new, more):
                p = b - 1
                if lag:
                    k_back(p, 3)
                if lag > 1:
                    norm_turned(p - 1)
                if lag:
                    k_reciprocals(p)
                    q_reciprocal(p, 0)
                if new:
                    q_tile_max(b, 0)
                if lag > 1:
                    norm_scale(p - 1, 0)
                if new:
                    q_tile_max(b, 1)
                if lag:
                    q_reciprocal(p, 1)
                if lag > 1:
                    norm_scale(p - 1, 1)
                if new:
                    k_maximum(b, 0)
                    q_tile_max(b, 2)
                    ctx_back(b)
                if lag:
                    mt_scale(p)
                if new:
                    k_maximum(b, 1)
                    k_back(b, 0)
                    q_block_max(b, 0)
                if more:
                    x_statistics(b + 1)
                if new:
                    q_block_max(b, 1)
                    q_max_parts(b)
                if more:
                    x_bias(b + 1)
                if new:
                    k_maximum(b, 2)
                    k_back(b, 1)
                    q_max_turned(b)
                if lag > 1:
                    statistics(p - 1)
                if new:
                    q_shift(b, 0)
                    k_maximum(b, 3)
                    k_back(b, 2)
                if lag:
                    norm_clamp(p)
                if new:
                    q_shift(b, 1)
                if lag:
                    norm_parts(p)

            dve.wait_ge(weights_in, 16 * ATT_DMAS)
            V.tensor_scalar_mul(gs[:, :], g_in[:, :], float(C) ** 0.5)
            dve.wait_ge(setup_T, 3)
            V.tensor_copy(WoT, bcast[:, 0:HD].rearrange("p (t c) -> p t c", t=T)).then_inc(setup_w, 1)
            for n, (parts, src) in enumerate(((WqT, bank6), (WkT, bank7))):
                hi, lo = [w[:, :].rearrange("p (t h d) -> p h t d", t=T, h=H) for w in parts]
                v = src.rearrange("p (h t d) -> p h t d", t=T, h=H)
                V.tensor_copy(hi, v).then_inc(setup_w, 1)
                dve.wait_ge(setup_w, 2 + 2 * n)
                V.tensor_tensor(lo, v, hi.bitcast(F32), ALU.subtract).then_inc(setup_w, 1)
            V.tensor_copy(sel_q[:, :, :], selq_in).then_inc(setup_w, 1)
            x_statistics(0)
            x_bias(0)
            dve.wait_ge(setup_u, 1)
            V.tensor_copy(U[:, :, :].rearrange("p h c -> p (h c)"), slot[0][:, :]).then_inc(u_done, 1)

            body(0, 0, True, True)
            body(1, 1, True, True)
            body(2, 2, True, True)
            with dve.Fori(3, B - 1) as b:
                body(b, 2, True, True)
            body(B - 1, 2, True, False)
            body(B, 2, False, False)
            norm_turned(B - 1)
            norm_scale(B - 1, 0)
            norm_scale(B - 1, 1)
            statistics(B - 1)

            dve.wait_ge(var2_done, 2 * B)
            V.tensor_scalar_add(ve2[:, :], var2[:, :, 0], LN_EPS).then_inc(ve2_done, 1)
            dve.wait_ge(rstd2_done, 1)
            V.scalar_tensor_tensor(nb2[:, :, 0], mean2[:, :, 0], -1.0, rstd2[:, :, 0], ALU.mult,
                                   ALU.mult).then_inc(nb2_done, 1)
            V.tensor_tensor(varh[:, :], var2[:, :, 0], rstd2[:, :, 0], ALU.mult).then_inc(varh_step, 1)
            dve.wait_ge(varh_step, 1)
            V.tensor_tensor(varh[:, :], varh[:, :], rstd2[:, :, 0], ALU.mult).then_inc(varh_step, 1)
            dve.wait_ge(logv_done, 1)
            V.reduce_sum(logsum[:, :], logv[:, :], AX).then_inc(logsum_done, 1)

            def h_scale(b, k):
                dve.wait_ge(nb2_done, 1)
                wait(dve, h_T, b - 1)
                wait(dve, y_done, b - 1)
                V.tensor_scalar(hbuf[:, k % 2, :], X[:, b, :], rstd2[:, b, :], nb2[:, b, :], ALU.mult,
                                ALU.add).then_inc(h_done, 1)

            def hT_low(b, k):
                dve.wait_ge(hT_hi_done, b + 1)
                cols = slice(k * C, (k + 1) * C)
                V.tensor_tensor(hT[1][:, :, cols], slot[1][:, :].rearrange("p (j c) -> p j c", j=J),
                                hT[0][:, :, cols].bitcast(F32), ALU.subtract).then_inc(hT_lo_done, 1)

            h_scale(0, 0)
            h_scale(1, 1)
            for n in range(2):
                dve.wait_ge(wu1_T, n + 1)
                hi, lo = [w[:, 4 * n:4 * n + 4, :].rearrange("p j u -> p (j u)") for w in Wu1T]
                V.tensor_copy(hi, slot[n][:, :]).then_inc(wu1_split, 1)
                dve.wait_ge(wu1_split, 2 * n + 1)
                V.tensor_tensor(lo, slot[n][:, :], hi.bitcast(F32), ALU.subtract).then_inc(wu1_split, 1)
            dve.wait_ge(wq_T, 1)
            hi, lo = [w[:, :, :].rearrange("p j d -> p (j d)") for w in WqfT]
            V.tensor_copy(hi, bcast[:, 0:HALF]).then_inc(wq_split, 1)
            dve.wait_ge(wq_split, 1)
            V.tensor_tensor(lo, bcast[:, 0:HALF], hi.bitcast(F32), ALU.subtract).then_inc(wq_split, 1)
            V.tensor_copy(WvdT[:, :, :].rearrange("p j d -> p (j d)"), bcast[:, HALF:N]).then_inc(wq_split, 1)
            dve.wait_ge(key_T, 1)
            V.tensor_copy(keysT[:, :], bank6[0:BOT, 0:NSLOT]).then_inc(key_copied, 1)
            V.tensor_copy(WrT[:, :], bank6[0:BOT, NSLOT:NSLOT + RDIM]).then_inc(key_copied, 1)
            dve.wait_ge(rk_prod, 1)
            V.tensor_copy(rkT[:, :], bank7[0:RDIM, 0:NSLOT]).then_inc(rk_copied, 1)
            for n in range(2):
                dve.wait_ge(val_T, n + 1)
                V.tensor_copy(valuesT[:, 4 * n:4 * n + 4, :].rearrange("p j u -> p (j u)"),
                              slot[n][:, :]).then_inc(val_copied, 1)
            dve.wait_ge(wq_T, 2)
            V.tensor_copy(WvuT[:, :], bcast[0:VB, :]).then_inc(score_ready, 1)
            dve.wait_ge(ffn_in, 16 * FFN_DMAS)
            V.tensor_scalar_mul(scoreB[0:BOT, NSLOT:2 * NSLOT], keysT[:, :], float(BOT) ** -0.5).then_inc(score_ready, 1)
            dve.wait_ge(b1_prod, 1)
            V.tensor_scalar_mul(scoreB[0:BOT, 0:NSLOT], bank6[0:BOT, 0:NSLOT], float(RDIM) ** -0.5).then_inc(score_ready, 1)
            for n, src in enumerate((bu2, gate_w, gate_b)):
                last = V.tensor_scalar_mul(half3[:, n:n + 1], src[:, :], 0.5)
            last.then_inc(score_ready, 1)
            dve.wait_ge(vv_prod, 1)
            V.tensor_copy(VV[:, :, :].rearrange("p s d -> p (s d)"), bank7[:, 0:2 * VB]).then_inc(vv_copied, 1)
            dve.wait_ge(logtotal, 1)
            V.tensor_scalar(logmean[:, :], bank6[:, 0:1], 1.0 / (B * C), 1e-6, ALU.mult, ALU.add).then_inc(normv_step, 1)
            dve.wait_ge(normv_step, 1)
            V.reciprocal(logrec[:, :], logmean[:, :]).then_inc(normv_step, 1)
            dve.wait_ge(normv_step, 2)
            V.tensor_scalar(varh[:, :], logv[:, :], logrec[:, :], 0.5, ALU.mult, ALU.mult).then_inc(normv_step, 1)
            dve.wait_ge(normv_step, 3)
            V.tensor_scalar_add(normv[:, :, :].rearrange("p g k -> p (g k)"), varh[:, :], 1.25).then_inc(normv_step, 1)

            def select(b, k):
                s0 = 3 * b
                dve.wait_ge(scores, b + 1)
                wait(dve, w_done, b)
                wait_apart(dve, select_step, s0)
                V.max(top8[:, :], bcast[:, GT:GT + NSLOT]).then_inc(select_step, 1)
                wait_apart(dve, select_step, s0 + 1)
                V.match_replace(replaced[:, :], top8[:, :], bcast[:, GT:GT + NSLOT], NEG).then_inc(select_step, 1)
                dve.wait_ge(select_step, s0 + 2)
                V.tensor_tensor(outside[:, :], replaced[:, :], bcast[:, GT:GT + NSLOT],
                                ALU.is_equal).then_inc(select_step, 1)
                dve.wait_ge(select_step, s0 + 3)
                V.scalar_tensor_tensor(logits[:, :], outside[:, :], NEG, bcast[:, GT + NSLOT:2 * GT], ALU.mult,
                                       ALU.add).then_inc(masked, 1)
                dve.wait_ge(masked, b + 1)
                V.tensor_reduce(nlmax[:, :], logits[:, :], AX, ALU.max, negate=True).then_inc(logits_ready, 1)

            def gate_first(g):
                s0 = 4 * g
                dve.wait_ge(gate_tanh, 2 * g + 1)
                V.scalar_tensor_tensor(gate[:, :], ga[:, :], 1.25, normv[:, g, :], ALU.mult, ALU.add).then_inc(gate_step, 1)
                dve.wait_ge(gate_step, s0 + 1)
                V.tensor_scalar(ga[:, :], gate[:, :], 0.0, 5.0, ALU.max, ALU.min).then_inc(gate_step, 1)
                dve.wait_ge(gate_step, s0 + 2)
                V.tensor_scalar(gate[:, :], ga[:, :], -TAU_LOW, 1.0 / (TAU_HIGH - TAU_LOW), ALU.add,
                                ALU.mult).then_inc(gate_step, 1)
                dve.wait_ge(gate_step, s0 + 3)
                V.tensor_scalar(ga[:, :], gate[:, :], 0.0, 1.0, ALU.max, ALU.min).then_inc(gate_arg, 1)

            def gate_second(g):
                dve.wait_ge(gate_tanh, 2 * g + 2)
                V.tensor_scalar(ga[:, :], gb[:, :], 0.5, 0.5, ALU.mult, ALU.add).then_inc(gate_step, 1)
                dve.wait_ge(gate_step, 4 * g + 4)
                V.scalar_tensor_tensor(gate[:, :], ga[:, :], EARLY_EXIT, ga[:, :], ALU.is_ge, ALU.mult).then_inc(gate_done, 1)

            def finish(b, k):
                V.reciprocal(wrec[:, :], wsum[:, k:k + 1]).then_inc(wrec_done, 1)
                dve.wait_ge(wrec_done, b + 1)
                wait(dve, y_ready, b)
                V.tensor_tensor(oscale[:, :], wrec[:, :], gate[:, k:k + 1], ALU.mult).then_inc(oscale_done, 1)
                dve.wait_ge(oscale_done, b + 1)
                dve.wait_ge(f_prod, b + 1)
                dve.wait_ge(y_done, b + 1)
                wait(dve, out_stored, 16 * (b - 1))
                V.scalar_tensor_tensor(y_out[:, k % 2, :], slot[0][:, :], oscale[:, :], X[:, b, :], ALU.mult,
                                       ALU.add).then_inc(y_ready, 1)

            def group(g, more):
                dve.wait_ge(query_prod, g + 1)
                V.tensor_copy(query[0:BOT, :], bcast[0:BOT, 0:GT]).then_inc(query_done, 1)
                for k in range(G):
                    b = g * G + k
                    select(b, k)
                    if more:
                        h_scale(b + G, k)
                    if k == 0:
                        gate_first(g)
                        gate_second(g)
                    if more:
                        hT_low(b + G, k)
                    dve.wait_ge(w_done, b + 1)
                    finish(b, k)

            hT_low(0, 0)
            h_scale(2, 2)
            hT_low(1, 1)
            h_scale(3, 3)
            hT_low(2, 2)
            hT_low(3, 3)
            group(0, True)
            with dve.Fori(1, B // G - 1) as g:
                group(g, True)
            group(B // G - 1, False)


def constants():
    import numpy as np
    head = np.arange(P) // DL
    head_ones = (head[:, None] == head[None]).astype(np.float32)
    select_q = np.zeros((2, J, H, J, H, DL), np.float32)
    for j in range(J):
        for h in range(H):
            select_q[:, j, h, j, h] = 1
    return {"identity": np.eye(P, dtype=np.float32), "head_ones": head_ones,
            "select_q": select_q.reshape(2 * J * H, J, P)}


INPUTS = ["x", "ctx_4096", "L0_xattn_Wq", "L0_xattn_Wk", "L0_xattn_Wv", "L0_xattn_Wo", "L0_xattn_bo", "L0_xattn_g",
          "L0_ffn_Wq", "L0_ffn_Wr", "L0_ffn_aux_keys", "L0_ffn_aux_values", "L0_ffn_Wvd", "L0_ffn_Wvu",
          "L0_ffn_Wu1", "L0_ffn_bu1", "L0_ffn_Wu2", "L0_ffn_bu2", "L0_ffn_gate_w1", "L0_ffn_gate_bias",
          "L0_ffn_log_rel"]


def layout(name, a):
    if name in ("L0_xattn_bo", "L0_xattn_g"):
        return a.reshape(C, 1)
    if name in ("L0_ffn_bu1", "L0_ffn_Wu2"):
        return a.reshape(UH // P, P).T
    if name in ("L0_ffn_bu2", "L0_ffn_gate_w1", "L0_ffn_gate_bias", "L0_ffn_log_rel"):
        return a.reshape(1, -1)
    return a


def kernel(**inputs):
    import numpy as np
    import concourse.bacc as bacc
    from concourse.bass_utils import run_bass_kernel_spmd

    nc = bacc.Bacc("TRN2", target_bir_lowering=False, num_devices=1)
    arrays = {n: np.ascontiguousarray(layout(n, np.asarray(inputs[n]))) for n in INPUTS} | constants()
    aps = {n: nc.dram_tensor(n, a.shape, mybir.dt.from_np(a.dtype), kind="ExternalInput").ap()
           for n, a in arrays.items()}
    out = nc.dram_tensor("out", (B, C, N), F32, kind="ExternalOutput").ap()
    attention_ffn_kernel(nc, out=out, **aps)
    r = run_bass_kernel_spmd(nc, [arrays], core_ids=[0])
    return r.results[0]["out"]
```

```python
import concourse.bass as bass
from concourse import mybir
from contextlib import ExitStack

F32 = mybir.dt.float32
F32R = mybir.dt.float32r
ALU = mybir.AluOpType
ACT = mybir.ActivationFunctionType
AX = mybir.AxisListType.X

P = 128
B = 16
C = 128
N = 1024
H, DH = 8, 64
HD = H * DH
T = HD // P
DL = DH // T
J = N // P
HALF = N // 2
LN_EPS = 1e-5
NORM_FLOOR = 1e-24

BOT, RDIM, NSLOT, TOPK, VB = 64, 48, 256, 8, 64
UH = N // 4
G = 4
NEG = -3.0e38
TAU_LOW, TAU_HIGH, EARLY_EXIT = 0.5, 2.0, 0.05


def wait(engine, sem, value):
    if isinstance(value, int) and value <= 0:
        return
    engine.wait_ge(sem, value)


def place(h):
    return (h % 2) * (H // 2) + h // 2


def attention_ffn_kernel(nc, x, ctx_4096, L0_xattn_Wq, L0_xattn_Wk, L0_xattn_Wv, L0_xattn_Wo, L0_xattn_bo,
                         L0_xattn_g, L0_ffn_Wq, L0_ffn_Wr, L0_ffn_aux_keys, L0_ffn_aux_values, L0_ffn_Wvd,
                         L0_ffn_Wvu, L0_ffn_Wu1, L0_ffn_bu1, L0_ffn_Wu2, L0_ffn_bu2, L0_ffn_gate_w1,
                         L0_ffn_gate_bias, L0_ffn_log_rel, identity, head_ones, select_q, out):
    ctx = ExitStack()
    with ctx:
        def sb(name, shape, dt=F32, scope=ctx):
            return scope.enter_context(nc.sbuf_tensor(name, shape, dt))

        def sem(name):
            return ctx.enter_context(nc.semaphore(name))

        X = sb("x_all", [P, B, N])
        ident = sb("ident", [P, P])
        ones = sb("ones", [P, P])
        var2 = sb("var2", [P, B, 1])
        mean2 = sb("mean2", [P, B, 1])
        half_neg = sb("half_neg", [P, B])

        def ps(name, shape):
            return ctx.enter_context(nc.psum_tensor(name, shape, F32))
        slot = [ps("slot0", [P, N]), ps("slot1", [P, N])]
        bcast = ps("bcast", [P, N])
        work = ps("work", [P, N])
        bank6, bank7 = work[:, 0:HALF], work[:, HALF:N]
        bank_q, bank_g = bcast[:, 0:HALF], bcast[:, HALF:N]

        k_slot = [slot[0], slot[1], slot[1], slot[1]]

        att = ExitStack()
        xn = sb("xn", [P, N], scope=att)
        xn_hi = sb("xn_hi", [P, N], F32R, att)
        xn_lo = sb("xn_lo", [P, N], F32R, att)
        ctx_hi = sb("ctx_hi", [P, N], F32R, att)
        ctx_lo = sb("ctx_lo", [P, N], F32R, att)
        WqT = [sb(f"WqT{s}", [P, HD], F32R, att) for s in ("_hi", "_lo")]
        WkT = [sb(f"WkT{s}", [P, HD], F32R, att) for s in ("_hi", "_lo")]
        ctx_in = sb("ctx_in", [P, N], scope=att)
        qred = sb("qred", [P, N], scope=att)
        qsb = sb("qsb", [P, T, N], scope=att)
        ek = sb("ek", [P, 2, N], scope=att)
        ekT = sb("ekT", [P, J, HD], scope=att)
        ctxT = sb("ctxT", [P, J, C], scope=att)
        qtot = sb("qtot", [P, N], scope=att)
        eq = sb("eq", [P, T, N], scope=att)
        U = sb("U", [P, H, C], scope=att)
        g_sb = sb("g_sb", [P, HD], scope=att)
        m_sb = sb("m_sb", [P, HD], scope=att)
        mt_sb = sb("mt_sb", [P, T, C], scope=att)
        o_sb = sb("o_sb", [P, N], scope=att)
        r_sb = sb("r_sb", [P, N], scope=att)
        sq_sb = sb("sq_sb", [P, N], scope=att)
        t_sb = sb("t_sb", [P, N], scope=att)
        l2c = sb("l2c", [P, J], scope=att)
        rn = sb("rn", [P, J], scope=att)
        rn_hl = sb("rn_hl", [P, 2 * J * H], F32R, att)
        rnT = sb("rnT", [P, P], F32R, att)
        sel_q = sb("sel_q", [P, J, P], F32R, att)
        same_head = sb("same_head", [P, P], scope=att)
        qm = sb("qm", [P, J * H], scope=att)
        qm_hl = sb("qm_hl", [P, 2 * J * H], F32R, att)
        qmT = sb("qmT", [P, P], F32R, att)
        nkm = sb("nkm", [P, T], scope=att)
        ksum = sb("ksum", [P, T], scope=att)
        krec = sb("krec", [P, T], scope=att)
        kscale = sb("kscale", [P, T], scope=att)
        st1 = sb("st1", [P, 12], scope=att)
        st2 = sb("st2", [P, 12], scope=att)
        mv1 = sb("mv1", [P, 2], scope=att)
        mv2 = sb("mv2", [P, 2], scope=att)
        ve = sb("ve", [P, 1], scope=att)
        rstd = sb("rstd", [P, 1], scope=att)
        nb = sb("nb", [P, 1], scope=att)
        bo = sb("bo", [P, 1], scope=att)
        g_in = sb("g_in", [P, 1], scope=att)
        gs = sb("gs", [P, 1], scope=att)
        Wq_in = eq[:, 1, 0:HD].rearrange("p (t c) -> p t c", t=T)
        Wk_in = eq[:, 1, HD:N].rearrange("p (t c) -> p t c", t=T)
        Wv_in = eq[:, 2, 0:HD].rearrange("p (t c) -> p t c", t=T)
        Wo_in = eq[:, 2, HD:N]
        WoT = eq[:, 3, 0:HD].rearrange("p (t c) -> p t c", t=T)
        selq_in = eq[:, 0, :].rearrange("p (j q) -> p j q", j=J)
        att.close()

        ffn = ExitStack()
        Wu1_in = sb("Wu1_in", [P, UH // P, N], scope=ffn)
        Wqv_in = sb("Wqv_in", [P, N], scope=ffn)
        values_in = sb("values_in", [P, NSLOT // P, N], scope=ffn)
        Wvu_in = sb("Wvu_in", [P, J, VB], scope=ffn)
        keys_in = sb("keys_in", [P, NSLOT // P, BOT], scope=ffn)
        Wr_in = sb("Wr_in", [RDIM, BOT], scope=ffn)
        bu1 = sb("bu1", [P, UH], scope=ffn)
        Wu2 = sb("Wu2", [P, UH], scope=ffn)
        bu2 = sb("bu2", [P, 1], scope=ffn)
        gate_w = sb("gate_w", [P, 1], scope=ffn)
        gate_b = sb("gate_b", [P, 1], scope=ffn)
        WuqT = [sb(f"WuqT{s}", [P, J, UH + BOT], F32R, ffn) for s in ("_hi", "_lo")]
        WvdT = sb("WvdT", [P, J, VB], scope=ffn)
        valuesT = sb("valuesT", [P, J, NSLOT], scope=ffn)
        WvuT = sb("WvuT", [P, N], scope=ffn)
        WrT = sb("WrT", [BOT, RDIM], scope=ffn)
        keysT = sb("keysT", [BOT, NSLOT], scope=ffn)
        rkT = sb("rkT", [RDIM, NSLOT], scope=ffn)
        VV = sb("VV", [P, NSLOT // P, P], scope=ffn)
        scoreB = sb("scoreB", [P, 2 * NSLOT], scope=ffn)
        half3 = sb("half3", [P, 3], scope=ffn)
        hbuf = sb("hbuf", [P, 2, N], scope=ffn)
        q_rows = sb("q_rows", [P, 2, P], scope=ffn)
        ve2 = sb("ve2", [P, B], scope=ffn)
        rstd2 = sb("rstd2", [P, B, 1], scope=ffn)
        nb2 = sb("nb2", [P, B, 1], scope=ffn)
        varh = sb("varh", [P, B], scope=ffn)
        logv = sb("logv", [P, B], scope=ffn)
        logsum = sb("logsum", [P, 1], scope=ffn)
        logmean = sb("logmean", [P, 1], scope=ffn)
        logrec = sb("logrec", [P, 1], scope=ffn)
        normv = sb("normv", [P, B], scope=ffn)
        hT = [sb(f"hT{s}", [P, 2, J, C], F32R, ffn) for s in ("_hi", "_lo")]
        units = sb("units", [P, 2, UH], scope=ffn)
        query = sb("query", [P, B, C], scope=ffn)
        q_now = sb("q_now", [P, 2, C], scope=ffn)
        learned = sb("learned", [P, B, 1], scope=ffn)
        top8 = sb("top8", [P, 2, TOPK], scope=ffn)
        replaced = sb("replaced", [P, NSLOT], scope=ffn)
        outside = sb("outside", [P, NSLOT], scope=ffn)
        logits = sb("logits", [P, 2, NSLOT], scope=ffn)
        nlmax = sb("nlmax", [P, 2], scope=ffn)
        w_sb = sb("w_sb", [P, 2, NSLOT], scope=ffn)
        wsum = sb("wsum", [P, B, 1], scope=ffn)
        wrec = sb("wrec", [P, 1], scope=ffn)
        oscale = sb("oscale", [P, 1], scope=ffn)
        wT = sb("wT", [P, NSLOT // P, C], scope=ffn)
        zT = sb("zT", [P, 2, C], scope=ffn)
        ga = sb("ga", [P, B], scope=ffn)
        gb = sb("gb", [P, B], scope=ffn)
        gate = sb("gate", [P, B, 1], scope=ffn)
        y_out = sb("y_out", [P, 2, N], scope=ffn)
        ffn.close()

        proj_in = sem("proj_in")
        weights_in = sem("weights_in")
        waits_apart = sem("waits_apart")
        x_in = sem("x_in")
        ctx_loaded = sem("ctx_loaded")
        consts = sem("consts")
        setup_T = sem("setup_T")
        setup_w = sem("setup_w")
        setup_u = sem("setup_u")
        u_done = sem("u_done")
        wo_copied = sem("wo_copied")
        x_split = sem("x_split")
        x_norm = sem("x_norm")
        x_stats = sem("x_stats")
        x_mv = sem("x_mv")
        x_ve = sem("x_ve")
        x_rstd = sem("x_rstd")
        x_nb = sem("x_nb")
        x_hi = sem("x_hi")
        ctx_hi_done = sem("ctx_hi_done")
        ctx_lo_done = sem("ctx_lo_done")
        q_prod = sem("q_prod")
        q_evac = sem("q_evac")
        k_prod = sem("k_prod")
        k_max = sem("k_max")
        k_exp = sem("k_exp")
        k_T = sem("k_T")
        ekT_front = sem("ekT_front")
        ekT_back = sem("ekT_back")
        ctxT_prod = sem("ctxT_prod")
        ctxT_front = sem("ctxT_front")
        ctxT_back = sem("ctxT_back")
        qmax_step = sem("qmax_step")
        qmax_T = sem("qmax_T")
        qm_done = sem("qm_done")
        qm_hi_done = sem("qm_hi_done")
        qm_split = sem("qm_split")
        qm_T = sem("qm_T")
        qmT_copied = sem("qmT_copied")
        qshift = sem("qshift")
        q_sub = sem("q_sub")
        q_exp = sem("q_exp")
        qsum_step = sem("qsum_step")
        q_sum = sem("q_sum")
        r_done = sem("r_done")
        q_mul = sem("q_mul")
        krec_done = sem("krec_done")
        kscale_done = sem("kscale_done")
        g_prod = sem("g_prod")
        g_copied = sem("g_copied")
        m_prod = sem("m_prod")
        m_copied = sem("m_copied")
        mt_T = sem("mt_T")
        mt_copied = sem("mt_copied")
        out_prod = sem("out_prod")
        o_copied = sem("o_copied")
        o_squared = sem("o_squared")
        ss_prod = sem("ss_prod")
        l2_clamped = sem("l2_clamped")
        rn_pow = sem("rn_pow")
        rn_hi_done = sem("rn_hi_done")
        rn_split = sem("rn_split")
        rn_T = sem("rn_T")
        rnT_copied = sem("rnT_copied")
        rn_spread = sem("rn_spread")
        t_scaled = sem("t_scaled")
        x1_done = sem("x1_done")
        stats2 = sem("stats2")
        mv2_done = sem("mv2_done")
        var2_done = sem("var2_done")
        ffn_in = sem("ffn_in")
        log_rel_in = sem("log_rel_in")
        out_stored = sem("out_stored")
        ffn_zeros = sem("ffn_zeros")
        wu1_T = sem("wu1_T")
        wu1_hi = sem("wu1_hi")
        wu1_lo = sem("wu1_lo")
        wqv_T = sem("wqv_T")
        wq_hi = sem("wq_hi")
        wq_lo = sem("wq_lo")
        wvd_copied = sem("wvd_copied")
        val_copied = sem("val_copied")
        wvu_T = sem("wvu_T")
        wvu_copied = sem("wvu_copied")
        key_copied = sem("key_copied")
        rstd2_done = sem("rstd2_done")
        query_ones = sem("query_ones")
        score_ready = sem("score_ready")
        val_T = sem("val_T")
        vv_prod = sem("vv_prod")
        vv_copied = sem("vv_copied")
        key_T = sem("key_T")
        rk_prod = sem("rk_prod")
        rk_copied = sem("rk_copied")
        b1_prod = sem("b1_prod")
        ve2_done = sem("ve2_done")
        nb2_done = sem("nb2_done")
        varh_step = sem("varh_step")
        logv_done = sem("logv_done")
        logsum_done = sem("logsum_done")
        logtotal = sem("logtotal")
        normv_step = sem("normv_step")
        h_done = sem("h_done")
        y_done = sem("y_done")
        h_T = sem("h_T")
        hT_hi_done = sem("hT_hi_done")
        hT_lo_done = sem("hT_lo_done")
        units_prod = sem("units_prod")
        units_biased = sem("units_biased")
        q_copied = sem("q_copied")
        q_T = sem("q_T")
        query_done = sem("query_done")
        q_fetched = sem("q_fetched")
        gelu_done = sem("gelu_done")
        gelu_weighted = sem("gelu_weighted")
        learned_done = sem("learned_done")
        gate_tanh = sem("gate_tanh")
        gate_step = sem("gate_step")
        gate_arg = sem("gate_arg")
        gate_done = sem("gate_done")
        scores = sem("scores")
        top_step = sem("top_step")
        masked = sem("masked")
        outside_done = sem("outside_done")
        logits_ready = sem("logits_ready")
        w_done = sem("w_done")
        w_T = sem("w_T")
        wT_copied = sem("wT_copied")
        z_prod = sem("z_prod")
        z_copied = sem("z_copied")
        f_prod = sem("f_prod")
        wrec_done = sem("wrec_done")
        oscale_done = sem("oscale_done")
        y_ready = sem("y_ready")

        block = ctx.enter_context(nc.Block())

        ATT_DMAS, FFN_DMAS = 6, 12

        def wait_apart(engine, sem, value):
            wait(engine, sem, value)
            engine.sem_inc(waits_apart, 1)

        @block.sync
        def _(sp):
            def load(b):
                wait_apart(sp, x_in, 16 * b)
                sp.dma_start(X[:, b, :], x[b]).then_inc(x_in, 16)
                wait_apart(sp, ctx_hi_done, b)
                wait_apart(sp, ctx_lo_done, b)
                wait_apart(sp, ctxT_prod, 2 * b)
                sp.dma_start(ctx_in[:, :], ctx_4096[b]).then_inc(ctx_loaded, 16)

            load(0)
            sp.dma_start(ident[:, :], identity).then_inc(proj_in, 16)
            for src, dst in ((L0_xattn_Wq, Wq_in), (L0_xattn_Wk, Wk_in)):
                sp.dma_start(dst, src.rearrange("(t p) c -> p t c", p=P)).then_inc(proj_in, 16)
            sp.dma_start(Wo_in, L0_xattn_Wo).then_inc(weights_in, 16)
            sp.dma_start(Wv_in, L0_xattn_Wv.rearrange("(t p) c -> p t c", p=P)).then_inc(weights_in, 16)
            sp.dma_start(selq_in, select_q).then_inc(weights_in, 16)
            sp.dma_start(same_head[:, :], head_ones).then_inc(weights_in, 16)
            sp.dma_start(bo[:, :], L0_xattn_bo).then_inc(weights_in, 16)
            sp.dma_start(g_in[:, :], L0_xattn_g).then_inc(weights_in, 16)

            with sp.Fori(1, B) as b:
                load(b)

            sp.wait_ge(q_prod, 4 * B)
            sp.wait_ge(k_prod, 4 * B)
            for src, dst in (
                (L0_ffn_Wu1.rearrange("(s p) n -> p s n", p=P), Wu1_in[:, :, :]),
                (L0_ffn_Wq, Wqv_in[0:BOT, :]),
                (L0_ffn_Wvd, Wqv_in[BOT:P, :]),
                (L0_ffn_aux_values.rearrange("(s p) n -> p s n", p=P), values_in[:, :, :]),
                (L0_ffn_Wvu.rearrange("(j p) v -> p j v", p=P), Wvu_in[:, :, :]),
                (L0_ffn_aux_keys.rearrange("(s p) d -> p s d", p=P), keys_in[:, :, :]),
                (L0_ffn_Wr, Wr_in[:, :]),
                (L0_ffn_bu1.broadcast_to([P, UH]), bu1[:, :]),
                (L0_ffn_Wu2.broadcast_to([P, UH]), Wu2[:, :]),
                (L0_ffn_bu2.broadcast_to([P, 1]), bu2[:, :]),
                (L0_ffn_gate_w1.broadcast_to([P, 1]), gate_w[:, :]),
                (L0_ffn_gate_bias.broadcast_to([P, 1]), gate_b[:, :]),
            ):
                sp.dma_start(dst, src).then_inc(ffn_in, 16)
            sp.wait_ge(ffn_zeros, 1)
            for n in range(2):
                sp.dma_start(scoreB[BOT:BOT + 1, n * NSLOT:(n + 1) * NSLOT], L0_ffn_log_rel).then_inc(log_rel_in, 16)

            def store(b, k):
                wait_apart(sp, out_stored, 16 * b)
                wait_apart(sp, y_ready, b + 1)
                sp.dma_start(out[b], y_out[:, k % 2, :]).then_inc(out_stored, 16)

            store(0, 0)
            store(1, 1)
            with sp.Fori(1, B // 2) as g:
                for k in range(2):
                    store(2 * g + k, k)
            sp.wait_ge(out_stored, 16 * B)

        @block.tensor
        def _(pe):
            pe.wait_ge(proj_in, 16 * 3)
            for dst, src in ((bank6, Wq_in), (bank7, Wk_in)):
                for t in range(T):
                    last = nc.tensor.transpose(dst[:, t * P:(t + 1) * P], src[:, t, :], ident[:, :])
                last.then_inc(setup_T, 1)
            pe.wait_ge(weights_in, 16 * ATT_DMAS)
            for t in range(T):
                last = nc.tensor.transpose(bank_q[:, t * P:(t + 1) * P], Wo_in[:, t * P:(t + 1) * P], ident[:, :])
            last.then_inc(setup_T, 1)
            pe.wait_ge(setup_w, 4)

            def head_products():
                pe.wait_ge(wo_copied, 1)
                for h in range(H):
                    r = DH * (h % 2)
                    last = nc.tensor.matmul(bcast[:, place(h) * C:(place(h) + 1) * C], Wv_in[r:r + DH, h // 2, :],
                                            WoT[r:r + DH, h // 2, :], start=True, stop=True)
                last.then_inc(setup_u, 1)

            def product(dst, lhs, rhs):
                nc.tensor.matmul(dst, lhs[0], rhs[0], start=True, stop=False)
                nc.tensor.matmul(dst, lhs[1], rhs[0], start=False, stop=False)
                return nc.tensor.matmul(dst, lhs[0], rhs[1], start=False, stop=True)

            def q_tile(b, t):
                for n in range(2):
                    cols = slice(n * HALF, (n + 1) * HALF)
                    last = product(slot[t % 2][:, cols], [w[:, t * P:(t + 1) * P] for w in WqT],
                                   [xn_hi[:, cols], xn_lo[:, cols]])
                last.then_inc(q_prod, 1)

            def k_tile(b, t):
                for n in range(2):
                    cols = slice(n * HALF, (n + 1) * HALF)
                    last = product(k_slot[t][:, cols], [w[:, t * P:(t + 1) * P] for w in WkT],
                                   [ctx_hi[:, cols], ctx_lo[:, cols]])
                last.then_inc(k_prod, 1)

            def blocks_T(src, done):
                for j in range(J):
                    last = nc.tensor.transpose(work[:, j * P:(j + 1) * P], src[:, j * P:(j + 1) * P], ident[:, :])
                    if j % 4 == 3:
                        last.then_inc(done, 1)

            def k_transpose(b, t):
                pe.wait_ge(k_exp, 4 * b + t + 1)
                if t:
                    pe.wait_ge(ekT_front, 4 * b + t)
                    pe.wait_ge(ekT_back, 4 * b + t)
                else:
                    pe.wait_ge(ctxT_front, b + 1)
                    pe.wait_ge(ctxT_back, b + 1)
                blocks_T(ek[:, t % 2, :], k_T)

            def ctx_transpose(b):
                wait(pe, r_done, 2 * b)
                blocks_T(ctx_in, ctxT_prod)

            def q_max_T(b, n):
                if n == 0:
                    pe.wait_ge(u_done, 1)
                    pe.wait_ge(qmax_step, 3 * (b + 1))
                    wait(pe, t_scaled, 2 * (b - 1))
                else:
                    pe.wait_ge(qm_done, 2 * b + 1)
                for j in range(4):
                    last = nc.tensor.transpose(bank_q[:, j * P:(j + 1) * P],
                                               qred[:, n * HALF + j * P:n * HALF + (j + 1) * P], ident[:, :])
                last.then_inc(qmax_T, 1)

            def q_max_turn(b):
                pe.wait_ge(qm_split, b + 1)
                nc.tensor.transpose(bank_q[:, 0:P], qm_hl[:, :].bitcast(F32), ident[:, :]).then_inc(qm_T, 1)

            def q_shift_spread(b, n):
                if n == 0:
                    pe.wait_ge(qmT_copied, b + 1)
                else:
                    pe.wait_ge(q_sub, 2 * b + 1)
                for j in range(4):
                    last = nc.tensor.matmul(bank_q[:, j * P:(j + 1) * P], sel_q[:, 4 * n + j, :], qmT[:, :],
                                            start=True, stop=True)
                last.then_inc(qshift, 1)

            def q_denominator(b, n):
                pe.wait_ge(qsum_step, 6 * b + 3 * (n + 1))
                if n == 0:
                    pe.wait_ge(q_sub, 2 * (b + 1))
                else:
                    pe.wait_ge(ekT_back, 4 * (b + 1))
                nc.tensor.matmul((bank_q, bank7)[n], same_head[:, :], qtot[:, n * HALF:(n + 1) * HALF], start=True,
                                 stop=True).then_inc(q_sum, 1)

            def norm_turn(b, halves):
                pe.wait_ge(rn_split, b + 1)
                pe.wait_ge(r_done, halves)
                nc.tensor.transpose(bank_q[:, 0:P], rn_hl[:, :].bitcast(F32), ident[:, :]).then_inc(rn_T, 1)

            def norm_spread(b, n):
                if n == 0:
                    pe.wait_ge(rnT_copied, b + 1)
                else:
                    pe.wait_ge(t_scaled, 2 * b + 1)
                for j in range(4):
                    last = nc.tensor.matmul(bank_q[:, j * P:(j + 1) * P], sel_q[:, 4 * n + j, :], rnT[:, :],
                                            start=True, stop=True)
                last.then_inc(rn_spread, 1)

            def g_tile(b, t):
                if t == 0:
                    wait(pe, mt_copied, b)
                pe.wait_ge(ekT_front, 4 * b + t + 1)
                pe.wait_ge(ekT_back, 4 * b + t + 1)
                for j in range(J):
                    last = nc.tensor.matmul(bank_g[:, t * P:(t + 1) * P], ctxT[:, j, :],
                                            ekT[:, j, t * P:(t + 1) * P], start=(j == 0), stop=(j == J - 1))
                last.then_inc(g_prod, 1)

            def m_product(b):
                pe.wait_ge(g_copied, b + 1)
                gv = g_sb[:, :].rearrange("p (t h d) -> p t h d", t=T, h=H)
                mv = bank_g.rearrange("p (t h d) -> p t h d", t=T, h=H)
                for h in range(H):
                    last = nc.tensor.matmul(mv[:, :, h, :], U[:, place(h), :], gv[:, :, h, :], start=True, stop=True)
                last.then_inc(m_prod, 1)

            def m_transpose(b):
                pe.wait_ge(m_copied, b + 1)
                for t in range(T):
                    last = nc.tensor.transpose(bank_g[:, t * P:(t + 1) * P], m_sb[:, t * P:(t + 1) * P], ident[:, :])
                last.then_inc(mt_T, 1)

            def out_half(b, n, slot_free):
                if slot_free is not None:
                    pe.wait_ge(k_exp, slot_free)
                pe.wait_ge(q_mul, 2 * b + n + 1)
                pe.wait_ge(mt_copied, b + 1)
                cols = slice(n * HALF, (n + 1) * HALF)
                for t in range(T):
                    last = nc.tensor.matmul(slot[0][:, cols], mt_sb[:, t, :], eq[:, t, cols],
                                            start=(t == 0), stop=(t == T - 1))
                last.then_inc(out_prod, 1)

            def square_sums(b):
                pe.wait_ge(o_squared, 2 * (b + 1))
                for j in range(J):
                    last = nc.tensor.matmul(slot[0][:, j:j + 1], sq_sb[:, j * P:(j + 1) * P],
                                            ones[:, 0:1], start=True, stop=True)
                last.then_inc(ss_prod, 1)

            def body(b, lag):
                p = b - 1
                pe.wait_ge(x_split, b + 1)
                wait(pe, k_exp, 4 * b - 3)
                wait(pe, l2_clamped, b - 1)
                q_tile(b, 0)
                if lag:
                    q_denominator(p, 0)
                    k_transpose(p, 3)
                wait(pe, k_exp, 4 * b)
                q_tile(b, 1)
                if lag:
                    g_tile(p, 3)
                if lag > 1:
                    norm_turn(p - 1, 2 * p + 1)
                pe.wait_ge(q_evac, 4 * b + 1)
                q_tile(b, 2)
                if lag > 1:
                    norm_spread(p - 1, 0)
                if lag:
                    q_denominator(p, 1)
                    m_product(p)
                else:
                    head_products()
                if lag > 1:
                    norm_spread(p - 1, 1)
                pe.wait_ge(q_evac, 4 * b + 2)
                q_tile(b, 3)
                pe.wait_ge(ctx_hi_done, b + 1)
                pe.wait_ge(ctx_lo_done, b + 1)
                pe.wait_ge(q_evac, 4 * b + 3)
                k_tile(b, 0)
                if lag:
                    m_transpose(p)
                ctx_transpose(b)
                pe.wait_ge(q_evac, 4 * b + 4)
                k_tile(b, 1)
                q_max_T(b, 0)
                k_transpose(b, 0)
                if lag:
                    out_half(p, 0, 4 * b + 1)
                q_max_T(b, 1)
                g_tile(b, 0)
                pe.wait_ge(k_exp, 4 * b + 2)
                k_tile(b, 2)
                k_transpose(b, 1)
                q_max_turn(b)
                if lag:
                    out_half(p, 1, None)
                q_shift_spread(b, 0)
                pe.wait_ge(k_exp, 4 * b + 3)
                k_tile(b, 3)
                k_transpose(b, 2)
                if lag:
                    square_sums(p)
                g_tile(b, 1)
                q_shift_spread(b, 1)
                g_tile(b, 2)
            body(0, 0)
            body(1, 1)
            body(2, 2)
            with pe.Fori(3, B) as b:
                body(b, 2)

            def wide_T(src, n, dst, done):
                for j in range(4 * n, 4 * n + 4):
                    for s in range(2):
                        last = nc.tensor.transpose(dst[:, (j % 4) * UH + s * P:(j % 4) * UH + (s + 1) * P],
                                                   src[:, s, j * P:(j + 1) * P], ident[:, :])
                last.then_inc(done, 1)

            z = B - 1
            q_denominator(z, 0)
            k_transpose(z, 3)
            g_tile(z, 3)
            norm_turn(z - 1, 2 * z + 1)
            norm_spread(z - 1, 0)
            q_denominator(z, 1)
            m_product(z)
            norm_spread(z - 1, 1)
            m_transpose(z)
            pe.wait_ge(ffn_in, 16 * FFN_DMAS)
            wide_T(Wu1_in, 0, slot[1], wu1_T)
            out_half(z, 0, None)
            pe.wait_ge(r_done, 2 * B)
            wide_T(Wu1_in, 1, work, wu1_T)
            out_half(z, 1, None)
            pe.wait_ge(wu1_hi, 1)
            pe.wait_ge(wu1_lo, 1)
            for j in range(J):
                last = nc.tensor.transpose(slot[1][:, j * P:(j + 1) * P], Wqv_in[:, j * P:(j + 1) * P], ident[:, :])
            last.then_inc(wqv_T, 1)
            square_sums(z)
            pe.wait_ge(wu1_hi, 2)
            pe.wait_ge(wu1_lo, 2)
            wide_T(values_in, 0, work, val_T)
            pe.wait_ge(l2_clamped, B)
            for j in range(J):
                last = nc.tensor.transpose(slot[0][0:VB, j * P:(j + 1) * P], Wvu_in[:, j, :], ident[:, :])
            last.then_inc(wvu_T, 1)
            pe.wait_ge(wq_hi, 1)
            pe.wait_ge(wq_lo, 1)
            pe.wait_ge(wvd_copied, 1)
            wide_T(values_in, 1, slot[1], val_T)
            norm_turn(z, 2 * B)
            norm_spread(z, 0)
            pe.wait_ge(val_copied, 1)
            for s in range(2):
                nc.tensor.transpose(bank6[0:BOT, s * P:(s + 1) * P], keys_in[:, s, :], ident[:, :])
            nc.tensor.transpose(bank6[0:BOT, NSLOT:NSLOT + RDIM], Wr_in[:, :],
                                ident[0:RDIM, 0:RDIM]).then_inc(key_T, 1)
            norm_spread(z, 1)
            pe.wait_ge(key_copied, 2)
            nc.tensor.matmul(bank7[0:RDIM, 0:NSLOT], WrT[:, :], keysT[:, :], start=True, stop=True).then_inc(rk_prod, 1)
            pe.wait_ge(rk_copied, 1)
            nc.tensor.matmul(bank6[0:BOT, 0:NSLOT], Wr_in[:, :], rkT[:, :], start=True, stop=True).then_inc(b1_prod, 1)

            pe.wait_ge(wvu_copied, 1)
            pe.wait_ge(val_copied, 2)
            pe.wait_ge(t_scaled, 2 * B)
            pe.wait_ge(mt_copied, B)

            def h_transpose(b, k):
                pe.wait_ge(h_done, b + 1)
                wait(pe, hT_hi_done, b - 1)
                wait(pe, hT_lo_done, b - 1)
                for j in range(J):
                    last = nc.tensor.transpose(slot[k][:, j * P:(j + 1) * P], hbuf[:, k, j * P:(j + 1) * P],
                                               ident[:, :])
                last.then_inc(h_T, 1)

            def hidden_products(b, k):
                pe.wait_ge(hT_hi_done, b + 1)
                pe.wait_ge(hT_lo_done, b + 1)
                wait(pe, units_biased, b - 1)
                wait(pe, q_copied, b - 1)
                for j in range(J):
                    for n, (a, c) in enumerate(((0, 0), (1, 0), (0, 1))):
                        last = nc.tensor.matmul(bcast[:, k * HALF:k * HALF + UH + BOT], hT[a][:, k, j, :],
                                                WuqT[c][:, j, :], start=(j == 0 and n == 0),
                                                stop=(j == J - 1 and n == 2))
                last.then_inc(units_prod, 1)

            def query_transpose(b, k):
                pe.wait_ge(q_copied, b + 1)
                wait(pe, query_done, b - 1)
                nc.tensor.transpose((bank6, bank7)[k][:, 0:P], q_rows[:, k, :], ident[:, :]).then_inc(q_T, 1)

            def value_products():
                pe.wait_ge(units_biased, 1)
                pe.wait_ge(q_copied, 1)
                for s in range(NSLOT // P):
                    for j in range(J):
                        last = nc.tensor.matmul(bcast[:, s * VB:(s + 1) * VB], valuesT[:, j, s * P:(s + 1) * P],
                                                WvdT[:, j, :], start=(j == 0), stop=(j == J - 1))
                last.then_inc(vv_prod, 1)

            def hidden_step(b, k, values=False):
                if not isinstance(b, int) or b + 1 < B:
                    h_transpose(b + 1, 1 - k)
                if not isinstance(b, int) or b >= 1:
                    query_transpose(b - 1, 1 - k)
                if values:
                    value_products()
                if not isinstance(b, int) or b < B:
                    hidden_products(b, k)

            h_transpose(0, 0)
            hidden_step(0, 0)
            pe.wait_ge(query_ones, 1)
            pe.wait_ge(score_ready, 3)
            hidden_step(1, 1, values=True)
            pe.wait_ge(vv_copied, 1)
            with pe.Fori(1, B // 2 - 1) as g:
                hidden_step(2 * g, 0)
                hidden_step(2 * g + 1, 1)
            hidden_step(B - 2, 0)
            hidden_step(B - 1, 1)
            hidden_step(B, 0)

            def score(b, k):
                pe.wait_ge(q_fetched, b + 1)
                wait(pe, logits_ready, b - 1)
                nc.tensor.matmul((bank6, bank7)[k], q_now[:, k, :], scoreB[:, :], start=True,
                                 stop=True).then_inc(scores, 1)

            def w_transpose(b, k):
                pe.wait_ge(w_done, b + 1)
                wait(pe, wT_copied, b)
                for s in range(NSLOT // P):
                    last = nc.tensor.transpose(bcast[:, s * C:(s + 1) * C], w_sb[:, k, s * P:(s + 1) * P],
                                               ident[:, :])
                last.then_inc(w_T, 1)

            def z_product(b):
                pe.wait_ge(wT_copied, b + 1)
                wait(pe, z_copied, b)
                for s in range(NSLOT // P):
                    last = nc.tensor.matmul(bcast[:, HALF:HALF + C], VV[:, s, :], wT[:, s, :],
                                            start=(s == 0), stop=(s == NSLOT // P - 1))
                last.then_inc(z_prod, 1)

            def f_product(b, k):
                pe.wait_ge(z_copied, b + 1)
                wait(pe, y_ready, b - 1)
                for n in range(2):
                    last = nc.tensor.matmul(slot[k][:, n * HALF:(n + 1) * HALF], zT[:, k, :],
                                            WvuT[:, n * HALF:(n + 1) * HALF], start=True, stop=True)
                last.then_inc(f_prod, 1)

            def value_step(b, k, new=True, old=True, older=True):
                if new:
                    score(b, k)
                if old:
                    w_transpose(b - 1, 1 - k)
                if older:
                    f_product(b - 2, k)
                if old:
                    z_product(b - 1)

            pe.wait_ge(units_biased, B)
            pe.wait_ge(log_rel_in, 16 * 2)
            pe.wait_ge(ffn_zeros, 3)
            pe.wait_ge(q_copied, B)
            value_step(0, 0, old=False, older=False)
            pe.wait_ge(logsum_done, 1)
            nc.tensor.matmul(slot[1][:, 0:1], ones[:, :], logsum[:, :], start=True, stop=True).then_inc(logtotal, 1)
            value_step(1, 1, older=False)
            value_step(2, 0)
            value_step(3, 1)
            with pe.Fori(2, B // 2) as g:
                value_step(2 * g, 0)
                value_step(2 * g + 1, 1)
            value_step(B, 0, new=False)
            value_step(B + 1, 1, new=False, old=False)

        @block.scalar
        def _(act):
            def ctx_high(b):
                act.wait_ge(ctx_loaded, 16 * (b + 1))
                wait(act, k_prod, 4 * b)
                wait(act, ctx_lo_done, b)
                nc.scalar.copy(ctx_hi[:, :], ctx_in[:, :]).then_inc(ctx_hi_done, 1)

            def x_layernorm(b):
                act.wait_ge(x_in, 16 * (b + 1))
                act.wait_ge(x_rstd, b + 1)
                act.wait_ge(x_nb, b + 1)
                wait(act, x_split, b)
                nc.scalar.activation(xn[:, :], X[:, b, :], ACT.Identity, bias=nb[:, :],
                                     scale=rstd[:, :]).then_inc(x_norm, 1)
                act.wait_ge(x_norm, b + 1)
                wait(act, q_prod, 4 * b)
                nc.scalar.copy(xn_hi[:, :], xn[:, :]).then_inc(x_hi, 1)

            def q_copy(b, t):
                act.wait_ge(q_prod, 4 * b + t + 1)
                wait(act, q_exp, 2 * b)
                nc.scalar.copy(qsb[:, t, :], slot[t % 2][:, :]).then_inc(q_evac, 1)

            def k_exponential(b, t):
                act.wait_ge(k_max, 4 * b + t + 1)
                wait(act, k_T, 8 * b + 2 * t - 2)
                wait(act, krec_done, b)
                nc.scalar.activation(ek[:, t % 2, :], k_slot[t][:, :], ACT.Exp, bias=nkm[:, t:t + 1],
                                     accum_out=ksum[:, t:t + 1]).then_inc(k_exp, 1)

            def k_front(b, t):
                act.wait_ge(k_T, 8 * b + 2 * t + 1)
                wait(act, g_prod, 4 * b)
                nc.scalar.copy(ekT[:, 0:4, t * P:(t + 1) * P],
                               bank6.rearrange("p (j d) -> p j d", d=P)).then_inc(ekT_front, 1)

            def k_back(b, t):
                act.wait_ge(k_T, 8 * b + 2 * t + 2)
                nc.scalar.copy(ekT[:, 4:J, t * P:(t + 1) * P],
                               bank7.rearrange("p (j d) -> p j d", d=P)).then_inc(ekT_back, 1)

            def ctx_front(b):
                act.wait_ge(ctxT_prod, 2 * b + 1)
                wait(act, g_prod, 4 * b)
                nc.scalar.copy(ctxT[:, 0:4, :], bank6.rearrange("p (j c) -> p j c", c=P)).then_inc(ctxT_front, 1)

            def out_copy(p, n):
                cols = slice(n * HALF, (n + 1) * HALF)
                act.wait_ge(out_prod, 2 * p + n + 1)
                wait(act, t_scaled, 2 * p)
                nc.scalar.activation(o_sb[:, cols], slot[0][:, cols], ACT.Identity,
                                     bias=bo[:, :]).then_inc(o_copied, 1)
                act.wait_ge(o_copied, 2 * p + n + 1)
                wait(act, ss_prod, p)
                nc.scalar.activation(sq_sb[:, cols], o_sb[:, cols], ACT.Square).then_inc(o_squared, 1)

            def q_exponential(b, n):
                cols = slice(n * HALF, (n + 1) * HALF)
                act.wait_ge(q_sub, 2 * b + n + 1)
                wait(act, out_prod, 2 * b)
                nc.scalar.activation(eq[:, :, cols], qsb[:, :, cols], ACT.Exp).then_inc(q_exp, 1)

            def g_copy(p):
                act.wait_ge(g_prod, 4 * (p + 1))
                wait(act, m_prod, p)
                nc.scalar.copy(g_sb[:, :], bank_g).then_inc(g_copied, 1)

            def m_copy(p):
                act.wait_ge(m_prod, p + 1)
                wait(act, mt_T, p)
                nc.scalar.copy(m_sb[:, :], bank_g).then_inc(m_copied, 1)

            def body(b, lag, more):
                p = b - 1
                if lag:
                    k_front(p, 3)
                    k_back(p, 3)
                q_copy(b, 0)
                q_copy(b, 1)
                if lag:
                    g_copy(p)
                q_copy(b, 2)
                if lag:
                    m_copy(p)
                q_copy(b, 3)
                ctx_front(b)
                k_exponential(b, 0)
                k_front(b, 0)
                k_exponential(b, 1)
                if lag:
                    out_copy(p, 0)
                if more:
                    x_layernorm(b + 1)
                k_front(b, 1)
                k_exponential(b, 2)
                if lag:
                    out_copy(p, 1)
                q_exponential(b, 0)
                k_front(b, 2)
                k_exponential(b, 3)
                if more:
                    ctx_high(b + 1)
                q_exponential(b, 1)
            x_layernorm(0)
            ctx_high(0)
            act.wait_ge(weights_in, 16 * ATT_DMAS)
            body(0, 0, True)
            body(1, 1, True)
            body(2, 2, True)
            with act.Fori(3, B - 1) as b:
                body(b, 2, True)
            body(B - 1, 2, False)

            def wu1_high(n):
                act.wait_ge(wu1_T, n + 1)
                nc.scalar.copy(WuqT[0][:, 4 * n:4 * n + 4, 0:UH],
                               (slot[1], work)[n][:, :].rearrange("p (j u) -> p j u", u=UH)).then_inc(wu1_hi, 1)

            def values_copy(n):
                act.wait_ge(val_T, n + 1)
                nc.scalar.copy(valuesT[:, 4 * n:4 * n + 4, :].rearrange("p j u -> p (j u)"),
                               (work, slot[1])[n][:, :]).then_inc(val_copied, 1)

            z = B - 1
            k_front(z, 3)
            k_back(z, 3)
            g_copy(z)
            m_copy(z)
            wu1_high(0)
            out_copy(z, 0)
            wu1_high(1)
            out_copy(z, 1)
            act.wait_ge(wqv_T, 1)
            nc.scalar.copy(WuqT[0][:, :, UH:UH + BOT],
                           slot[1][:, :].rearrange("p (j d) -> p j d", j=J)[:, :, 0:BOT]).then_inc(wq_hi, 1)
            values_copy(0)
            act.wait_ge(wvu_T, 1)
            nc.scalar.copy(WvuT[0:VB, :], slot[0][0:VB, :]).then_inc(wvu_copied, 1)
            values_copy(1)

            def h_scale(b, k, part=2):
                act.wait_ge(nb2_done, part)
                wait(act, h_T, b - 1)
                wait(act, y_done, b - 1)
                nc.scalar.activation(hbuf[:, k, :], X[:, b, :], ACT.Identity, bias=nb2[:, b, :],
                                     scale=rstd2[:, b, :]).then_inc(h_done, 1)

            def hT_high(b, k):
                act.wait_ge(h_T, b + 1)
                wait(act, units_prod, b - 1)
                nc.scalar.copy(hT[0][:, k, :, :], slot[k][:, :].rearrange("p (j c) -> p j c", j=J)).then_inc(hT_hi_done, 1)

            def unit_gelu(b, k):
                act.wait_ge(units_biased, b + 1)
                nc.scalar.activation(units[:, k, :], units[:, k, :], ACT.Gelu_apprx_tanh).then_inc(gelu_done, 1)

            def unit_sum(b, k):
                act.wait_ge(gelu_weighted, b + 1)
                nc.scalar.activation(units[:, k, :], units[:, k, :], ACT.Identity,
                                     accum_out=learned[:, b, :]).then_inc(learned_done, 1)

            def hidden_step(b, k, old=True, new=True, after=True, part=2):
                if new:
                    hT_high(b + 1, 1 - k)
                if old:
                    unit_gelu(b - 1, 1 - k)
                if after:
                    h_scale(b + 2, k, part)
                if old:
                    unit_sum(b - 1, 1 - k)

            h_scale(0, 0, part=1)
            h_scale(1, 1, part=1)
            hT_high(0, 0)
            hidden_step(0, 0, old=False, part=1)
            hidden_step(1, 1, part=1)
            with act.Fori(1, B // 2 - 1) as g:
                hidden_step(2 * g, 0)
                hidden_step(2 * g + 1, 1)
            hidden_step(B - 2, 0, after=False)
            hidden_step(B - 1, 1, new=False, after=False)
            unit_gelu(B - 1, 1)
            act.wait_ge(varh_step, 2)
            nc.scalar.activation(logv[:, :], varh[:, :], ACT.Ln, bias=ones[:, 0:1]).then_inc(logv_done, 1)
            unit_sum(B - 1, 1)

            def softmax_exp(b, k):
                act.wait_ge(logits_ready, b + 1)
                wait(act, w_T, b - 1)
                nc.scalar.activation(w_sb[:, k, :], logits[:, k, :], ACT.Exp, bias=nlmax[:, k:k + 1],
                                     accum_out=wsum[:, b, :]).then_inc(w_done, 1)

            def fetch_query(b, k):
                act.wait_ge(query_done, B)
                wait(act, scores, b - 1)
                nc.scalar.copy(q_now[:, k, :], query[:, b, :]).then_inc(q_fetched, 1)

            def wT_copy(b):
                act.wait_ge(w_T, b + 1)
                wait(act, z_prod, b)
                nc.scalar.copy(wT[:, :, :].rearrange("p s c -> p (s c)"), bcast[:, 0:NSLOT]).then_inc(wT_copied, 1)

            def zT_copy(b, k):
                act.wait_ge(z_prod, b + 1)
                wait(act, f_prod, b - 1)
                nc.scalar.copy(zT[:, k, :], bcast[:, HALF:HALF + C]).then_inc(z_copied, 1)

            def value_step(b, k, old=True, new=True, after=True):
                if new and after:
                    fetch_query(b + 1, 1 - k)
                if old:
                    wT_copy(b - 1)
                    zT_copy(b - 1, 1 - k)
                if new:
                    softmax_exp(b, k)

            fetch_query(0, 0)
            act.wait_ge(learned_done, B)
            nc.scalar.activation(ga[:, :], learned[:, :, 0], ACT.Tanh, bias=half3[:, 0:1],
                                 scale=0.5).then_inc(gate_tanh, 1)
            value_step(0, 0, old=False)
            act.wait_ge(gate_arg, 1)
            nc.scalar.activation(gb[:, :], ga[:, :], ACT.Tanh, bias=half3[:, 2:3],
                                 scale=half3[:, 1:2]).then_inc(gate_tanh, 1)
            value_step(1, 1)
            value_step(2, 0)
            value_step(3, 1)
            with act.Fori(2, B // 2 - 1) as g:
                value_step(2 * g, 0)
                value_step(2 * g + 1, 1)
            value_step(B - 2, 0)
            value_step(B - 1, 1, after=False)
            value_step(B, 0, new=False)

        @block.gpsimd
        def _(pool):
            nc.gpsimd.memset(ones[:, :], 1.0).then_inc(consts, 1)
            nc.gpsimd.memset(half_neg[:, :], -0.5).then_inc(consts, 1)
            pool.wait_ge(consts, 2)

            def chain(done, base, ops):
                for s, (dst, a, c, sem_in, val) in enumerate(ops):
                    pool.wait_ge(sem_in, val)
                    if s:
                        pool.wait_ge(done, base + s)
                    nc.gpsimd.tensor_tensor(dst, a, c, ALU.add).then_inc(done, 1)

            def x_low(b):
                pool.wait_ge(x_hi, b + 1)
                wait(pool, q_prod, 4 * b)
                nc.gpsimd.tensor_tensor(xn_lo[:, :], xn[:, :], xn_hi[:, :].bitcast(F32),
                                        ALU.subtract).then_inc(x_split, 1)

            def ctx_low(b):
                pool.wait_ge(ctx_hi_done, b + 1)
                nc.gpsimd.tensor_tensor(ctx_lo[:, :], ctx_in[:, :], ctx_hi[:, :].bitcast(F32),
                                        ALU.subtract).then_inc(ctx_lo_done, 1)

            def rstd_pow(b):
                pool.wait_ge(x_ve, b + 1)
                wait(pool, x_norm, b)
                wait(pool, x_nb, b)
                nc.gpsimd.tensor_tensor(rstd[:, :], ve[:, :], half_neg[:, 0:1], ALU.pow).then_inc(x_rstd, 1)

            def q_scale(p, n):
                pool.wait_ge(r_done, 2 * p + n + 1)
                cols = slice(n * HALF, (n + 1) * HALF)
                nc.gpsimd.tensor_tensor(eq[:, :, cols], eq[:, :, cols],
                                        r_sb[:, cols].unsqueeze(1).broadcast_to([P, T, HALF]),
                                        ALU.mult).then_inc(q_mul, 1)

            def norm_pow(p):
                pool.wait_ge(l2_clamped, p + 1)
                wait(pool, rn_split, p)
                nc.gpsimd.tensor_tensor(rn[:, :], l2c[:, :], half_neg[:, 0:J], ALU.pow).then_inc(rn_pow, 1)

            def residual(p):
                pool.wait_ge(t_scaled, 2 * (p + 1))
                nc.gpsimd.tensor_tensor(X[:, p, :], X[:, p, :], t_sb[:, :], ALU.add).then_inc(x1_done, 1)

            def q_sums(b, n):
                wait(pool, q_sum, 2 * b)
                cols = slice(n * HALF, (n + 1) * HALF)
                e = [eq[:, t, cols] for t in range(T)]
                r = qtot[:, cols]
                chain(qsum_step, 6 * b + 3 * n, [
                    (r, e[0], e[1], q_exp, 2 * b + n + 1),
                    (r, r, e[2], q_exp, 2 * b + n + 1),
                    (r, r, e[3], q_exp, 2 * b + n + 1)])

            def body(b, lag, more):
                p = b - 1
                if lag:
                    q_scale(p, 0)
                    q_scale(p, 1)
                if more:
                    rstd_pow(b + 1)
                if lag > 1:
                    residual(p - 1)
                if more:
                    x_low(b + 1)
                q_sums(b, 0)
                if lag:
                    norm_pow(p)
                if more:
                    ctx_low(b + 1)
                q_sums(b, 1)
            rstd_pow(0)
            x_low(0)
            ctx_low(0)
            body(0, 0, True)
            body(1, 1, True)
            body(2, 2, True)
            with pool.Fori(3, B - 1) as b:
                body(b, 2, True)
            body(B - 1, 2, False)

            def scale_pow(n, batches):
                pool.wait_ge(ve2_done, n + 1)
                nc.gpsimd.tensor_tensor(rstd2[:, batches, 0], ve2[:, batches], half_neg[:, batches],
                                        ALU.pow).then_inc(rstd2_done, 1)

            z = B - 1
            q_scale(z, 0)
            q_scale(z, 1)
            residual(z - 1)
            norm_pow(z)
            scale_pow(0, slice(0, B - 1))
            pool.wait_ge(rn_pow, B)
            residual(z)
            pool.wait_ge(rstd2_done, 1)
            pool.wait_ge(x1_done, B)
            nc.gpsimd.memset(q_rows[:, :, BOT:P], 1.0).then_inc(query_ones, 1)
            pool.wait_ge(query_ones, 1)
            nc.gpsimd.memset(scoreB[BOT:P, :], 0.0).then_inc(ffn_zeros, 1)
            pool.wait_ge(ffn_zeros, 1)
            nc.gpsimd.memset(WvuT[VB:P, :], 0.0).then_inc(ffn_zeros, 1)
            pool.wait_ge(ffn_zeros, 2)
            nc.gpsimd.memset(VV[:, :, VB:P], 0.0).then_inc(ffn_zeros, 1)
            pool.wait_ge(ffn_zeros, 3)

            def add_h(b, k):
                pool.wait_ge(h_done, b + 1)
                nc.gpsimd.tensor_tensor(X[:, b, :], X[:, b, :], hbuf[:, k % 2, :], ALU.add).then_inc(y_done, 1)

            add_h(0, 0)
            add_h(1, 1)
            scale_pow(1, slice(B - 1, B))
            with pool.Fori(1, B // 2) as g:
                for k in range(2):
                    add_h(2 * g + k, k)

        @block.vector
        def _(dve):
            V = nc.vector

            def x_statistics(b):
                dve.wait_ge(x_in, 16 * (b + 1))
                wait_apart(dve, x_norm, b)
                for s in range(2):
                    V.bn_stats(st1[:, 6 * s:6 * s + 6], X[:, b, s * HALF:(s + 1) * HALF]).then_inc(x_stats, 1)
                wait_apart(dve, x_stats, 2 * (b + 1))
                V.bn_aggr(mv1[:, :], st1[:, :]).then_inc(x_mv, 1)
                dve.wait_ge(x_mv, b + 1)
                V.tensor_scalar_add(ve[:, :], mv1[:, 1:2], LN_EPS).then_inc(x_ve, 1)

            def x_bias(b):
                dve.wait_ge(x_rstd, b + 1)
                V.scalar_tensor_tensor(nb[:, :], mv1[:, 0:1], -1.0, rstd[:, :], ALU.mult,
                                       ALU.mult).then_inc(x_nb, 1)

            def k_reciprocals(p):
                dve.wait_ge(k_exp, 4 * (p + 1))
                V.reciprocal(krec[:, :], ksum[:, :]).then_inc(krec_done, 1)
                dve.wait_ge(krec_done, p + 1)
                wait(dve, mt_copied, p)
                V.tensor_scalar_mul(kscale[:, :], krec[:, :], float(DH) ** -0.5).then_inc(kscale_done, 1)

            def mt_scale(p):
                dve.wait_ge(mt_T, p + 1)
                dve.wait_ge(kscale_done, p + 1)
                wait(dve, out_prod, 2 * p)
                V.tensor_tensor(mt_sb[:, :, :], bank_g.rearrange("p (t c) -> p t c", t=T),
                                kscale[:, :].unsqueeze(2).broadcast_to([P, T, C]), ALU.mult).then_inc(mt_copied, 1)

            def q_tile_max(b, s):
                q = [qsb[:, t, :] for t in range(T)]
                if s == 0:
                    wait(dve, qmax_T, 2 * b)
                else:
                    dve.wait_ge(qmax_step, 3 * b + s)
                dve.wait_ge(q_evac, 4 * b + 2 + s)
                V.tensor_tensor(qred[:, :], q[0] if s == 0 else qred[:, :], q[s + 1], ALU.max).then_inc(qmax_step, 1)

            def k_maximum(b, t):
                dve.wait_ge(k_prod, 4 * b + t + 1)
                wait(dve, k_exp, 4 * b)
                V.tensor_reduce(nkm[:, t:t + 1], k_slot[t][:, :], AX, ALU.max, negate=True).then_inc(k_max, 1)

            def k_back(b, t):
                dve.wait_ge(k_T, 8 * b + 2 * t + 2)
                wait(dve, g_prod, 4 * b)
                V.tensor_copy(ekT[:, 4:J, t * P:(t + 1) * P],
                              bank7.rearrange("p (j d) -> p j d", d=P)).then_inc(ekT_back, 1)

            def ctx_back(b):
                dve.wait_ge(ctxT_prod, 2 * b + 2)
                wait(dve, g_prod, 4 * b)
                V.tensor_copy(ctxT[:, 4:J, :], bank7.rearrange("p (j c) -> p j c", c=P)).then_inc(ctxT_back, 1)

            def q_block_max(b, n):
                dve.wait_ge(qmax_T, 2 * b + n + 1)
                wait(dve, qm_split, b)
                V.tensor_reduce(qm[:, 4 * n * H:4 * (n + 1) * H], bank_q.rearrange("p (m d) -> p m d", d=DL), AX,
                                ALU.max).then_inc(qm_done, 1)

            def q_max_parts(b):
                dve.wait_ge(qm_done, 2 * (b + 1))
                wait(dve, qm_T, b)
                hi, lo = qm_hl[:, 0:J * H], qm_hl[:, J * H:2 * J * H]
                V.tensor_copy(hi, qm[:, :]).then_inc(qm_hi_done, 1)
                dve.wait_ge(qm_hi_done, b + 1)
                V.tensor_tensor(lo, qm[:, :], hi.bitcast(F32), ALU.subtract).then_inc(qm_split, 1)

            def q_max_turned(b):
                dve.wait_ge(qm_T, b + 1)
                wait(dve, qshift, 2 * b)
                V.tensor_copy(qmT[:, :], bank_q[:, 0:P]).then_inc(qmT_copied, 1)

            def q_shift(b, n):
                cols = slice(n * HALF, (n + 1) * HALF)
                dve.wait_ge(qshift, 2 * b + n + 1)
                V.tensor_tensor(qsb[:, :, cols], qsb[:, :, cols],
                                bank_q.unsqueeze(1).broadcast_to([P, T, HALF]), ALU.subtract).then_inc(q_sub, 1)

            def q_reciprocal(p, n):
                dve.wait_ge(q_sum, 2 * p + n + 1)
                wait(dve, q_mul, 2 * p)
                V.reciprocal(r_sb[:, n * HALF:(n + 1) * HALF], (bank_q, bank7)[n]).then_inc(r_done, 1)

            def norm_clamp(p):
                dve.wait_ge(ss_prod, p + 1)
                wait(dve, rn_pow, p)
                V.tensor_scalar_max(l2c[:, :], slot[0][:, 0:J], NORM_FLOOR).then_inc(l2_clamped, 1)

            def norm_parts(p):
                hi, lo = [rn_hl[:, s * J * H:(s + 1) * J * H].rearrange("p (j h) -> p j h", j=J) for s in (0, 1)]
                src = rn[:, :].unsqueeze(2).broadcast_to([P, J, H])
                dve.wait_ge(rn_pow, p + 1)
                wait(dve, rn_T, p)
                V.tensor_copy(hi, src).then_inc(rn_hi_done, 1)
                dve.wait_ge(rn_hi_done, p + 1)
                V.tensor_tensor(lo, src, hi.bitcast(F32), ALU.subtract).then_inc(rn_split, 1)

            def norm_turned(p):
                dve.wait_ge(rn_T, p + 1)
                wait(dve, rn_spread, 2 * p)
                V.tensor_copy(rnT[:, :], bank_q[:, 0:P]).then_inc(rnT_copied, 1)

            def norm_scale(p, n):
                cols = slice(n * HALF, (n + 1) * HALF)
                dve.wait_ge(rn_spread, 2 * p + n + 1)
                wait(dve, x1_done, p)
                V.scalar_tensor_tensor(t_sb[:, cols], o_sb[:, cols], gs[:, :], bank_q, ALU.mult,
                                       ALU.mult).then_inc(t_scaled, 1)

            def statistics(p):
                wait_apart(dve, x1_done, p + 1)
                for s in range(2):
                    V.bn_stats(st2[:, 6 * s:6 * s + 6], X[:, p, s * HALF:(s + 1) * HALF]).then_inc(stats2, 1)
                dve.wait_ge(stats2, 2 * (p + 1))
                wait_apart(dve, var2_done, 2 * p)
                V.bn_aggr(mv2[:, :], st2[:, :]).then_inc(mv2_done, 1)
                dve.wait_ge(mv2_done, p + 1)
                V.tensor_copy(mean2[:, p, :], mv2[:, 0:1]).then_inc(var2_done, 1)
                V.tensor_copy(var2[:, p, :], mv2[:, 1:2]).then_inc(var2_done, 1)

            def head_copy():
                dve.wait_ge(setup_u, 1)
                V.tensor_copy(U[:, :, :].rearrange("p h c -> p (h c)"), bcast[:, :]).then_inc(u_done, 1)

            def body(b, lag, more):
                p = b - 1
                if lag:
                    q_reciprocal(p, 0)
                    k_reciprocals(p)
                if lag > 1:
                    norm_parts(p - 1)
                    norm_turned(p - 1)
                q_tile_max(b, 0)
                if lag > 1:
                    norm_scale(p - 1, 0)
                if lag:
                    q_reciprocal(p, 1)
                else:
                    head_copy()
                q_tile_max(b, 1)
                if lag > 1:
                    norm_scale(p - 1, 1)
                k_maximum(b, 0)
                q_tile_max(b, 2)
                ctx_back(b)
                if lag:
                    mt_scale(p)
                k_maximum(b, 1)
                k_back(b, 0)
                q_block_max(b, 0)
                if more:
                    x_statistics(b + 1)
                q_block_max(b, 1)
                q_max_parts(b)
                if more:
                    x_bias(b + 1)
                k_maximum(b, 2)
                k_back(b, 1)
                q_max_turned(b)
                if lag > 1:
                    statistics(p - 1)
                q_shift(b, 0)
                if lag:
                    norm_clamp(p)
                k_maximum(b, 3)
                k_back(b, 2)
                q_shift(b, 1)

            x_statistics(0)
            x_bias(0)
            for n, (parts, src) in enumerate(((WqT, bank6), (WkT, bank7))):
                dve.wait_ge(setup_T, n + 1)
                hi, lo = [w[:, :].rearrange("p (t h d) -> p h t d", t=T, h=H) for w in parts]
                v = src.rearrange("p (h t d) -> p h t d", t=T, h=H)
                V.tensor_copy(hi, v).then_inc(setup_w, 1)
                dve.wait_ge(setup_w, 1 + 2 * n)
                V.tensor_tensor(lo, v, hi.bitcast(F32), ALU.subtract).then_inc(setup_w, 1)
            dve.wait_ge(setup_T, 3)
            V.tensor_copy(WoT, bank_q.rearrange("p (t c) -> p t c", t=T)).then_inc(wo_copied, 1)
            dve.wait_ge(weights_in, 16 * ATT_DMAS)
            V.tensor_scalar_mul(gs[:, :], g_in[:, :], float(C) ** 0.5)
            V.tensor_copy(sel_q[:, :, :], selq_in).then_inc(setup_w, 1)
            body(0, 0, True)
            body(1, 1, True)
            body(2, 2, True)
            with dve.Fori(3, B - 1) as b:
                body(b, 2, True)
            body(B - 1, 2, False)

            def scale_sum(n, batches):
                dve.wait_ge(var2_done, 2 * (B - 1 + n))
                V.tensor_scalar_add(ve2[:, batches], var2[:, batches, 0], LN_EPS).then_inc(ve2_done, 1)

            def scale_bias(n, batches):
                dve.wait_ge(rstd2_done, n + 1)
                V.scalar_tensor_tensor(nb2[:, batches, 0], mean2[:, batches, 0], -1.0, rstd2[:, batches, 0], ALU.mult,
                                       ALU.mult).then_inc(nb2_done, 1)

            def wu1_low(n):
                dve.wait_ge(wu1_hi, n + 1)
                hi, lo = [w[:, 4 * n:4 * n + 4, 0:UH] for w in WuqT]
                V.tensor_tensor(lo, (slot[1], work)[n][:, :].rearrange("p (j u) -> p j u", u=UH), hi.bitcast(F32),
                                ALU.subtract).then_inc(wu1_lo, 1)

            z = B - 1
            q_reciprocal(z, 0)
            k_reciprocals(z)
            norm_parts(z - 1)
            norm_turned(z - 1)
            norm_scale(z - 1, 0)
            q_reciprocal(z, 1)
            norm_scale(z - 1, 1)
            mt_scale(z)
            wu1_low(0)
            statistics(z - 1)
            scale_sum(0, slice(0, B - 1))
            wu1_low(1)
            norm_clamp(z)
            dve.wait_ge(wq_hi, 1)
            both = slot[1][:, :].rearrange("p (j d) -> p j d", j=J)
            V.tensor_tensor(WuqT[1][:, :, UH:UH + BOT], both[:, :, 0:BOT], WuqT[0][:, :, UH:UH + BOT].bitcast(F32),
                            ALU.subtract).then_inc(wq_lo, 1)
            V.tensor_copy(WvdT[:, :, :], both[:, :, BOT:P]).then_inc(wvd_copied, 1)
            norm_parts(z)
            norm_turned(z)
            scale_bias(0, slice(0, B - 1))
            norm_scale(z, 0)
            dve.wait_ge(key_T, 1)
            V.tensor_copy(keysT[:, :], bank6[0:BOT, 0:NSLOT]).then_inc(key_copied, 1)
            V.tensor_copy(WrT[:, :], bank6[0:BOT, NSLOT:NSLOT + RDIM]).then_inc(key_copied, 1)
            norm_scale(z, 1)
            dve.wait_ge(rk_prod, 1)
            V.tensor_copy(rkT[:, :], bank7[0:RDIM, 0:NSLOT]).then_inc(rk_copied, 1)
            dve.wait_ge(key_copied, 2)
            V.tensor_scalar_mul(scoreB[0:BOT, NSLOT:2 * NSLOT], keysT[:, :], float(BOT) ** -0.5).then_inc(score_ready, 1)
            for n, src in enumerate((bu2, gate_w, gate_b)):
                last = V.tensor_scalar_mul(half3[:, n:n + 1], src[:, :], 0.5)
            last.then_inc(score_ready, 1)
            dve.wait_ge(b1_prod, 1)
            V.tensor_scalar_mul(scoreB[0:BOT, 0:NSLOT], bank6[0:BOT, 0:NSLOT], float(RDIM) ** -0.5).then_inc(score_ready, 1)

            def hT_low(b, k):
                dve.wait_ge(hT_hi_done, b + 1)
                wait(dve, units_prod, b - 1)
                V.tensor_tensor(hT[1][:, k, :, :], slot[k][:, :].rearrange("p (j c) -> p j c", j=J),
                                hT[0][:, k, :, :].bitcast(F32), ALU.subtract).then_inc(hT_lo_done, 1)

            def unit_bias(b, k):
                dve.wait_ge(units_prod, b + 1)
                wait(dve, learned_done, b - 1)
                V.tensor_tensor(units[:, k, :], bcast[:, k * HALF:k * HALF + UH], bu1[:, :],
                                ALU.add).then_inc(units_biased, 1)

            def query_rows(b, k):
                wait(dve, q_T, b - 1)
                V.tensor_copy(q_rows[:, k, 0:BOT], bcast[:, k * HALF + UH:k * HALF + UH + BOT]).then_inc(q_copied, 1)

            def query_copy(b, k):
                dve.wait_ge(q_T, b + 1)
                V.tensor_copy(query[:, b, :], (bank6, bank7)[k][:, 0:P]).then_inc(query_done, 1)

            def unit_weights(b, k):
                dve.wait_ge(gelu_done, b + 1)
                V.tensor_tensor(units[:, k, :], units[:, k, :], Wu2[:, :], ALU.mult).then_inc(gelu_weighted, 1)

            def hidden_step(b, k, old=True, new=True, last=False):
                if new:
                    hT_low(b + 1, 1 - k)
                if old:
                    unit_weights(b - 1, 1 - k)
                if not last:
                    unit_bias(b, k)
                    query_rows(b, k)
                if old:
                    query_copy(b - 1, 1 - k)

            hT_low(0, 0)
            statistics(z)
            scale_sum(1, slice(z, B))
            hidden_step(0, 0, old=False)
            scale_bias(1, slice(z, B))
            V.tensor_tensor(varh[:, :], var2[:, :, 0], rstd2[:, :, 0], ALU.mult).then_inc(varh_step, 1)
            dve.wait_ge(varh_step, 1)
            V.tensor_tensor(varh[:, :], varh[:, :], rstd2[:, :, 0], ALU.mult).then_inc(varh_step, 1)
            hidden_step(1, 1)
            dve.wait_ge(vv_prod, 1)
            V.tensor_copy(VV[:, :, 0:VB], bcast[:, 0:2 * VB].rearrange("p (s d) -> p s d", d=VB)).then_inc(vv_copied, 1)
            with dve.Fori(1, B // 2 - 1) as g:
                hidden_step(2 * g, 0)
                hidden_step(2 * g + 1, 1)
            hidden_step(B - 2, 0)
            hidden_step(B - 1, 1, new=False)
            hidden_step(B, 0, new=False, last=True)

            def top(b, k):
                score = (bank6, bank7)[k][:, 0:NSLOT]
                dve.wait_ge(scores, b + 1)
                wait_apart(dve, masked, b)
                V.max(top8[:, k, :], score).then_inc(top_step, 1)

            def replace(b, k):
                score = (bank6, bank7)[k][:, 0:NSLOT]
                wait_apart(dve, top_step, 2 * b + 1)
                V.match_replace(replaced[:, :], top8[:, k, :], score, NEG).then_inc(top_step, 1)

            def mask(b, k):
                both = (bank6, bank7)[k]
                dve.wait_ge(top_step, 2 * b + 2)
                V.tensor_tensor(outside[:, :], replaced[:, :], both[:, 0:NSLOT], ALU.is_equal).then_inc(outside_done, 1)
                dve.wait_ge(outside_done, b + 1)
                wait(dve, w_done, b - 1)
                V.scalar_tensor_tensor(logits[:, k, :], outside[:, :], NEG, both[:, NSLOT:2 * NSLOT], ALU.mult,
                                       ALU.add).then_inc(masked, 1)

            def logit_max(b, k):
                dve.wait_ge(masked, b + 1)
                V.tensor_reduce(nlmax[:, k:k + 1], logits[:, k, :], AX, ALU.max, negate=True).then_inc(logits_ready, 1)

            def output_reciprocal(b):
                dve.wait_ge(w_done, b + 1)
                wait(dve, oscale_done, b)
                V.reciprocal(wrec[:, :], wsum[:, b, :]).then_inc(wrec_done, 1)

            def output_scale(b):
                dve.wait_ge(wrec_done, b + 1)
                wait(dve, y_ready, b)
                V.tensor_tensor(oscale[:, :], wrec[:, :], gate[:, b, :], ALU.mult).then_inc(oscale_done, 1)

            def finish(b, k):
                dve.wait_ge(oscale_done, b + 1)
                dve.wait_ge(f_prod, b + 1)
                dve.wait_ge(y_done, b + 1)
                wait(dve, out_stored, 16 * (b - 1))
                V.scalar_tensor_tensor(y_out[:, k, :], slot[k][:, :], oscale[:, :], X[:, b, :], ALU.mult,
                                       ALU.add).then_inc(y_ready, 1)

            def value_step(b, k, new=True, older=True):
                if new:
                    top(b, k)
                if older:
                    output_reciprocal(b - 2)
                if new:
                    replace(b, k)
                if older:
                    output_scale(b - 2)
                if new:
                    mask(b, k)
                    logit_max(b, k)
                if older:
                    finish(b - 2, k)

            dve.wait_ge(logv_done, 1)
            V.reduce_sum(logsum[:, :], logv[:, :], AX).then_inc(logsum_done, 1)
            value_step(0, 0, older=False)

            dve.wait_ge(logtotal, 1)
            V.tensor_scalar(logmean[:, :], slot[1][:, 0:1], 1.0 / (B * C), 1e-6, ALU.mult, ALU.add).then_inc(normv_step, 1)
            dve.wait_ge(normv_step, 1)
            V.reciprocal(logrec[:, :], logmean[:, :]).then_inc(normv_step, 1)
            dve.wait_ge(normv_step, 2)
            V.tensor_scalar(varh[:, :], logv[:, :], logrec[:, :], 0.5, ALU.mult, ALU.mult).then_inc(normv_step, 1)
            dve.wait_ge(normv_step, 3)
            V.tensor_scalar_add(normv[:, :], varh[:, :], 1.25).then_inc(normv_step, 1)
            dve.wait_ge(normv_step, 4)

            dve.wait_ge(gate_tanh, 1)
            V.scalar_tensor_tensor(gb[:, :], ga[:, :], 1.25, normv[:, :], ALU.mult, ALU.add).then_inc(gate_step, 1)
            dve.wait_ge(gate_step, 1)
            V.tensor_scalar(ga[:, :], gb[:, :], 0.0, 5.0, ALU.max, ALU.min).then_inc(gate_step, 1)
            dve.wait_ge(gate_step, 2)
            V.tensor_scalar(gb[:, :], ga[:, :], -TAU_LOW, 1.0 / (TAU_HIGH - TAU_LOW), ALU.add,
                            ALU.mult).then_inc(gate_step, 1)
            dve.wait_ge(gate_step, 3)
            V.tensor_scalar(ga[:, :], gb[:, :], 0.0, 1.0, ALU.max, ALU.min).then_inc(gate_arg, 1)
            dve.wait_ge(gate_tanh, 2)
            V.tensor_scalar(ga[:, :], gb[:, :], 0.5, 0.5, ALU.mult, ALU.add).then_inc(gate_step, 1)
            dve.wait_ge(gate_step, 4)
            V.scalar_tensor_tensor(gate[:, :, 0], ga[:, :], EARLY_EXIT, ga[:, :], ALU.is_ge,
                                   ALU.mult).then_inc(gate_done, 1)
            dve.wait_ge(gate_done, 1)

            value_step(1, 1, older=False)
            value_step(2, 0)
            value_step(3, 1)
            with dve.Fori(2, B // 2) as g:
                value_step(2 * g, 0)
                value_step(2 * g + 1, 1)
            value_step(B, 0, new=False)
            value_step(B + 1, 1, new=False)


def constants():
    import numpy as np
    head = np.arange(P) // DL
    head_ones = (head[:, None] == head[None]).astype(np.float32)
    select_q = np.zeros((2, J, H, J, H, DL), np.float32)
    for j in range(J):
        for h in range(H):
            select_q[:, j, h, j, h] = 1
    return {"identity": np.eye(P, dtype=np.float32), "head_ones": head_ones,
            "select_q": select_q.reshape(2 * J * H, J, P)}


INPUTS = ["x", "ctx_4096", "L0_xattn_Wq", "L0_xattn_Wk", "L0_xattn_Wv", "L0_xattn_Wo", "L0_xattn_bo", "L0_xattn_g",
          "L0_ffn_Wq", "L0_ffn_Wr", "L0_ffn_aux_keys", "L0_ffn_aux_values", "L0_ffn_Wvd", "L0_ffn_Wvu",
          "L0_ffn_Wu1", "L0_ffn_bu1", "L0_ffn_Wu2", "L0_ffn_bu2", "L0_ffn_gate_w1", "L0_ffn_gate_bias",
          "L0_ffn_log_rel"]


def layout(name, a):
    if name in ("L0_xattn_bo", "L0_xattn_g"):
        return a.reshape(C, 1)
    if name in ("L0_ffn_bu1", "L0_ffn_Wu2", "L0_ffn_bu2", "L0_ffn_gate_w1", "L0_ffn_gate_bias", "L0_ffn_log_rel"):
        return a.reshape(1, -1)
    return a


def kernel(**inputs):
    import numpy as np
    import concourse.bacc as bacc
    from concourse.bass_utils import run_bass_kernel_spmd

    nc = bacc.Bacc("TRN2", target_bir_lowering=False, num_devices=1)
    arrays = {n: np.ascontiguousarray(layout(n, np.asarray(inputs[n]))) for n in INPUTS} | constants()
    aps = {n: nc.dram_tensor(n, a.shape, mybir.dt.from_np(a.dtype), kind="ExternalInput").ap()
           for n, a in arrays.items()}
    out = nc.dram_tensor("out", (B, C, N), F32, kind="ExternalOutput").ap()
    attention_ffn_kernel(nc, out=out, **aps)
    r = run_bass_kernel_spmd(nc, [arrays], core_ids=[0])
    return r.results[0]["out"]
```
